# Optimizing a Trainium2 kernel written in Bass

```python
import numpy as np
import jax
import jax.numpy as jnp

def _softmax(x, axis=-1):
    return jax.nn.softmax(x, axis=axis)

def _gelu(x):
    return jax.nn.gelu(x, approximate=True)

def _silu(x):
    return jax.nn.silu(x)

def _sigmoid(x):
    return jax.nn.sigmoid(x)

def _layernorm(x, axis=-1, eps=1e-05):
    m = jnp.mean(x, axis=axis, keepdims=True)
    v = jnp.var(x, axis=axis, keepdims=True)
    return (x - m) / jnp.sqrt(v + eps)

def _scatter_add(tgt, idx, src, axis=0):
    return tgt.at[idx].add(src)

def _segment_sum(src, seg, n):
    return jax.ops.segment_sum(src, seg, n)
kernel_name = 'mk_flamingo_gated_d2_seqx_r8_bb069c'

def setup_inputs(seed: int=0):
    np.random.seed(seed)
    _w = jnp.asarray

    def _rec_inputs():
        import jax
        import jax.numpy as jnp
        _rk = jax.random.key(seed)
        x = -0.0003929 + 0.9999 * jax.random.normal(jax.random.fold_in(_rk, 1), (16, 64, 512), jnp.float32)
        _lenS = 64 - jax.random.randint(jax.random.fold_in(_rk, 7), (16,), 0, max(1, 64 // 4) + 1, jnp.int32)
        _lenS2 = 64 - jax.random.randint(jax.random.fold_in(_rk, 8), (16,), 0, max(1, 64 // 4) + 1, jnp.int32)
        _ctx_4096P = jax.random.normal(jax.random.fold_in(_rk, 11), (16, 16, 512), jnp.float32)
        _ctx_4096c = jax.random.dirichlet(jax.random.fold_in(_rk, 511), 0.3 * jnp.ones((16,), jnp.float32), (16, 64))
        _ctx_4096t = jnp.einsum('bsk,bkd->bsd', _ctx_4096c, _ctx_4096P)
        _ctx_4096t = _ctx_4096t * jax.lax.rsqrt(jnp.mean(jnp.square(_ctx_4096t)) + 1e-12) * 0.953939
        ctx_4096 = 2.81802e-05 + 1.00001 * (_ctx_4096t + 0.3 * jax.random.normal(jax.random.fold_in(_rk, 611), (16, 64, 512), jnp.float32))
        pos_BxS2 = jnp.broadcast_to(jnp.arange(64, dtype=jnp.int32), (16, 64))
        _validS = jnp.arange(64)[None, :] < _lenS[:, None]
        _validS2 = jnp.arange(64)[None, :] < _lenS2[:, None]
        _causal = jnp.tril(jnp.ones((64, 64), dtype=bool))
        mask_BxSxS2_ik0 = jnp.where(jnp.broadcast_to(_validS2[:, None, :], (16, 64, 64)), 0, 1).astype(jnp.int32)
        mask_1x1xSxS2_ff0 = jnp.where(jnp.ones((1, 1, 64, 64), dtype=bool), 0.0, -1000000000.0).astype(jnp.float32)
        _g = jax.random.normal(jax.random.fold_in(_rk, 9001), (2, 2), jnp.float32)
        _g = jnp.sign(_g) * jnp.maximum(jnp.abs(_g), 1.0) + (_g == 0) * 1.0
        g_xattn = _g[0]
        g_ffn = _g[1]
        return (x, ctx_4096, pos_BxS2, mask_BxSxS2_ik0, mask_1x1xSxS2_ff0, g_xattn, g_ffn)
    x, ctx_4096, pos_BxS2, mask_BxSxS2_ik0, mask_1x1xSxS2_ff0, g_xattn, g_ffn = _rec_inputs()

    def _L0_xattn_setup():
        import jax, jax.numpy as jnp
        import numpy as np
        B, S, E = (2, 256, 512)
        H, KVH, D = (32, 8, 128)
        GROUPS = H // KVH
        MAX_POS = 512
        ROPE_THETA = 10000.0

        def _rope_tables(max_pos, dim, theta):
            inv_freq = 1.0 / theta ** (jnp.arange(0, dim, 2, dtype=jnp.float32) / dim)
            t = jnp.arange(max_pos, dtype=jnp.float32)
            freqs = jnp.einsum('i,j->ij', t, inv_freq)
            emb = jnp.concatenate([freqs, freqs], axis=-1)
            return (jnp.cos(emb), jnp.sin(emb))

        def _rotate_half(x):
            x1, x2 = (x[..., :x.shape[-1] // 2], x[..., x.shape[-1] // 2:])
            return jnp.concatenate([-x2, x1], axis=-1)
        key = jax.random.key(seed)
        ks = jax.random.split(key, 8)
        scale_w = 1.0 / np.sqrt(E)
        query = jax.random.normal(ks[0], (B, S, E), dtype=jnp.float32)
        k_in = jax.random.normal(ks[1], (B, S, E), dtype=jnp.float32)
        v_in = jax.random.normal(ks[2], (B, S, E), dtype=jnp.float32)
        position_ids = jnp.broadcast_to(jnp.arange(S, dtype=jnp.int64), (B, S))
        src_mask = jnp.tril(jnp.ones((S, S), dtype=jnp.int32))
        src_mask = jnp.broadcast_to(src_mask, (B, S, S))
        Wq = jax.random.normal(ks[3], (E, H * D), dtype=jnp.float32) * scale_w
        Wk = jax.random.normal(ks[4], (E, KVH * D), dtype=jnp.float32) * scale_w
        Wv = jax.random.normal(ks[5], (E, KVH * D), dtype=jnp.float32) * scale_w
        Wo = jax.random.normal(ks[6], (H * D, E), dtype=jnp.float32) * scale_w
        return {'query': query, 'key': k_in, 'value': v_in, 'position_ids': position_ids, 'src_mask': src_mask, 'Wq': Wq, 'Wk': Wk, 'Wv': Wv, 'Wo': Wo}
    _L0_xattn_all = _L0_xattn_setup()
    _L0_xattn_in = {k: v for k, v in _L0_xattn_all.items() if k in ('Wq', 'Wk', 'Wv', 'Wo')}
    del _L0_xattn_all

    def _L0_ffn_setup():
        import jax, jax.numpy as jnp
        import numpy as np
        NUM_EXPERTS = 16
        TOP_K = 2
        INTER = 56
        key = jax.random.key(seed)
        k1, k2, k3, k4, k5 = jax.random.split(key, 5)
        B, S, H = (4, 256, 512)
        scale = 0.02
        return {'hid': jax.random.normal(k1, (B, S, H), dtype=jnp.float32), 'gate_w': jax.random.normal(k2, (NUM_EXPERTS, H), dtype=jnp.float32) * scale, 'u': jax.random.normal(k3, (NUM_EXPERTS * INTER, H), dtype=jnp.float32) * scale, 'g': jax.random.normal(k4, (NUM_EXPERTS * INTER, H), dtype=jnp.float32) * scale, 'd': jax.random.normal(k5, (H, NUM_EXPERTS * INTER), dtype=jnp.float32) * scale}
    _L0_ffn_all = _L0_ffn_setup()
    _L0_ffn_in = {k: v for k, v in _L0_ffn_all.items() if k in ('gate_w', 'u', 'g', 'd')}
    del _L0_ffn_all

    def _L1_xattn_setup():
        import jax, jax.numpy as jnp
        import numpy as np
        B, Q, K, D = (1, 128, 6404, 512)
        H, KVH, HD = (32, 8, 128)
        GROUPS = H // KVH
        EPS = 1e-05

        def _rmsnorm(x, w):
            xf = x.astype(jnp.float32)
            var = jnp.mean(xf * xf, axis=-1, keepdims=True)
            return (xf * jax.lax.rsqrt(var + EPS)).astype(x.dtype) * w
        key = jax.random.key(seed)
        ks = jax.random.split(key, 8)
        s = 0.02
        return {'hidden_states': jax.random.normal(ks[0], (B, Q, D), jnp.float32), 'cross_attention_states': jax.random.normal(ks[1], (B, K, D), jnp.float32), 'attention_mask': jnp.zeros((B, 1, Q, K), jnp.float32), 'Wq': jax.random.normal(ks[2], (H * HD, D), jnp.float32) * s, 'Wk': jax.random.normal(ks[3], (KVH * HD, D), jnp.float32) * s, 'Wv': jax.random.normal(ks[4], (KVH * HD, D), jnp.float32) * s, 'Wo': jax.random.normal(ks[5], (D, H * HD), jnp.float32) * s, 'q_norm_w': jnp.ones((HD,), jnp.float32), 'k_norm_w': jnp.ones((HD,), jnp.float32)}
    _L1_xattn_all = _L1_xattn_setup()
    _L1_xattn_in = {k: v for k, v in _L1_xattn_all.items() if k in ('Wq', 'Wk', 'Wv', 'Wo', 'q_norm_w', 'k_norm_w')}
    del _L1_xattn_all

    def _L1_ffn_setup():
        import jax, jax.numpy as jnp
        import numpy as np
        LORA_R = 16
        SCALE = 16.0 / np.sqrt(16.0)
        NUM_EXPERTS = 4
        TOP_K = 2
        IN_F = 512
        OUT_F = 512
        key = jax.random.key(seed)
        k_x, k_a, k_b, k_r = jax.random.split(key, 4)
        x = jax.random.normal(k_x, (2, 256, IN_F), dtype=jnp.float32)
        A = jax.random.normal(k_a, (NUM_EXPERTS, LORA_R, IN_F), dtype=jnp.float32) * (1.0 / np.sqrt(IN_F))
        B = jax.random.normal(k_b, (NUM_EXPERTS, OUT_F, LORA_R), dtype=jnp.float32) * 0.02
        Wr = jax.random.normal(k_r, (NUM_EXPERTS, IN_F), dtype=jnp.float32) * 0.02
        return {'x': x, 'A': A, 'B': B, 'Wr': Wr}
    _L1_ffn_all = _L1_ffn_setup()
    _L1_ffn_in = {k: v for k, v in _L1_ffn_all.items() if k in ('A', 'B', 'Wr')}
    del _L1_ffn_all
    return {'x': x, 'ctx_4096': ctx_4096, 'pos_BxS2': pos_BxS2, 'mask_BxSxS2_ik0': mask_BxSxS2_ik0, 'mask_1x1xSxS2_ff0': mask_1x1xSxS2_ff0, 'g_xattn': g_xattn, 'g_ffn': g_ffn, 'L0_xattn_Wq': _L0_xattn_in['Wq'], 'L0_xattn_Wk': _L0_xattn_in['Wk'], 'L0_xattn_Wv': _L0_xattn_in['Wv'], 'L0_xattn_Wo': _L0_xattn_in['Wo'], 'L0_ffn_gate_w': _L0_ffn_in['gate_w'], 'L0_ffn_u': _L0_ffn_in['u'], 'L0_ffn_g': _L0_ffn_in['g'], 'L0_ffn_d': _L0_ffn_in['d'], 'L1_xattn_Wq': _L1_xattn_in['Wq'], 'L1_xattn_Wk': _L1_xattn_in['Wk'], 'L1_xattn_Wv': _L1_xattn_in['Wv'], 'L1_xattn_Wo': _L1_xattn_in['Wo'], 'L1_xattn_q_norm_w': _L1_xattn_in['q_norm_w'], 'L1_xattn_k_norm_w': _L1_xattn_in['k_norm_w'], 'L1_ffn_A': _L1_ffn_in['A'], 'L1_ffn_B': _L1_ffn_in['B'], 'L1_ffn_Wr': _L1_ffn_in['Wr']}

def reference(x, ctx_4096, pos_BxS2, mask_BxSxS2_ik0, mask_1x1xSxS2_ff0, g_xattn, g_ffn, L0_xattn_Wq, L0_xattn_Wk, L0_xattn_Wv, L0_xattn_Wo, L0_ffn_gate_w, L0_ffn_u, L0_ffn_g, L0_ffn_d, L1_xattn_Wq, L1_xattn_Wk, L1_xattn_Wv, L1_xattn_Wo, L1_xattn_q_norm_w, L1_xattn_k_norm_w, L1_ffn_A, L1_ffn_B, L1_ffn_Wr):
    import jax
    import jax.numpy as jnp

    def _L0_xattn_ref(query, key, value, position_ids, src_mask, Wq, Wk, Wv, Wo):
        import jax, jax.numpy as jnp
        import numpy as np
        B, S, E = (2, 256, 512)
        H, KVH, D = (32, 8, 128)
        GROUPS = H // KVH
        MAX_POS = 512
        ROPE_THETA = 10000.0

        def _rope_tables(max_pos, dim, theta):
            inv_freq = 1.0 / theta ** (jnp.arange(0, dim, 2, dtype=jnp.float32) / dim)
            t = jnp.arange(max_pos, dtype=jnp.float32)
            freqs = jnp.einsum('i,j->ij', t, inv_freq)
            emb = jnp.concatenate([freqs, freqs], axis=-1)
            return (jnp.cos(emb), jnp.sin(emb))

        def _rotate_half(x):
            x1, x2 = (x[..., :x.shape[-1] // 2], x[..., x.shape[-1] // 2:])
            return jnp.concatenate([-x2, x1], axis=-1)
        nb, q_len, _ = query.shape
        q = (query @ Wq).reshape(nb, q_len, H, D).transpose(0, 2, 1, 3)
        k = (key @ Wk).reshape(nb, q_len, KVH, D).transpose(0, 2, 1, 3)
        v = (value @ Wv).reshape(nb, q_len, KVH, D).transpose(0, 2, 1, 3)
        cos_t, sin_t = _rope_tables(MAX_POS, D, ROPE_THETA)
        cos = cos_t[position_ids][:, None]
        sin = sin_t[position_ids][:, None]
        q = q * cos + _rotate_half(q) * sin
        k = k * cos + _rotate_half(k) * sin
        k = jnp.repeat(k, GROUPS, axis=1)
        v = jnp.repeat(v, GROUPS, axis=1)
        scores = jnp.einsum('bhqd,bhkd->bhqk', q, k) / jnp.sqrt(jnp.float32(D))
        mask = src_mask[:, None]
        scores = jnp.where(mask == 0, jnp.float32(-1000000000.0), scores)
        attn = jax.nn.softmax(scores, axis=-1)
        x = jnp.einsum('bhqk,bhkd->bhqd', attn, v)
        x = x.transpose(0, 2, 1, 3).reshape(nb, q_len, H * D)
        return x @ Wo

    def _L0_ffn_ref(hid, gate_w, u, g, d):
        import jax, jax.numpy as jnp
        import numpy as np
        NUM_EXPERTS = 16
        TOP_K = 2
        INTER = 56
        B, S, H = hid.shape
        x = hid.reshape(-1, H)
        bs = x.shape[0]
        logits = x @ gate_w.T
        probs = jax.nn.softmax(logits.astype(jnp.float32), axis=-1)
        vals, idx = jax.lax.top_k(probs, TOP_K)
        vals = vals / jnp.sum(vals, axis=-1, keepdims=True)
        rows = jnp.arange(bs)[:, None]
        w = jnp.zeros((bs, NUM_EXPERTS), dtype=jnp.float32).at[rows, idx].set(vals)
        w = w.astype(x.dtype)
        gate_out = (x @ g.T).reshape(bs, NUM_EXPERTS, INTER)
        up_out = (x @ u.T).reshape(bs, NUM_EXPERTS, INTER)
        h = jax.nn.silu(gate_out) * up_out
        d_r = d.reshape(H, NUM_EXPERTS, INTER)
        out = jnp.einsum('bei,hei,be->bh', h, d_r, w)
        return out.reshape(B, S, H)

    def _L1_xattn_ref(hidden_states, cross_attention_states, attention_mask, Wq, Wk, Wv, Wo, q_norm_w, k_norm_w):
        import jax, jax.numpy as jnp
        import numpy as np
        B, Q, K, D = (1, 128, 6404, 512)
        H, KVH, HD = (32, 8, 128)
        GROUPS = H // KVH
        EPS = 1e-05

        def _rmsnorm(x, w):
            xf = x.astype(jnp.float32)
            var = jnp.mean(xf * xf, axis=-1, keepdims=True)
            return (xf * jax.lax.rsqrt(var + EPS)).astype(x.dtype) * w
        bsz, q_len, _ = hidden_states.shape
        kv_len = cross_attention_states.shape[1]
        q = (hidden_states @ Wq.T).reshape(bsz, q_len, H, HD).transpose(0, 2, 1, 3)
        k = (cross_attention_states @ Wk.T).reshape(bsz, kv_len, KVH, HD).transpose(0, 2, 1, 3)
        v = (cross_attention_states @ Wv.T).reshape(bsz, kv_len, KVH, HD).transpose(0, 2, 1, 3)
        q = _rmsnorm(q, q_norm_w)
        k = jnp.repeat(k, GROUPS, axis=1)
        v = jnp.repeat(v, GROUPS, axis=1)
        k = _rmsnorm(k, k_norm_w)
        scale = 1.0 / np.sqrt(HD)
        scores = jnp.einsum('bhqd,bhkd->bhqk', q, k) * scale
        scores = scores + attention_mask[:, :, :, :kv_len]
        probs = jax.nn.softmax(scores.astype(jnp.float32), axis=-1).astype(q.dtype)
        out = jnp.einsum('bhqk,bhkd->bhqd', probs, v)
        out = out.transpose(0, 2, 1, 3).reshape(bsz, q_len, H * HD)
        return out @ Wo.T

    def _L1_ffn_ref(x, A, B, Wr):
        import jax, jax.numpy as jnp
        import numpy as np
        LORA_R = 16
        SCALE = 16.0 / np.sqrt(16.0)
        NUM_EXPERTS = 4
        TOP_K = 2
        IN_F = 512
        OUT_F = 512
        orig_shape = x.shape
        flat = x.reshape(-1, orig_shape[-1])
        logits = flat @ Wr.T
        topk_vals, topk_idx = jax.lax.top_k(logits, TOP_K)
        T = flat.shape[0]
        neg_inf = jnp.finfo(logits.dtype).min
        sparse = jnp.full_like(logits, neg_inf)
        rows = jnp.arange(T)[:, None]
        sparse = sparse.at[rows, topk_idx].set(topk_vals)
        gates = jax.nn.softmax(sparse, axis=-1)
        mid = jnp.einsum('tf,erf->ter', flat, A)
        all_deltas = jnp.einsum('ter,eor->teo', mid, B) * SCALE
        delta = jnp.sum(gates[:, :, None] * all_deltas, axis=1)
        return delta.reshape(*orig_shape[:-1], -1)
    x = x + jnp.tanh(g_xattn[0]) * _L0_xattn_ref(_layernorm(x, axis=-1), ctx_4096, ctx_4096, pos_BxS2, mask_BxSxS2_ik0, L0_xattn_Wq, L0_xattn_Wk, L0_xattn_Wv, L0_xattn_Wo)
    x = x + jnp.tanh(g_ffn[0]) * _L0_ffn_ref(_layernorm(x, axis=-1), L0_ffn_gate_w, L0_ffn_u, L0_ffn_g, L0_ffn_d)
    x = x + jnp.tanh(g_xattn[1]) * _L1_xattn_ref(_layernorm(x, axis=-1), ctx_4096, mask_1x1xSxS2_ff0, L1_xattn_Wq, L1_xattn_Wk, L1_xattn_Wv, L1_xattn_Wo, L1_xattn_q_norm_w, L1_xattn_k_norm_w)
    x = x + jnp.tanh(g_ffn[1]) * _L1_ffn_ref(_layernorm(x, axis=-1), L1_ffn_A, L1_ffn_B, L1_ffn_Wr)
    return x

_drawn_inputs = setup_inputs


def setup_inputs(seed=0):
    import zlib

    import numpy as np

    out = dict(_drawn_inputs(seed))
    spreads = {'g_ffn': (-1.0, 0.6), 'L1_xattn_q_norm_w': (1.0, 0.6), 'L1_xattn_k_norm_w': (1.0, 0.6)}
    factors = {'L0_ffn_gate_w': 8.0, 'L0_ffn_u': 8.0, 'L0_ffn_g': 8.0, 'L0_ffn_d': 8.0}
    for name, (base, spread) in spreads.items():
        noise = np.random.default_rng([zlib.crc32(name.encode()), seed]).standard_normal(out[name].shape)
        drawn = base * np.exp(spread * noise) if base else spread * noise
        out[name] = jnp.asarray(drawn.astype(out[name].dtype))
    for name, factor in factors.items():
        out[name] = (out[name] * factor).astype(out[name].dtype)
    return out
```

```python
from contextlib import ExitStack

import concourse.bass as bass
import numpy as np
from concourse import mybir

P = 128
B, S, E = 16, 64, 512
T = B * S
NT = T // P
KC = E // P
H, G, D = 32, 8, 128
J = H // G
GB = 4
NB = G // GB
BW = GB * D
HALF = T // 2
PAIRS = NT // 2
JS = J * S
SC = PAIRS * JS
QB = 32
NQ = SC // QB
MAX_POS, THETA = 512, 10000.0
PC = MAX_POS // P
NX, INTER = 16, 56
FI = NX * INTER
FT = FI // P
FH = FI // 2
XH = NX // 2
LX, LR, LO = 4, 16, 512
LM = LX * LR
LORA_SCALE = 16.0 / float(np.sqrt(16.0))
EPS = 1e-5
MASKED = -1000000000.0
BIG = 3.0e38
TAKEN, NO_MATCH = 3.3e38, 3.2e38

F32 = mybir.dt.float32
FR = mybir.dt.float32r
I32 = mybir.dt.int32
ALU = mybir.AluOpType
ACT = mybir.ActivationFunctionType
AX = mybir.AxisListType.X


def rope_constants():
    inv = np.float32(1.0) / np.float32(THETA) ** (np.arange(0, D, 2, dtype=np.float32) / np.float32(D))
    ang = np.arange(MAX_POS, dtype=np.float32)[:, None] * inv.astype(np.float32)[None, :]
    c, s = np.cos(ang).astype(np.float32), np.sin(ang).astype(np.float32)
    q = np.float32(1.0 / np.sqrt(D))
    return np.concatenate([c * q, c * q, s * q, -s * q, c, s], axis=1).astype(np.float32)


def build(nc, x, ctx_in, pos, mask0, mask1, g_xattn, g_ffn, Wq0, Wk0, Wv0, Wo0, gate_w, up_w, glu_w, down_w,
          Wq1, Wk1, Wv1, Wo1, q_norm, k_norm, lora_a, lora_b, lora_r, rope_c, out):
    stack = ExitStack()

    class Stage:

        def __init__(self, name, again=None, earlier=None):
            self.name, self.made, self.earlier = name, again.made if again else {}, earlier or {}

        def __getitem__(self, what):
            if what not in self.made:
                self.made[what] = stack.enter_context(nc.semaphore(f"{self.name}_{what}"))
            return self.made[what]

        def __call__(self, what, n):
            return self[what], n + self.earlier.get(what, 0)

    def alloc(where, *buffers):
        return [where.enter_context(nc.sbuf_tensor(n, shape, dt)) for n, shape, dt in buffers]

    with stack:
        ps_q = [stack.enter_context(nc.psum_tensor(f"ps_q{i}", [P, 512], F32)) for i in range(2)]
        ps_s = stack.enter_context(nc.psum_tensor("ps_s", [P, SC], F32))
        ps_b = [stack.enter_context(nc.psum_tensor(f"ps_b{i}", [P, 512], F32)) for i in range(4)]
        ps_h = [ps_s[:, 0:512], ps_s[:, 512:1024]]

        (x_sb, hT_hi, hT_lo, cos_q, sin_q, ident, ones, gates_in, gates, eps_ln, eps_rms, zero_b, ln_buf, ln_stats, ln_mv,
         ln_sd, ln_rs) = alloc(
            stack, ("x_sb", [P, NT, E], F32), ("hT_hi", [P, KC, T], FR), ("hT_lo", [P, KC, T], FR),
            ("cos_q", [P, T], F32), ("sin_q", [P, T], F32), ("ident", [P, P], F32), ("ones", [P, S], F32),
            ("gates_in", [P, 4], F32), ("gates", [P, 4], F32), ("eps_ln", [P, 1], F32), ("eps_rms", [P, 1], F32),
            ("zero_b", [P, 1], F32), ("ln_buf", [P, 2, E], F32), ("ln_stats", [P, NT, 6], F32), ("ln_mv", [P, NT, 2], F32),
            ("ln_sd", [P, NT], F32), ("ln_rs", [P, NT], F32))

        kT_dram = nc.dram_tensor("kT_spill", [2, G, P, T], F32, kind="Internal").ap()
        v_hi_dram = nc.dram_tensor("v_hi_spill", [2, G, P, T], F32, kind="Internal").ap()
        v_lo_dram = nc.dram_tensor("v_lo_spill", [2, G, P, T], F32, kind="Internal").ap()

        with ExitStack() as here:
            (cT_hi, cT_lo, cs_k, kw_raw, kw_hi, kw_lo, k_t1, k_t2, k_sq, k_ss) = alloc(
                here, ("cT_hi", [P, KC, T], FR), ("cT_lo", [P, KC, T], FR), ("cs_k", [P, NT, D], F32),
                ("kw_raw", [P, 2, KC, BW], F32), ("kw_hi", [P, 2, KC, BW], FR), ("kw_lo", [P, 2, KC, BW], FR),
                ("k_t1", [P, 2, BW], F32), ("k_t2", [P, 2, BW], F32), ("k_sq", [P, 1, BW], F32), ("k_ss", [P, 3, GB], F32))
            with ExitStack() as a:
                c_raw, onehot, pos_i, pos_f, rope_sb, lane_i, lane_f = alloc(
                    a, ("c_raw", [P, NT, E], F32), ("onehot", [P, PC, T], F32), ("pos_i", [P, T], I32),
                    ("pos_f", [P, T], F32), ("rope_sb", [P, PC, 3 * D], F32), ("lane_i", [P, 1], I32), ("lane_f", [P, PC], F32))
            with ExitStack() as a:
                kT_st, vs_hi, vs_lo = alloc(
                    a, ("kT_st", [P, GB, T], F32), ("vs_hi", [P, NT, BW], FR), ("vs_lo", [P, NT, BW], FR))

        with ExitStack() as here:
            (wq_raw, wq_hi, wq_lo, wo_raw, wo_hi, wo_lo, kT, v_hi, v_lo, qT, s_sb, p_sb, pT, p_hi, p_lo, o_hi, o_lo,
             mx_a, mx_b, mx_c, sm_a, sm_b, sm_c, p_rec) = alloc(
                here, ("wq_raw", [P, KC, 512], F32), ("wq_hi", [P, KC, J * D], FR), ("wq_lo", [P, KC, J * D], FR),
                ("wo_raw", [P, J, E], F32), ("wo_hi", [P, J, E], FR), ("wo_lo", [P, J, E], FR),
                ("kT", [P, 2, HALF], F32), ("v_hi", [P, NT, D], FR), ("v_lo", [P, NT, D], FR),
                ("qT", [P, 2, J, HALF], F32), ("s_sb", [P, SC], F32), ("p_sb", [P, SC], F32), ("pT", [P, SC], F32),
                ("p_hi", [P, SC], FR), ("p_lo", [P, SC], FR),
                ("o_hi", [P, PAIRS, J, P], FR), ("o_lo", [P, PAIRS, J, P], FR),
                ("mx_a", [P, NQ], F32), ("mx_b", [P, NQ], F32), ("mx_c", [P, NQ], F32),
                ("sm_a", [P, NQ], F32), ("sm_b", [P, NQ], F32), ("sm_c", [P, NQ], F32), ("p_rec", [P, NQ], F32))
            with ExitStack() as a:
                q_t1, q_t2, mask_i, keep0, offset0 = alloc(
                    a, ("q_t1", [P, 2, HALF], F32), ("q_t2", [P, 2, HALF], F32), ("mask_i", [P, 2, PAIRS, 2, QB], I32),
                    ("keep0", [P, 2, PAIRS, 2, QB], F32), ("offset0", [P, 2, PAIRS, 2, QB], F32))
            with ExitStack() as a:
                q_sq, r_ln, r_q, s_raw, mask1_sb, qk_in, qk_w = alloc(
                    a, ("q_sq", [P, J, HALF], F32), ("r_ln", [P, SC], F32), ("r_q", [P, SC], F32), ("s_raw", [P, SC], F32),
                    ("mask1_sb", [P, 2, QB], F32), ("qk_in", [P, 2], F32), ("qk_w", [P, 1], F32))

        with ExitStack() as here:
            gT_hi, gT_lo, uT_hi, uT_lo, dT_hi, dT_lo, rT_hi, rT_lo = alloc(
                here, ("gT_hi", [P, KC, FI], FR), ("gT_lo", [P, KC, FI], FR), ("uT_hi", [P, KC, FI], FR),
                ("uT_lo", [P, KC, FI], FR), ("dT_hi", [P, FT, E], FR), ("dT_lo", [P, FT, E], FR),
                ("rT_hi", [P, KC, P], FR), ("rT_lo", [P, KC, P], FR))
            (x_lgT, x_lg, x_mx, x_ex, x_sum, x_rec, x_p, x_top, x_rep, x_two, x_w) = alloc(
                here, ("x_lgT", [NX, T], F32), ("x_lg", [P, NT, NX], F32), ("x_mx", [P, NT], F32), ("x_ex", [P, NT, NX], F32),
                ("x_sum", [P, NT], F32), ("x_rec", [P, NT], F32), ("x_p", [P, NT, NX], F32), ("x_top", [P, NT, 8], F32),
                ("x_rep", [P, NT, NX], F32), ("x_two", [P, NT], F32), ("x_w", [P, NT, NX], F32))
            with ExitStack() as a:
                g_raw, u_raw, d_raw, r_raw = alloc(
                    a, ("g_raw", [P, FT, E], F32), ("u_raw", [P, FT, E], F32), ("d_raw", [P, KC, FI], F32), ("r_raw", [NX, E], F32))
            with ExitStack() as a:
                f_hi, f_lo, sg, gu, hid, hdT_hi, hdT_lo = alloc(
                    a, ("f_hi", [P, 2, KC, P], FR), ("f_lo", [P, 2, KC, P], FR), ("sg", [P, 2, FH], F32), ("gu", [P, 2, FH], F32),
                    ("hid", [P, FI], F32), ("hdT_hi", [P, FT, P], FR), ("hdT_lo", [P, FT, P], FR))

        with ExitStack() as here:
            (a_raw, b_raw, aT_hi, aT_lo, bT_hi, bT_lo, m_T, l_lg, l_top, l_rep, l_mx, l_ex, l_sum, l_rec, l_m, mT_hi, mT_lo) = alloc(
                here, ("a_raw", [LM + LX, E], F32), ("b_raw", [P, LO // P, LX, LR], F32), ("aT_hi", [P, KC, P], FR),
                ("aT_lo", [P, KC, P], FR), ("bT_hi", [LM, LO], FR), ("bT_lo", [LM, LO], FR), ("m_T", [LM + LX, T], F32),
                ("l_lg", [P, NT, 8], F32), ("l_top", [P, NT, 8], F32), ("l_rep", [P, NT, 8], F32), ("l_mx", [P, NT], F32),
                ("l_ex", [P, NT, LX], F32), ("l_sum", [P, NT], F32), ("l_rec", [P, NT], F32), ("l_m", [P, NT, LX, LR], F32),
                ("mT_hi", [LM, T], FR), ("mT_lo", [LM, T], FR))

        prep, kv = Stage("prep"), Stage("kv")
        units = 2 * G
        att_signals = {"wq_in": 16 * G, "wo_in": 16 * G, "k_in0": 16 * G, "k_in1": 16 * G, "v_in": 32 * G, "mask_in": 16 * 4 * 2 * PAIRS,
                       "wq_hi": J * G, "wq_lo": J * G, "wo_hi": J * G, "wo_lo": J * G}
        for per_unit, names in ((1, "scored s_turned s_masked mx_part mx_other s_max s_shifted p_exp sm_part sm_other sm_all p_rec "
                                    "p_normed p_turned p_hi p_lo"),
                                (J, "q_done q_rot o_done o_hi o_lo y_done y_added")):
            for name in names.split():
                att_signals[name] = per_unit * units
        ln_signals = {"sd": 1, "rs": 1} | dict.fromkeys(("stats", "moments", "normed", "transposed", "hi", "lo"), NT)
        att = [Stage("att")]
        att.append(Stage("att", att[0], att_signals))
        lns = [Stage("ln")]
        for n in range(1, 4):
            lns.append(Stage("ln", lns[0], {k: n * v for k, v in ln_signals.items()}))
        moe, lora = Stage("moe"), Stage("lora")
        xt = x.flatten_outer_dims().rearrange("(i p) e -> p i e", p=P)
        ct = ctx_in.flatten_outer_dims().rearrange("(i p) e -> p i e", p=P)
        ot = out.flatten_outer_dims().rearrange("(i p) e -> p i e", p=P)
        WQ, WK, WV, WO = [Wq0, Wq1], [Wk0, Wk1], [Wv0, Wv1], [Wo0, Wo1]

        block = stack.enter_context(nc.Block())

        def wide(t, inner):
            return t.unsqueeze(2).to_broadcast([t.shape[0], t.shape[1], inner])

        def three(dst, l_hi, l_lo, r_hi, r_lo, first, last):
            nc.tensor.matmul(dst, l_hi, r_hi, start=first, stop=False)
            nc.tensor.matmul(dst, l_hi, r_lo, start=False, stop=False)
            return nc.tensor.matmul(dst, l_lo, r_hi, start=False, stop=last)

        def ln_stats_dve(dve, c, done):
            for i in range(NT):
                dve.wait_ge(*done(i))
                nc.vector.bn_stats(ln_stats[:, i, :], x_sb[:, i, :]).then_inc(c["stats"], 1)
            for i in range(NT):
                dve.wait_ge(*c("stats", i + 1))
                nc.vector.bn_aggr(ln_mv[:, i, :], ln_stats[:, i, :]).then_inc(c["moments"], 1)

        def ln_act_sd(act, c):
            act.wait_ge(*c("moments", NT))
            nc.scalar.activation(ln_sd[:, :], ln_mv[:, :, 1], ACT.Sqrt, bias=eps_ln[:, 0:1]).then_inc(c["sd"], 1)

        def ln_apply_dve(dve, c):
            dve.wait_ge(*c("sd", 1))
            nc.vector.reciprocal(ln_rs[:, :], ln_sd[:, :]).then_inc(c["rs"], 1)
            dve.wait_ge(*c("rs", 1))

            def low(i):
                dve.wait_ge(*c("hi", i + 1))
                nc.vector.tensor_tensor(hT_lo[:, :, i * P:(i + 1) * P], ps_h[i % 2].rearrange("p (k t) -> p k t", k=KC),
                                        hT_hi[:, :, i * P:(i + 1) * P].bitcast(F32), ALU.subtract).then_inc(c["lo"], 1)

            for i in range(NT):
                if i >= 2:
                    dve.wait_ge(*c("transposed", i - 1))
                nc.vector.tensor_scalar(ln_buf[:, i % 2, :], x_sb[:, i, :], ln_mv[:, i, 0:1], ln_rs[:, i:i + 1],
                                        ALU.subtract, ALU.mult).then_inc(c["normed"], 1)
                if i >= 1:
                    low(i - 1)
            low(NT - 1)

        def ln_pe(pe, c):
            for i in range(NT):
                pe.wait_ge(*c("normed", i + 1))
                if i >= 2:
                    pe.wait_ge(*c("lo", i - 1))
                for k in range(KC):
                    last = nc.tensor.transpose(ps_h[i % 2][:, k * P:(k + 1) * P], ln_buf[:, i % 2, k * P:(k + 1) * P], ident[:, :])
                last.then_inc(c["transposed"], 1)

        def ln_act(act, c):
            for i in range(NT):
                act.wait_ge(*c("transposed", i + 1))
                nc.scalar.activation(hT_hi[:, :, i * P:(i + 1) * P], ps_h[i % 2].rearrange("p (k t) -> p k t", k=KC),
                                     ACT.Copy).then_inc(c["hi"], 1)

        def prep_sync(sp):
            c = prep
            hn = NT // 2
            for h in range(2):
                sp.dma_start(c_raw[:, h * hn:(h + 1) * hn, :], ct[:, h * hn:(h + 1) * hn, :]).then_inc(c[f"ctx{h}"], 16)
            sp.dma_start(pos_i[:, :], pos.rearrange("b s -> (b s)").partition_broadcast(P)).then_inc(c["pos"], 16)
            sp.dma_start(rope_sb[:, :, :], rope_c.rearrange("(c p) d -> p c d", p=P)).then_inc(c["rope"], 16)

        def prep_sync_late(sp):
            c = prep
            sp.dma_start(x_sb[:, :, :], xt).then_inc(c["x"], 16)
            sp.dma_start(gates_in[:, 0:2], g_xattn.partition_broadcast(P)).then_inc(c["gates_in"], 16)
            sp.dma_start(gates_in[:, 2:4], g_ffn.partition_broadcast(P)).then_inc(c["gates_in"], 16)

        def prep_pool(pool):
            c = prep
            nc.gpsimd.memset(ident[:, :], 0.0).then_inc(c["cleared"], 1)
            nc.gpsimd.memset(ones[:, :], 1.0).then_inc(c["consts"], 1)
            nc.gpsimd.memset(eps_ln[:, :], EPS).then_inc(c["consts"], 1)
            nc.gpsimd.memset(eps_rms[:, :], D * EPS).then_inc(c["consts"], 1)
            nc.gpsimd.memset(zero_b[:, :], 0.0).then_inc(c["consts"], 1)
            nc.gpsimd.iota(lane_i[:, :], pattern=[[0, 1]], base=0, channel_multiplier=1).then_inc(c["lane"], 1)
            pool.wait_ge(c["cleared"], 1)
            nc.gpsimd.affine_select(out=ident[:, :], in_=ident[:, :], compare_op=ALU.not_equal, fill=1.0, base=0,
                                    pattern=[[-1, P]], channel_multiplier=1).then_inc(c["ident"], 1)

        def prep_dve(dve):
            c = prep
            dve.wait_ge(c["lane"], 1)
            for k in range(PC):
                nc.vector.tensor_scalar(lane_f[:, k:k + 1], lane_i[:, :], float(k * P), None, ALU.add).then_inc(c["lane_f"], 1)
            dve.wait_ge(c["pos"], 16)
            nc.vector.tensor_copy(pos_f[:, :], pos_i[:, :]).then_inc(c["pos_f"], 1)
            dve.wait_ge(c["pos_f"], 1)
            nc.vector.tensor_scalar(onehot[:, 0, :], pos_f[:, :], 0.0, float(MAX_POS), ALU.is_lt, ALU.mult).then_inc(c["pos_f"], 1)
            dve.wait_ge(c["pos_f"], 2)
            nc.vector.tensor_tensor(pos_f[:, :], pos_f[:, :], onehot[:, 0, :], ALU.add).then_inc(c["pos_f"], 1)
            dve.wait_ge(c["pos_f"], 3)
            nc.vector.tensor_scalar(pos_f[:, :], pos_f[:, :], 0.0, float(MAX_POS - 1), ALU.max, ALU.min).then_inc(c["pos_f"], 1)
            dve.wait_ge(c["pos_f"], 4)
            dve.wait_ge(c["lane_f"], PC)
            for k in range(PC):
                nc.vector.tensor_scalar(onehot[:, k, :], pos_f[:, :], lane_f[:, k:k + 1], None, ALU.is_equal).then_inc(c["onehot"], 1)
            for i in range(NT):
                dve.wait_ge(c["ctx_hi"], i + 1)
                nc.vector.tensor_tensor(cT_lo[:, :, i * P:(i + 1) * P], ps_h[i % 2].rearrange("p (k t) -> p k t", k=KC),
                                        cT_hi[:, :, i * P:(i + 1) * P].bitcast(F32), ALU.subtract).then_inc(c["ctx_lo"], 1)

        def prep_pe(pe):
            c = prep
            pe.wait_ge(c["ident"], 1)
            for i in range(NT):
                if i % (NT // 2) == 0:
                    pe.wait_ge(c[f"ctx{2 * i // NT}"], 16)
                if i >= 2:
                    pe.wait_ge(c["ctx_lo"], i - 1)
                for k in range(KC):
                    last = nc.tensor.transpose(ps_h[i % 2][:, k * P:(k + 1) * P], c_raw[:, i, k * P:(k + 1) * P], ident[:, :])
                last.then_inc(c["ctx_t"], 1)
            pe.wait_ge(c["onehot"], PC)
            pe.wait_ge(c["rope"], 16)
            for n in range(4):
                kind, h = divmod(n, 2)
                for k in range(PC):
                    last = nc.tensor.matmul(ps_b[n][:, :], rope_sb[:, k, kind * D:(kind + 1) * D],
                                            onehot[:, k, h * HALF:(h + 1) * HALF], start=k == 0, stop=k == PC - 1)
                last.then_inc(c["table_q"], 1)
            for i in range(NT):
                for k in range(PC):
                    last = nc.tensor.matmul(ps_q[i // 4][:, (i % 4) * D:(i % 4 + 1) * D], onehot[:, k, i * P:(i + 1) * P],
                                            rope_sb[:, k, 2 * D:3 * D], start=k == 0, stop=k == PC - 1)
                last.then_inc(c["table_k"], 1)

        def prep_act(act):
            c = prep
            for i in range(NT):
                act.wait_ge(c["ctx_t"], i + 1)
                nc.scalar.activation(cT_hi[:, :, i * P:(i + 1) * P], ps_h[i % 2].rearrange("p (k t) -> p k t", k=KC),
                                     ACT.Copy).then_inc(c["ctx_hi"], 1)
            for n in range(4):
                kind, h = divmod(n, 2)
                act.wait_ge(c["table_q"], n + 1)
                nc.scalar.activation((cos_q, sin_q)[kind][:, h * HALF:(h + 1) * HALF], ps_b[n][:, :], ACT.Copy).then_inc(c["tables"], 1)
            for b in range(2):
                act.wait_ge(c["table_k"], 4 * b + 4)
                nc.scalar.activation(cs_k[:, 4 * b:4 * b + 4, :], ps_q[b].rearrange("p (i d) -> p i d", d=D), ACT.Copy).then_inc(c["tables"], 1)

        def kv_sync_load(sp, cb, b):
            lay, w = divmod(b, 2)
            src = (WK, WV)[w][lay]
            if lay == 0:
                view = src[:, cb * BW:(cb + 1) * BW].rearrange("(k p) c -> p k c", p=P)
            else:
                view = src[cb * BW:(cb + 1) * BW, :].rearrange("(r p) e -> p r e", p=P)
            sp.dma_start(kw_raw[:, w, :, :], view).then_inc(kv[f"raw{w}"], 16)

        def kv_sync_spill(sp, cb, b):
            c = kv
            lay, w = divmod(b, 2)
            if w == 0:
                sp.wait_ge(c[f"k_staged{lay}"], NT * (cb + 1))
                sp.dma_start(kT_dram[lay, cb * GB:(cb + 1) * GB, :, :].rearrange("g p t -> p g t"), kT_st[:, :, :]).then_inc(c["k_spilled"], 16)
            else:
                sp.wait_ge(c["v_hi"], NT * (2 * cb + lay + 1))
                sp.wait_ge(c["v_lo"], NT * (2 * cb + lay + 1))
                for st, dr in ((vs_hi, v_hi_dram), (vs_lo, v_lo_dram)):
                    for g in range(GB):
                        sp.dma_start(dr[lay, cb * GB + g, :, :].rearrange("p (i d) -> p i d", d=D), st[:, :, g * D:(g + 1) * D].bitcast(F32)).then_inc(c["v_spilled"], 16)

        def kv_sync(sp):
            c = kv
            kv_sync_load(sp, 0, 0)
            kv_sync_load(sp, 0, 1)
            prep_sync_late(sp)
            for cb in range(NB):
                for w in range(2):
                    sp.wait_ge(c["w0_hi"], 8 * cb + 4 * w + 4)
                    sp.wait_ge(c["w0_lo"], 8 * cb + 4 * w + 4)
                    kv_sync_load(sp, cb, 2 + w)
                kv_sync_spill(sp, cb, 0)
                kv_sync_spill(sp, cb, 1)
                for w in range(2):
                    if cb + 1 < NB:
                        sp.wait_ge(c["w1_t"], 8 * cb + 4 * w + 4)
                        kv_sync_load(sp, cb + 1, w)
                kv_sync_spill(sp, cb, 2)
                kv_sync_spill(sp, cb, 3)

        def kv_pe(pe):
            c = kv

            def weights_t(cb, b):
                w = b % 2
                pe.wait_ge(c[f"raw{w}"], 16 * (2 * cb + 2))
                for k in range(KC):
                    n = 8 * cb + 4 * w + k
                    if not (cb == 0 and n < 2):
                        pe.wait_ge(c["w1_lo"], n - 1 if k >= 2 or b == 3 else 8 * cb)
                    for r in range(KC):
                        last = nc.tensor.transpose(ps_b[2 + k % 2][:, r * P:(r + 1) * P], kw_raw[:, w, r, k * P:(k + 1) * P], ident[:, :])
                    last.then_inc(c["w1_t"], 1)

            def keys_t(cb, lay, i):
                pe.wait_ge(c[f"k_done{lay}"], NT * cb + i + 1)
                if i >= 2:
                    pe.wait_ge(c[f"k_staged{lay}"], NT * cb + i - 1)
                elif lay:
                    pe.wait_ge(c["k_staged0"], NT * (cb + 1))
                elif not cb == 0:
                    pe.wait_ge(c["k_staged1"], NT * cb)
                for g in range(GB):
                    last = nc.tensor.transpose(ps_b[i % 2][:, g * P:(g + 1) * P], k_t1[:, i % 2, g * D:(g + 1) * D], ident[:, :])
                last.then_inc(c["k_t"], 1)

            pe.wait_ge(prep["ctx_lo"], NT)
            pe.wait_ge(prep["tables"], 6)

            def columns(cb):
                for b in range(4):
                    lay, w = divmod(b, 2)
                    if lay == 0:
                        pe.wait_ge(c["w0_hi"], 8 * cb + 4 * w + 4)
                        pe.wait_ge(c["w0_lo"], 8 * cb + 4 * w + 4)
                    else:
                        pe.wait_ge(c["w1_hi"], 8 * cb + 4 * w + 4)
                        pe.wait_ge(c["w1_lo"], 8 * cb + 4 * w + 4)
                    for i in range(NT):
                        bb, ii = (b, i - 2) if i >= 2 else (b - 1, NT - 2 + i)
                        if bb < 0 and cb == 0:
                            pass
                        elif bb < 0:
                            pe.wait_ge(c["v_lo"], 2 * NT * cb - 1 + i)
                        elif bb % 2:
                            pe.wait_ge(c["v_lo"], NT * (2 * cb + bb // 2) + ii + 1)
                        else:
                            pe.wait_ge(c[("k_read0", "k_done1")[bb // 2]], NT * cb + ii + 1)
                        for k in range(KC):
                            last = three(ps_q[i % 2][:, :], cT_hi[:, k, i * P:(i + 1) * P], cT_lo[:, k, i * P:(i + 1) * P],
                                         kw_hi[:, w, k, :], kw_lo[:, w, k, :], k == 0, k == KC - 1)
                        last.then_inc(c["tile"], 1)
                        if w == 0 and i >= 1:
                            keys_t(cb, lay, i - 1)
                        if w == 1 and i == 0:
                            keys_t(cb, lay, NT - 1)
                        if i == 3 and b in (1, 2):
                            weights_t(cb, b + 1)

            for cb in range(NB):
                columns(cb)

        def kv_act(act):
            c = kv

            def columns(cb):

                def weights_hi(b):
                    lay, w = divmod(b, 2)
                    if lay == 0:
                        act.wait_ge(c[f"raw{w}"], 16 * (2 * cb + 1))
                        if not cb == 0:
                            act.wait_ge(c["tile"], 4 * NT * cb)
                    for k in range(KC):
                        if lay == 0:
                            src = kw_raw[:, w, k, :]
                        else:
                            act.wait_ge(c["w1_t"], 8 * cb + 4 * w + k + 1)
                            src = ps_b[2 + k % 2][:, :]
                        nc.scalar.activation(kw_hi[:, w, k, :], src, ACT.Copy).then_inc(c[f"w{lay}_hi"], 1)

                def stage_keys(lay, i):
                    act.wait_ge(c["k_t"], NT * (2 * cb + lay) + i + 1)
                    if i == 0 and not (cb == 0 and lay == 0):
                        act.wait_ge(c["k_spilled"], 16 * (2 * cb + lay))
                    nc.scalar.activation(kT_st[:, :, i * P:(i + 1) * P], ps_b[i % 2].rearrange("p (g t) -> p g t", g=GB),
                                         ACT.Copy).then_inc(c[f"k_staged{lay}"], 1)

                def values_hi(lay, i):
                    act.wait_ge(c["tile"], NT * (4 * cb + 2 * lay + 1) + i + 1)
                    if i == 0 and not (cb == 0 and lay == 0):
                        act.wait_ge(c["v_spilled"], 16 * 2 * GB * (2 * cb + lay))
                    nc.scalar.activation(vs_hi[:, i, :], ps_q[i % 2][:, :], ACT.Copy).then_inc(c["v_hi"], 1)

                weights_hi(0)
                weights_hi(1)
                for i in range(NT - 1):
                    stage_keys(0, i)
                for i in range(NT):
                    values_hi(0, i)
                    if i == 0:
                        stage_keys(0, NT - 1)
                    if i == 3:
                        weights_hi(2)
                for i in range(NT):
                    act.wait_ge(c["tile"], NT * (4 * cb + 2) + i + 1)
                    if not (cb == 0 and i == 0):
                        act.wait_ge(c["k_ssq"], NT * cb + i)
                    nc.scalar.activation(k_sq[:, 0, :], ps_q[i % 2][:, :], ACT.Square).then_inc(c["k_sq"], 1)
                    act.wait_ge(c["k_ssq"], NT * cb + i + 1)
                    nc.scalar.activation(k_ss[:, 1, :], k_ss[:, 0, :], ACT.Sqrt, bias=eps_ln[:, 0:1], scale=1.0 / D).then_inc(c["k_rms"], 1)
                    if i >= 1:
                        stage_keys(1, i - 1)
                    if i == 3:
                        weights_hi(3)
                for i in range(NT):
                    values_hi(1, i)
                    if i == 0:
                        stage_keys(1, NT - 1)

            for cb in range(NB):
                columns(cb)

        def kv_pool(pool):
            c = kv

            def columns(cb):

                def weights_lo(w, k):
                    pool.wait_ge(c["w0_hi"], 8 * cb + 4 * w + k + 1)
                    nc.gpsimd.tensor_tensor(kw_lo[:, w, k, :], kw_raw[:, w, k, :], kw_hi[:, w, k, :].bitcast(F32),
                                            ALU.subtract).then_inc(c["w0_lo"], 1)

                for k in range(KC):
                    weights_lo(0, k)
                for i in range(NT):
                    pool.wait_ge(c["k_read0"], NT * cb + i + 1)
                    nc.gpsimd.tensor_tensor(k_t1[:, i % 2, :], k_t1[:, i % 2, :], k_t2[:, i % 2, :], ALU.add).then_inc(c["k_done0"], 1)
                    if i < KC:
                        weights_lo(1, i)

            for cb in range(NB):
                columns(cb)

        def kv_dve(dve):
            c = kv
            h = D // 2
            dve.wait_ge(prep["tables"], 6)

            def columns(cb):

                def weights_lo(b):
                    w = b % 2
                    for k in range(KC):
                        dve.wait_ge(c["w1_hi"], 8 * cb + 4 * w + k + 1)
                        nc.vector.tensor_tensor(kw_lo[:, w, k, :], ps_b[2 + k % 2][:, :], kw_hi[:, w, k, :].bitcast(F32),
                                                ALU.subtract).then_inc(c["w1_lo"], 1)

                def values_lo(lay, i):
                    dve.wait_ge(c["v_hi"], NT * (2 * cb + lay) + i + 1)
                    nc.vector.tensor_tensor(vs_lo[:, i, :], ps_q[i % 2][:, :], vs_hi[:, i, :].bitcast(F32),
                                            ALU.subtract).then_inc(c["v_lo"], 1)

                for i in range(NT):
                    dve.wait_ge(c["tile"], NT * 4 * cb + i + 1)
                    if i >= 2:
                        dve.wait_ge(c["k_t"], NT * 2 * cb + i - 1)
                    elif not cb == 0:
                        dve.wait_ge(c["k_t"], NT * 2 * cb)
                    key = ps_q[i % 2].rearrange("p (g u d) -> p g u d", g=GB, u=2)
                    t1 = k_t1[:, i % 2, :].rearrange("p (g u d) -> p g u d", g=GB, u=2)
                    t2 = k_t2[:, i % 2, :].rearrange("p (g u d) -> p g u d", g=GB, u=2)
                    cos = cs_k[:, i, 0:h].unsqueeze(1).to_broadcast([P, GB, h])
                    sin = cs_k[:, i, h:D].unsqueeze(1).to_broadcast([P, GB, h])
                    for u in range(2):
                        nc.vector.tensor_tensor(t1[:, :, u, :], key[:, :, u, :], cos, ALU.mult).then_inc(c["k_cos"], 1)
                    nc.vector.scalar_tensor_tensor(t2[:, :, 0, :], key[:, :, 1, :], -1.0, sin, ALU.mult, ALU.mult).then_inc(c["k_cos"], 1)
                    nc.vector.tensor_tensor(t2[:, :, 1, :], key[:, :, 0, :], sin, ALU.mult).then_inc(c["k_read0"], 1)
                for i in range(NT):
                    values_lo(0, i)
                    if i == 3:
                        weights_lo(2)
                for i in range(NT):
                    dve.wait_ge(c["k_sq"], NT * cb + i + 1)
                    nc.vector.tensor_reduce(k_ss[:, 0, :], k_sq[:, 0, :].rearrange("p (g d) -> p g d", g=GB), AX, ALU.add).then_inc(c["k_ssq"], 1)
                    dve.wait_ge(c["k_rms"], NT * cb + i + 1)
                    nc.vector.reciprocal(k_ss[:, 2, :], k_ss[:, 1, :]).then_inc(c["k_rrms"], 1)
                    dve.wait_ge(c["k_rrms"], NT * cb + i + 1)
                    if i < 2:
                        dve.wait_ge(c["k_t"], NT * (2 * cb + 1))
                    else:
                        dve.wait_ge(c["k_t"], NT * (2 * cb + 1) + i - 1)
                    nc.vector.tensor_tensor(k_t1[:, i % 2, :].rearrange("p (g d) -> p g d", g=GB), ps_q[i % 2].rearrange("p (g d) -> p g d", g=GB),
                                            wide(k_ss[:, 2, :], D), ALU.mult).then_inc(c["k_done1"], 1)
                    if i == 3:
                        weights_lo(3)
                for i in range(NT):
                    values_lo(1, i)

            for cb in range(NB):
                columns(cb)

        def att_sync(sp, lay):
            c = att[lay]

            def load_wq(g):
                if lay == 0:
                    view = Wq0.rearrange("(k p) (g n) -> g p k n", p=P, g=G)[g]
                else:
                    view = Wq1.rearrange("(g j p) e -> g p j e", p=P, g=G)[g]
                sp.dma_start(wq_raw[:, :, :], view).then_inc(c["wq_in"], 16)

            def load_wo(g):
                if lay == 0:
                    view = Wo0.rearrange("(g j p) e -> g p j e", p=P, g=G)[g]
                else:
                    view = Wo1.rearrange("(k p) (g n) -> g p k n", p=P, g=G)[g]
                sp.dma_start(wo_raw[:, :, :], view).then_inc(c["wo_in"], 16)

            def load_k(g, h):
                sp.dma_start(kT[:, h, :], kT_dram[lay, g, :, h * HALF:(h + 1) * HALF]).then_inc(c[f"k_in{h}"], 16)

            def load_v(g):
                sp.dma_start(v_hi[:, :, :].bitcast(F32), v_hi_dram[lay, g].rearrange("p (i d) -> p i d", d=D)).then_inc(c["v_in"], 16)
                sp.dma_start(v_lo[:, :, :].bitcast(F32), v_lo_dram[lay, g].rearrange("p (i d) -> p i d", d=D)).then_inc(c["v_in"], 16)

            def wo_split(n):
                sp.wait_ge(*c("wo_hi", 4 * n))
                sp.wait_ge(*c("wo_lo", 4 * n))

            def wq_split(n):
                sp.wait_ge(*c("wq_hi", 4 * n))
                sp.wait_ge(*c("wq_lo", 4 * n))

            if lay == 0:
                sp.wait_ge(kv["k_spilled"], 16 * 2 * NB)
                sp.wait_ge(kv["v_spilled"], 16 * 2 * GB * 2 * NB)
            else:
                sp.wait_ge(moe["x_added"], NT)
            load_wq(0)
            if lay == 0:
                for h in range(2):
                    for par in range(2):
                        for kb in range(2):
                            q0 = par * S + kb * QB
                            for t in range(PAIRS):
                                sp.dma_start(mask_i[q0:q0 + QB, h, t, :, :],
                                             mask0[h * 2 * PAIRS + 2 * t + par, :, kb * QB:(kb + 1) * QB].rearrange("(a q) k -> q a k", q=QB)).then_inc(c["mask_in"], 16)
            else:
                for par in range(2):
                    for kb in range(2):
                        q0 = par * S + kb * QB
                        sp.dma_start(mask1_sb[q0:q0 + QB, :, :],
                                     mask1[0, 0, :, kb * QB:(kb + 1) * QB].rearrange("(a q) k -> q a k", q=QB)).then_inc(c["mask_in"], 16)
                sp.dma_start(qk_in[:, 0:1], q_norm.unsqueeze(1)).then_inc(c["qk_in"], 16)
                sp.dma_start(qk_in[:, 1:2], k_norm.unsqueeze(1)).then_inc(c["qk_in"], 16)
            load_k(0, 0)
            load_k(0, 1)
            load_wo(0)
            load_v(0)
            wq_split(1)
            load_wq(1)
            sp.wait_ge(*c("scored", 1))
            load_k(1, 0)
            wq_split(2)
            load_wq(2)

            def steady(g, wq, k):
                wo_split(g)
                load_wo(g)
                sp.wait_ge(*c("scored", 2 * g))
                load_k(g, 1)
                if k:
                    sp.wait_ge(*c("scored", 2 * g + 1))
                    load_k(g + 1, 0)
                sp.wait_ge(*c("o_done", 8 * g))
                load_v(g)
                if wq:
                    wq_split(g + 2)
                    load_wq(g + 2)

            for g in range(1, G - 2):
                steady(g, True, True)
            steady(G - 2, False, True)
            steady(G - 1, False, False)

        def att_steps(eng, step):
            step(0, 0, True, False, False, False)
            step(0, 1, True, True, False, True)
            step(1, 0, True, True, True, False)
            step(1, 1, True, True, True, True)
            with eng.Fori(2, G - 1) as g:
                step(g, 0, True, True, True, False)
                step(g, 1, True, True, True, True)
            step(G - 1, 0, True, True, True, False)
            step(G - 1, 1, True, True, True, False)
            step(G, 0, False, True, True, False)
            step(G, 1, False, False, True, False)

        def att_pe(pe, lay):
            c = att[lay]

            def project(g, h, j):
                n = 4 * (2 * g + h) + j
                if h == 0:
                    ready = 4 * g + ((3, 4, 4, 4)[j] if lay else j + 1)
                    pe.wait_ge(*c("wq_hi", ready))
                    pe.wait_ge(*c("wq_lo", ready))
                if not (isinstance(g, int) and n < 2):
                    pe.wait_ge(*c("q_rot" if lay else "q_read", n - 1))
                for k in range(KC):
                    last = three(ps_q[j % 2][:, :], wq_hi[:, k, j * D:(j + 1) * D], wq_lo[:, k, j * D:(j + 1) * D],
                                 hT_hi[:, k, h * HALF:(h + 1) * HALF], hT_lo[:, k, h * HALF:(h + 1) * HALF], k == 0, k == KC - 1)
                last.then_inc(c["q_done"], 1)

            def square_sums(u, h):
                pe.wait_ge(*c("q_sq", 4 * u + 4))
                if not (isinstance(u, int) and u == 0):
                    pe.wait_ge(*c("s_scaled", u))
                for t in range(PAIRS):
                    for par in range(2):
                        b = (2 * t + par) * S
                        last = nc.tensor.matmul(ps_s[par * S:(par + 1) * S, t * JS:(t + 1) * JS], ones[:, :], q_sq[:, :, b:b + S],
                                                start=True, stop=True)
                last.then_inc(c["ssq"], 1)

            def score(u, h, g):
                pe.wait_ge(*c("q_rot", 4 * u + 4))
                pe.wait_ge(*c(f"k_in{h}", 16 * (g + 1)))
                if lay:
                    pe.wait_ge(*c("r_ln", u + 1))
                elif not (isinstance(u, int) and u == 0):
                    pe.wait_ge(*c("s_turned", u))
                for t in range(PAIRS):
                    for par in range(2):
                        b = (2 * t + par) * S
                        last = nc.tensor.matmul(ps_s[par * S:(par + 1) * S, t * JS:(t + 1) * JS], kT[:, h, b:b + S], qT[:, h, :, b:b + S],
                                                start=True, stop=True)
                last.then_inc(c["scored"], 1)

            def values(u, h, g):
                pe.wait_ge(*c("p_hi", u + 1))
                pe.wait_ge(*c("p_lo", u + 1))
                pe.wait_ge(*c("v_in", 32 * (g + 1)))
                if not (isinstance(u, int) and u == 0):
                    pe.wait_ge(*c("y_added", 4 * u))
                if lay and h == 0:
                    pe.wait_ge(*c("wo_hi", 4 * g + 4))
                    pe.wait_ge(*c("wo_lo", 4 * g + 4))
                for half in range(2):
                    for tt in range(2):
                        t = 2 * half + tt
                        cols = slice(t * JS, (t + 1) * JS)
                        for n, (v_part, p_part) in enumerate(((v_hi, p_hi), (v_hi, p_lo), (v_lo, p_hi))):
                            for par in range(2):
                                rows = slice(par * S, (par + 1) * S)
                                last = nc.tensor.matmul(ps_b[2 * half + par][:, tt * JS:(tt + 1) * JS], v_part[rows, h * PAIRS + t, :],
                                                        p_part[rows, cols], start=n == 0, stop=n == 2)
                                if tt == 1 and n == 2:
                                    last.then_inc(c["o_done"], 1)

            def project_out(u, h, g, t):
                if t % 2 == 0:
                    pe.wait_ge(*c("o_hi", 4 * u + t + 2))
                    pe.wait_ge(*c("o_lo", 4 * u + t + 2))
                if t == 0 and h == 0:
                    pe.wait_ge(*c("wo_hi", 4 * g + 4))
                    pe.wait_ge(*c("wo_lo", 4 * g + 4))
                for j in range(J):
                    last = three(ps_b[t][:, :], o_hi[:, t, j, :], o_lo[:, t, j, :], wo_hi[:, j, :], wo_lo[:, j, :], j == 0, j == J - 1)
                last.then_inc(c["y_done"], 1)

            def wo_turn(g):
                pe.wait_ge(*c("wo_in", 16 * (g + 1)))
                if not (isinstance(g, int) and g == 0):
                    pe.wait_ge(*c("y_added", 8 * g))
                for j in range(J):
                    for k in range(KC):
                        last = nc.tensor.transpose(ps_b[j][:, k * P:(k + 1) * P], wo_raw[:, k, j * D:(j + 1) * D], ident[:, :])
                    last.then_inc(c["wo_t"], 1)

            def wq_turn(g, j):
                if j == 0:
                    pe.wait_ge(*c("wq_in", 16 * (g + 1)))
                if j < 2 and not (isinstance(g, int) and g == 0):
                    pe.wait_ge(*c("q_rot", 8 * g - 1 + j))
                if j >= 2:
                    pe.wait_ge(*c("wq_lo", 4 * g + j - 1))
                for k in range(KC):
                    last = nc.tensor.transpose(ps_q[j % 2][:, k * P:(k + 1) * P], wq_raw[:, j, k * P:(k + 1) * P], ident[:, :])
                last.then_inc(c["wq_t"], 1)

            def step(g, h, do_project, do_score, do_finish, next_wq):
                us, up = 2 * g + h - 1, 2 * g + h - 2
                if do_score and lay:
                    square_sums(us, 1 - h)
                if do_project:
                    project(g, h, 0)
                if do_score:
                    score(us, 1 - h, g if h else g - 1)
                if lay and do_finish and h == 0:
                    wo_turn(g - 1)
                if do_project:
                    project(g, h, 1)
                    project(g, h, 2)
                if do_finish:
                    values(up, h, g - 1)
                if do_project:
                    project(g, h, 3)
                for t in range(PAIRS):
                    if lay and next_wq:
                        wq_turn(g + 1, t)
                    if do_finish:
                        project_out(up, h, g - 1, t)

            pe.wait_ge(*lns[2 * lay]("lo", NT))
            if lay:
                for j in range(J):
                    wq_turn(0, j)
            att_steps(pe, step)

        def att_act(act, lay):
            c = att[lay]

            def wq_high(g, j):
                if lay:
                    act.wait_ge(*c("wq_t", 4 * g + j + 1))
                    src = ps_q[j % 2].rearrange("p (k d) -> p k d", k=KC)
                else:
                    act.wait_ge(*c("wq_in", 16 * (g + 1)))
                    if not (isinstance(g, int) and g == 0):
                        act.wait_ge(*c("q_done", 8 * g - J + j + 1))
                    src = wq_raw[:, :, j * D:(j + 1) * D]
                nc.scalar.activation(wq_hi[:, :, j * D:(j + 1) * D], src, ACT.Copy).then_inc(c["wq_hi"], 1)

            def wo_high(g, j):
                if lay:
                    act.wait_ge(*c("wo_t", 4 * g + j + 1))
                    src = ps_b[j][:, :]
                else:
                    act.wait_ge(*c("wo_in", 16 * (g + 1)))
                    if not (isinstance(g, int) and g == 0):
                        act.wait_ge(*c("y_done", 8 * g))
                    src = wo_raw[:, j, :]
                nc.scalar.activation(wo_hi[:, j, :], src, ACT.Copy).then_inc(c["wo_hi"], 1)

            def queries(u, h, j):
                act.wait_ge(*c("q_done", 4 * u + j + 1))
                if j == 0 and not (isinstance(u, int) and u == 0):
                    act.wait_ge(*c("ssq", u))
                nc.scalar.activation(q_sq[:, j, :], ps_q[j % 2][:, :], ACT.Square).then_inc(c["q_sq"], 1)
                nc.scalar.activation(qT[:, h, j, :], ps_q[j % 2][:, :], ACT.Copy, scale=qk_w[:, 0:1]).then_inc(c["q_rot"], 1)

            def norms(u):
                act.wait_ge(*c("ssq", u + 1))
                nc.scalar.activation(r_ln[:, :], ps_s[:, :], ACT.Ln, bias=eps_rms[:, 0:1]).then_inc(c["r_ln"], 1)
                act.wait_ge(*c("r_ln", u + 1))
                if not (isinstance(u, int) and u == 0):
                    act.wait_ge(*c("s_scaled", u))
                nc.scalar.activation(r_q[:, :], r_ln[:, :], ACT.Exp, bias=zero_b[:, 0:1], scale=-0.5).then_inc(c["r_q"], 1)

            def exponentials(u):
                act.wait_ge(*c("s_shifted", u + 1))
                nc.scalar.activation(p_sb[:, :], s_sb[:, :], ACT.Exp, bias=zero_b[:, 0:1]).then_inc(c["p_exp"], 1)

            def probs_high(u):
                act.wait_ge(*c("p_turned", u + 1))
                if not (isinstance(u, int) and u == 0):
                    act.wait_ge(*c("o_done", 4 * u))
                nc.scalar.activation(p_hi[:, :], pT[:, :], ACT.Copy).then_inc(c["p_hi"], 1)

            def out_high(u, n):
                half, par = divmod(n, 2)
                act.wait_ge(*c("o_done", 4 * u + n + 1))
                nc.scalar.activation(o_hi[:, 2 * half:2 * half + 2, :, par * S:(par + 1) * S],
                                     ps_b[n].rearrange("p (t j q) -> p t j q", t=2, j=J), ACT.Copy).then_inc(c["o_hi"], 1)

            def step(g, h, do_project, do_score, do_finish, next_wq):
                uq, us, up = 2 * g + h, 2 * g + h - 1, 2 * g + h - 2
                if do_score and lay:
                    norms(us)
                if do_finish and h == 0 and lay == 0:
                    for j in range(J):
                        wo_high(g - 1, j)
                for j in range(J):
                    if j == 3 and do_finish:
                        for n in range(4):
                            out_high(up, n)
                    if do_project and lay:
                        queries(uq, h, j)
                    if next_wq and lay == 0 and j < 3:
                        wq_high(g + 1, j)
                    if j == 0 and do_finish and h == 0 and lay:
                        for jj in range(J):
                            wo_high(g - 1, jj)
                if next_wq and lay:
                    wq_high(g + 1, 0)
                if do_score:
                    exponentials(us)
                if next_wq:
                    for j in (1, 2) if lay else (3,):
                        wq_high(g + 1, j)
                if do_score:
                    probs_high(us)
                if next_wq and lay:
                    wq_high(g + 1, 3)

            if lay:
                act.wait_ge(*c("qk_w", 1))
            for j in range(J):
                wq_high(0, j)
            att_steps(act, step)

        def att_pool(pool, lay):
            c = att[lay]

            def wq_low(g, j):
                pool.wait_ge(*c("wq_hi", 4 * g + j + 1))
                nc.gpsimd.tensor_tensor(wq_lo[:, :, j * D:(j + 1) * D], wq_raw[:, :, j * D:(j + 1) * D],
                                        wq_hi[:, :, j * D:(j + 1) * D].bitcast(F32), ALU.subtract).then_inc(c["wq_lo"], 1)

            def wo_low(g, j):
                pool.wait_ge(*c("wo_hi", 4 * g + j + 1))
                nc.gpsimd.tensor_tensor(wo_lo[:, j, :], wo_raw[:, j, :], wo_hi[:, j, :].bitcast(F32), ALU.subtract).then_inc(c["wo_lo"], 1)

            def rotate(u, h, j):
                pool.wait_ge(*c("q_read", 4 * u + j + 1))
                nc.gpsimd.tensor_tensor(qT[:, h, j, :], q_t1[:, j % 2, :], q_t2[:, j % 2, :], ALU.add).then_inc(c["q_rot"], 1)

            def mask(u, h):
                sc = s_sb.rearrange("p (t j n) -> p t j n", t=PAIRS, j=J)
                if lay == 0:
                    pool.wait_ge(*c("s_kept", u + 1))
                    m = offset0[:, h, :, :, :].rearrange("p t a k -> p t (a k)").unsqueeze(2).to_broadcast([P, PAIRS, J, S])
                    last = nc.gpsimd.tensor_tensor(sc, sc, m, ALU.add)
                else:
                    pool.wait_ge(*c("s_turned", u + 1))
                    m = mask1_sb.rearrange("p a k -> p (a k)").unsqueeze(1).to_broadcast([P, PAIRS * J, S])
                    sc = s_sb.rearrange("p (n k) -> p n k", k=S)
                    last = nc.gpsimd.tensor_tensor(sc, sc, m, ALU.add)
                last.then_inc(c["s_masked"], 1)

            def shift(u):
                pool.wait_ge(*c("s_max", u + 1))
                sc = s_sb.rearrange("p (n k) -> p n k", k=QB)
                nc.gpsimd.tensor_tensor(sc, sc, wide(mx_c[:, :], QB), ALU.subtract).then_inc(c["s_shifted"], 1)

            def normalise(u):
                pool.wait_ge(*c("p_rec", u + 1))
                pr = p_sb.rearrange("p (n k) -> p n k", k=QB)
                nc.gpsimd.tensor_tensor(pr, pr, wide(p_rec[:, :], QB), ALU.mult).then_inc(c["p_normed"], 1)

            def probs_low(u):
                pool.wait_ge(*c("p_hi", u + 1))
                nc.gpsimd.tensor_tensor(p_lo[:, :], pT[:, :], p_hi[:, :].bitcast(F32), ALU.subtract).then_inc(c["p_lo"], 1)

            def step(g, h, do_project, do_score, do_finish, next_wq):
                uq, us = 2 * g + h, 2 * g + h - 1

                def added(j):
                    if do_project and lay == 0:
                        rotate(uq, h, j)

                def split(wo, wq):
                    if lay == 0:
                        for j in wo if do_finish and h == 0 else ():
                            wo_low(g - 1, j)
                        for j in wq if next_wq else ():
                            wq_low(g + 1, j)

                split((0, 1), ())
                added(0)
                split((2,), (0,))
                if do_score:
                    mask(us, 1 - h)
                added(1)
                added(2)
                split((3,), (1,))
                if do_score:
                    shift(us)
                added(3)
                split((), (2,))
                if do_score:
                    normalise(us)
                split((), (3,))
                if do_score:
                    probs_low(us)

            if lay == 0:
                for j in range(J):
                    wq_low(0, j)
                pool.wait_ge(*c("masks", 2))
            else:
                pool.wait_ge(*c("mask_in", 16 * 4))
            att_steps(pool, step)

        def att_dve(dve, lay):
            c = att[lay]

            def wq_low(g, j):
                dve.wait_ge(*c("wq_hi", 4 * g + j + 1))
                nc.vector.tensor_tensor(wq_lo[:, :, j * D:(j + 1) * D], ps_q[j % 2].rearrange("p (k d) -> p k d", k=KC),
                                        wq_hi[:, :, j * D:(j + 1) * D].bitcast(F32), ALU.subtract).then_inc(c["wq_lo"], 1)

            def wo_low(g, j):
                dve.wait_ge(*c("wo_hi", 4 * g + j + 1))
                nc.vector.tensor_tensor(wo_lo[:, j, :], ps_b[j][:, :], wo_hi[:, j, :].bitcast(F32), ALU.subtract).then_inc(c["wo_lo"], 1)

            def rotate(u, h, j):
                n = 4 * u + j
                dve.wait_ge(*c("q_done", n + 1))
                if not (isinstance(u, int) and n < 2):
                    dve.wait_ge(*c("q_rot", n - 1))
                tok = slice(h * HALF, (h + 1) * HALF)
                half = D // 2
                nc.vector.tensor_tensor(q_t1[:, j % 2, :], ps_q[j % 2][:, :], cos_q[:, tok], ALU.mult).then_inc(c["q_cos"], 1)
                nc.vector.tensor_tensor(q_t2[0:half, j % 2, :], ps_q[j % 2][half:D, :], sin_q[half:D, tok], ALU.mult).then_inc(c["q_cos"], 1)
                nc.vector.tensor_tensor(q_t2[half:D, j % 2, :], ps_q[j % 2][0:half, :], sin_q[0:half, tok], ALU.mult).then_inc(c["q_read"], 1)

            def turn_scores(u, h):
                dve.wait_ge(*c("scored", u + 1))
                src = ps_s[:, :]
                if lay:
                    dve.wait_ge(*c("r_q", u + 1))
                    nc.vector.tensor_tensor(s_raw[:, :], ps_s[:, :], r_q[:, :], ALU.mult).then_inc(c["s_scaled"], 1)
                    dve.wait_ge(*c("s_scaled", u + 1))
                    src = s_raw[:, :]
                nc.vector.transpose(s_sb[:, :], src).then_inc(c["s_turned"], 1)
                if lay == 0:
                    dve.wait_ge(*c("s_turned", u + 1))
                    sc = s_sb.rearrange("p (t j n) -> p t j n", t=PAIRS, j=J)
                    m = keep0[:, h, :, :, :].rearrange("p t a k -> p t (a k)").unsqueeze(2).to_broadcast([P, PAIRS, J, S])
                    nc.vector.tensor_tensor(sc, sc, m, ALU.mult).then_inc(c["s_kept"], 1)

            def across(dst, src):
                for k in range(4):
                    last = nc.vector.tensor_copy(dst[k * QB:(k + 1) * QB, :], src[(k ^ 1) * QB:((k ^ 1) + 1) * QB, :])
                return last

            def maxima(u):
                dve.wait_ge(*c("s_masked", u + 1))
                nc.vector.tensor_reduce(mx_a[:, :], s_sb.rearrange("p (n k) -> p n k", k=QB), AX, ALU.max).then_inc(c["mx_part"], 1)
                dve.wait_ge(*c("mx_part", u + 1))
                across(mx_b, mx_a).then_inc(c["mx_other"], 1)
                dve.wait_ge(*c("mx_other", u + 1))
                nc.vector.tensor_tensor(mx_c[:, :], mx_a[:, :], mx_b[:, :], ALU.max).then_inc(c["s_max"], 1)

            def sums(u):
                dve.wait_ge(*c("p_exp", u + 1))
                nc.vector.tensor_reduce(sm_a[:, :], p_sb.rearrange("p (n k) -> p n k", k=QB), AX, ALU.add).then_inc(c["sm_part"], 1)
                dve.wait_ge(*c("sm_part", u + 1))
                across(sm_b, sm_a).then_inc(c["sm_other"], 1)
                dve.wait_ge(*c("sm_other", u + 1))
                nc.vector.tensor_tensor(sm_c[:, :], sm_a[:, :], sm_b[:, :], ALU.add).then_inc(c["sm_all"], 1)
                dve.wait_ge(*c("sm_all", u + 1))
                nc.vector.reciprocal(p_rec[:, :], sm_c[:, :]).then_inc(c["p_rec"], 1)

            def turn_probs(u):
                dve.wait_ge(*c("p_normed", u + 1))
                nc.vector.transpose(pT[:, :], p_sb[:, :]).then_inc(c["p_turned"], 1)

            def out_low(u, n):
                half, par = divmod(n, 2)
                dve.wait_ge(*c("o_hi", 4 * u + n + 1))
                part = (slice(None), slice(2 * half, 2 * half + 2), slice(None), slice(par * S, (par + 1) * S))
                nc.vector.tensor_tensor(o_lo[part], ps_b[n].rearrange("p (t j q) -> p t j q", t=2, j=J),
                                        o_hi[part].bitcast(F32), ALU.subtract).then_inc(c["o_lo"], 1)

            def add_output(u, h, t):
                n = 4 * u + t
                dve.wait_ge(*c("y_done", n + 1))
                if not (isinstance(u, int) and u == 0):
                    dve.wait_ge(*c("y_added", 4 * u))
                i = h * PAIRS + t
                nc.vector.scalar_tensor_tensor(x_sb[:, i, :], ps_b[t][:, :], gates[:, lay:lay + 1], x_sb[:, i, :],
                                               ALU.mult, ALU.add).then_inc(c["y_added"], 1)

            def step(g, h, do_project, do_score, do_finish, next_wq):
                uq, us, up = 2 * g + h, 2 * g + h - 1, 2 * g + h - 2

                def rotated(j):
                    if do_project and lay == 0:
                        rotate(uq, h, j)

                def end(t):
                    if next_wq and lay:
                        wq_low(g + 1, t)
                    if do_finish:
                        add_output(up, h, t)

                rotated(0)
                if do_score:
                    turn_scores(us, 1 - h)
                if do_finish and lay and h == 0:
                    for j in range(J):
                        wo_low(g - 1, j)
                rotated(1)
                rotated(2)
                if do_finish:
                    out_low(up, 0)
                    out_low(up, 1)
                if do_score:
                    maxima(us)
                if do_finish:
                    out_low(up, 2)
                    out_low(up, 3)
                rotated(3)
                end(0)
                if do_score:
                    sums(us)
                end(1)
                end(2)
                if do_score:
                    turn_probs(us)
                end(3)

            if lay == 0:
                dve.wait_ge(*c("mask_in", 16 * 4 * 2 * PAIRS))
                nc.vector.tensor_scalar(keep0[:, :], mask_i[:, :], 0.0, None, ALU.not_equal).then_inc(c["masks"], 1)
                nc.vector.tensor_scalar(offset0[:, :], mask_i[:, :], 0.0, MASKED, ALU.is_equal, ALU.mult).then_inc(c["masks"], 1)
                dve.wait_ge(*c("masks", 2))
            else:
                dve.wait_ge(*c("qk_in", 32))
                nc.vector.tensor_tensor(qk_w[:, :], qk_in[:, 0:1], qk_in[:, 1:2], ALU.mult).then_inc(c["qk_w"], 1)
                for j in range(J):
                    wq_low(0, j)
            att_steps(dve, step)

        def moe_sync(sp):
            c = moe
            sp.wait_ge(*att[0]("y_added", 2 * G * PAIRS))
            sp.dma_start(r_raw[:, :], gate_w).then_inc(c["r_in"], 16)
            sp.dma_start(g_raw[:, :, :], glu_w.rearrange("(n p) e -> p n e", p=P)).then_inc(c["g_in"], 16)
            sp.dma_start(u_raw[:, :, :], up_w.rearrange("(n p) e -> p n e", p=P)).then_inc(c["u_in"], 16)
            sp.dma_start(d_raw[:, :, :], down_w.rearrange("(k p) n -> p k n", p=P)).then_inc(c["d_in"], 16)

        turns = [("r", 0)] + [(w, n) for w in "gud" for n in range(FT)]

        def turned(w, n):
            bank = ps_b[turns.index((w, n)) % 2]
            view = bank.rearrange("p (k i) -> p k i", k=KC)
            if w == "r":
                return rT_hi[:, :, 0:NX], rT_lo[:, :, 0:NX], view[:, :, 0:NX]
            if w == "d":
                return dT_hi[:, n, :], dT_lo[:, n, :], bank[:, :]
            hi, lo = {"g": (gT_hi, gT_lo), "u": (uT_hi, uT_lo)}[w]
            return hi[:, :, n * P:(n + 1) * P], lo[:, :, n * P:(n + 1) * P], view

        def moe_pe(pe):
            c = moe
            for m, (w, n) in enumerate(turns):
                if n == 0:
                    pe.wait_ge(c[f"{w}_in"], 16)
                if m >= 2:
                    pe.wait_ge(c["w_lo"], m - 1)
                for k in range(KC):
                    if w == "r":
                        last = nc.tensor.transpose(ps_b[m % 2][:, k * P:k * P + NX], r_raw[:, k * P:(k + 1) * P], ident[0:NX, 0:NX])
                    elif w == "d":
                        last = nc.tensor.transpose(ps_b[m % 2][:, k * P:(k + 1) * P], d_raw[:, k, n * P:(n + 1) * P], ident[:, :])
                    else:
                        raw = {"g": g_raw, "u": u_raw}[w]
                        last = nc.tensor.transpose(ps_b[m % 2][:, k * P:(k + 1) * P], raw[:, n, k * P:(k + 1) * P], ident[:, :])
                last.then_inc(c["w_t"], 1)
            pe.wait_ge(*lns[1]("lo", NT))
            pe.wait_ge(c["w_lo"], len(turns))
            pe.wait_ge(c["r_zero"], 2)
            for h in range(2):
                for k in range(KC):
                    last = three(ps_q[h][:, :], rT_hi[:, k, :], rT_lo[:, k, :], hT_hi[:, k, h * HALF:(h + 1) * HALF],
                                 hT_lo[:, k, h * HALF:(h + 1) * HALF], k == 0, k == KC - 1)
                last.then_inc(c["logits"], 1)
            for i in range(NT):
                if i % PAIRS == 0:
                    pe.wait_ge(c["lgT"], i // PAIRS + 1)
                last = nc.tensor.transpose(ps_h[0][:, i * NX:(i + 1) * NX], x_lgT[:, i * P:(i + 1) * P], ident[0:NX, 0:NX])
            last.then_inc(c["lg_t"], 1)

            def up(i, r, half):
                if half == 0:
                    pe.wait_ge(c["f_hi"], i + 1)
                    pe.wait_ge(c["f_lo"], i + 1)
                if not (isinstance(i, int) and i == 0):
                    pe.wait_ge(c["gu"], 2 * i + half - 1)
                for bank, hi, lo, name in ((ps_q[half], gT_hi, gT_lo, "g_done"), (ps_b[half], uT_hi, uT_lo, "u_done")):
                    for k in range(KC):
                        last = three(bank[:, 0:FH], f_hi[:, r, k, :], f_lo[:, r, k, :], hi[:, k, half * FH:(half + 1) * FH],
                                     lo[:, k, half * FH:(half + 1) * FH], k == 0, k == KC - 1)
                    last.then_inc(c[name], 1)

            def hidden_t(i):
                pe.wait_ge(c["hid"], 2 * i + 2)
                if not (isinstance(i, int) and i == 0):
                    pe.wait_ge(c["hdT_lo"], 2 * i)
                for n in range(FT):
                    last = nc.tensor.transpose(ps_h[n // 4][:, (n % 4) * P:(n % 4 + 1) * P], hid[:, n * P:(n + 1) * P], ident[:, :])
                last.then_inc(c["hid_t"], 1)

            def down(i, r):
                pe.wait_ge(c["hdT_lo"], 2 * i + 2)
                if not (isinstance(i, int) and i < 2):
                    pe.wait_ge(c["x_added"], i - 1)
                for n in range(FT):
                    last = three(ps_b[2 + r][:, :], hdT_hi[:, n, :], hdT_lo[:, n, :], dT_hi[:, n, :], dT_lo[:, n, :], n == 0, n == FT - 1)
                last.then_inc(c["down"], 1)

            def tile(i, r, before):
                up(i, r, 0)
                if before:
                    hidden_t(i - 1)
                up(i, r, 1)
                if before:
                    down(i - 1, 1 - r)

            pe.wait_ge(c["x_lg"], 1)
            tile(0, 0, False)
            tile(1, 1, True)
            tile(2, 0, True)
            with pe.Fori(1, NT // 2 - 1) as m:
                tile(2 * m + 1, 1, True)
                tile(2 * m + 2, 0, True)
            tile(NT - 1, 1, True)
            hidden_t(NT - 1)
            down(NT - 1, 1)

        def moe_act(act):
            c = moe
            for m, (w, n) in enumerate(turns):
                act.wait_ge(c["w_t"], m + 1)
                hi, lo, src = turned(w, n)
                nc.scalar.activation(hi, src, ACT.Copy).then_inc(c["w_hi"], 1)
            for h in range(2):
                act.wait_ge(c["logits"], h + 1)
                nc.scalar.activation(x_lgT[:, h * HALF:(h + 1) * HALF], ps_q[h][0:NX, :], ACT.Copy).then_inc(c["lgT"], 1)
            act.wait_ge(c["x_lg"], 1)
            nc.scalar.activation(x_ex[:, :, :], x_lg[:, :, :], ACT.Exp, bias=zero_b[:, 0:1]).then_inc(c["x_ex"], 1)

            def silu(i, half):
                act.wait_ge(c["g_done"], 2 * i + half + 1)
                if not (isinstance(i, int) and i == 0):
                    act.wait_ge(c["gu"], 2 * i + half - 1)
                nc.scalar.activation(sg[:, half, :], ps_q[half][:, 0:FH], ACT.Silu, bias=zero_b[:, 0:1]).then_inc(c["silu"], 1)

            def tokens(i, r):
                if not (isinstance(i, int) and i < 2):
                    act.wait_ge(c["u_done"], 2 * i - 2)
                nc.scalar.activation(f_hi[:, r, :, :], hT_hi[:, :, bass.ts(i, P)].bitcast(F32), ACT.Copy).then_inc(c["f_hi"], 1)

            def hidden_hi(i):
                for b, (n0, n1) in enumerate(((0, 4), (4, FT))):
                    act.wait_ge(c["hid_t"], i + 1)
                    if not (isinstance(i, int) and i == 0):
                        act.wait_ge(c["down"], i)
                    nc.scalar.activation(hdT_hi[:, n0:n1, :], ps_h[b][:, 0:(n1 - n0) * P].rearrange("p (n t) -> p n t", t=P),
                                         ACT.Copy).then_inc(c["hdT_hi"], 1)

            def tile(i, r, before, after):
                if after:
                    tokens(i + 1, 1 - r)
                silu(i, 0)
                if before:
                    hidden_hi(i - 1)
                silu(i, 1)

            tokens(0, 0)
            tile(0, 0, False, True)
            tile(1, 1, True, True)
            tile(2, 0, True, True)
            with act.Fori(1, NT // 2 - 1) as m:
                tile(2 * m + 1, 1, True, True)
                tile(2 * m + 2, 0, True, True)
            tile(NT - 1, 1, True, False)
            hidden_hi(NT - 1)

        def moe_pool(pool):
            c = moe
            pool.wait_ge(*att[0]("y_added", 2 * G * PAIRS))
            nc.gpsimd.memset(x_top[:, :, :], -1.0).then_inc(c["top_clear"], 1)

            def tokens(i, r):
                if not (isinstance(i, int) and i < 2):
                    pool.wait_ge(c["u_done"], 2 * i - 2)
                nc.gpsimd.tensor_copy(f_lo[:, r, :, :], hT_lo[:, :, bass.ts(i, P)].bitcast(F32)).then_inc(c["f_lo"], 1)

            def weigh(i, half):
                pool.wait_ge(c["gu"], 2 * i + half + 1)
                if not (isinstance(i, int) and i == 0):
                    pool.wait_ge(c["hid_t"], i)
                w = x_w[:, bass.ds(i, 1), half * XH:(half + 1) * XH].rearrange("p o e -> p (o e)")
                nc.gpsimd.tensor_tensor(hid[:, half * FH:(half + 1) * FH].rearrange("p (e n) -> p e n", e=XH),
                                        gu[:, half, :].rearrange("p (e n) -> p e n", e=XH), wide(w, INTER), ALU.mult).then_inc(c["hid"], 1)

            def tile(i, r, after):
                if after:
                    tokens(i + 1, 1 - r)
                weigh(i, 0)
                weigh(i, 1)

            pool.wait_ge(c["w_lo"], len(turns))
            pool.wait_ge(*lns[1]("lo", NT))
            tokens(0, 0)
            pool.wait_ge(c["x_w"], 1)
            tile(0, 0, True)
            tile(1, 1, True)
            tile(2, 0, True)
            with pool.Fori(1, NT // 2 - 1) as m:
                tile(2 * m + 1, 1, True)
                tile(2 * m + 2, 0, True)
            tile(NT - 1, 1, False)

        def moe_dve(dve):
            c = moe
            dve.wait_ge(*att[0]("y_added", 2 * G * PAIRS))
            nc.vector.memset(rT_hi[:, :, NX:P].bitcast(F32), 0.0).then_inc(c["r_zero"], 1)
            nc.vector.memset(rT_lo[:, :, NX:P].bitcast(F32), 0.0).then_inc(c["r_zero"], 1)
            for m, (w, n) in enumerate(turns):
                dve.wait_ge(c["w_hi"], m + 1)
                hi, lo, src = turned(w, n)
                nc.vector.tensor_tensor(lo, src, hi.bitcast(F32), ALU.subtract).then_inc(c["w_lo"], 1)
            lg = ps_h[0][:, 0:NT * NX].rearrange("p (i e) -> p i e", e=NX)
            dve.wait_ge(c["lg_t"], 1)
            nc.vector.tensor_reduce(x_mx[:, :], lg, AX, ALU.max).then_inc(c["route"], 1)
            dve.wait_ge(c["route"], 1)
            nc.vector.tensor_tensor(x_lg[:, :, :], lg, wide(x_mx[:, :], NX), ALU.subtract).then_inc(c["x_lg"], 1)
            dve.wait_ge(c["x_ex"], 1)
            nc.vector.tensor_reduce(x_sum[:, :], x_ex[:, :, :], AX, ALU.add).then_inc(c["route"], 1)
            dve.wait_ge(c["route"], 2)
            nc.vector.reciprocal(x_rec[:, :], x_sum[:, :]).then_inc(c["route"], 1)
            dve.wait_ge(c["route"], 3)
            nc.vector.tensor_tensor(x_p[:, :, :], x_ex[:, :, :], wide(x_rec[:, :], NX), ALU.mult).then_inc(c["route"], 1)
            dve.wait_ge(c["route"], 4)
            for i in range(NT):
                nc.vector.max(x_rep[:, i, 0:8], x_p[:, i, :]).then_inc(c["route"], 1)
            dve.wait_ge(c["route"], 4 + NT)
            dve.wait_ge(c["top_clear"], 1)
            nc.vector.tensor_copy(x_top[:, :, 0:2], x_rep[:, :, 0:2]).then_inc(c["route"], 1)
            nc.vector.tensor_tensor(x_two[:, :], x_rep[:, :, 0], x_rep[:, :, 1], ALU.add).then_inc(c["route"], 1)
            dve.wait_ge(c["route"], 6 + NT)
            nc.vector.reciprocal(x_rec[:, :], x_two[:, :]).then_inc(c["route"], 1)
            for i in range(NT):
                nc.vector.match_replace(x_rep[:, i, :], x_top[:, i, :], x_p[:, i, :], -1.0).then_inc(c["route"], 1)
            dve.wait_ge(c["route"], 7 + 2 * NT)
            nc.vector.tensor_scalar(x_rep[:, :, :], x_rep[:, :, :], 0.0, None, ALU.max).then_inc(c["route"], 1)
            dve.wait_ge(c["route"], 8 + 2 * NT)
            nc.vector.tensor_tensor(x_p[:, :, :], x_p[:, :, :], x_rep[:, :, :], ALU.subtract).then_inc(c["route"], 1)
            dve.wait_ge(c["route"], 9 + 2 * NT)
            nc.vector.tensor_tensor(x_w[:, :, :], x_p[:, :, :], wide(x_rec[:, :], NX), ALU.mult).then_inc(c["x_w"], 1)

            def gated(i, half):
                dve.wait_ge(c["silu"], 2 * i + half + 1)
                dve.wait_ge(c["u_done"], 2 * i + half + 1)
                if not (isinstance(i, int) and i == 0):
                    dve.wait_ge(c["hid"], 2 * i + half - 1)
                nc.vector.tensor_tensor(gu[:, half, :], ps_b[half][:, 0:FH], sg[:, half, :], ALU.mult).then_inc(c["gu"], 1)

            def hidden_lo(i):
                for b, (n0, n1) in enumerate(((0, 4), (4, FT))):
                    dve.wait_ge(c["hdT_hi"], 2 * i + b + 1)
                    nc.vector.tensor_tensor(hdT_lo[:, n0:n1, :], ps_h[b][:, 0:(n1 - n0) * P].rearrange("p (n t) -> p n t", t=P),
                                            hdT_hi[:, n0:n1, :].bitcast(F32), ALU.subtract).then_inc(c["hdT_lo"], 1)

            def add_output(i, r):
                dve.wait_ge(c["down"], i + 1)
                xi = x_sb[:, bass.ds(i, 1), :].rearrange("p o e -> p (o e)")
                nc.vector.scalar_tensor_tensor(xi, ps_b[2 + r][:, :], gates[:, 2:3], xi, ALU.mult, ALU.add).then_inc(c["x_added"], 1)

            def tile(i, r, before):
                gated(i, 0)
                if before:
                    hidden_lo(i - 1)
                gated(i, 1)
                if before:
                    add_output(i - 1, 1 - r)

            tile(0, 0, False)
            tile(1, 1, True)
            tile(2, 0, True)
            with dve.Fori(1, NT // 2 - 1) as m:
                tile(2 * m + 1, 1, True)
                tile(2 * m + 2, 0, True)
            tile(NT - 1, 1, True)
            hidden_lo(NT - 1)
            add_output(NT - 1, 1)

        def lora_sync(sp):
            c = lora
            sp.wait_ge(*att[1]("y_added", 2 * G * PAIRS))
            sp.dma_start(a_raw[0:LM, :], lora_a.rearrange("e r f -> (e r) f")).then_inc(c["a_in"], 16)
            sp.dma_start(a_raw[LM:LM + LX, :], lora_r).then_inc(c["a_in"], 16)
            for e in range(LX):
                sp.dma_start(b_raw[:, :, e, :], lora_b[e].rearrange("(n p) r -> p n r", p=P)).then_inc(c["b_in"], 16)
            for i in range(NT):
                sp.wait_ge(c["x_added"], i + 1)
                sp.dma_start(ot[:, i, :], x_sb[:, i, :]).then_inc(c["out"], 16)
            sp.wait_ge(c["out"], 16 * NT)

        def lora_pe(pe):
            c = lora
            n = LM + LX
            pe.wait_ge(c["a_in"], 32)
            for k in range(KC):
                last = nc.tensor.transpose(ps_b[0][:, k * P:k * P + n], a_raw[:, k * P:(k + 1) * P], ident[0:n, 0:n])
            last.then_inc(c["w_t"], 1)
            pe.wait_ge(c["b_in"], 16 * LX)
            for k in range(LO // P):
                last = nc.tensor.transpose(ps_b[1][0:LM, k * P:(k + 1) * P], b_raw[:, k, :, :].rearrange("p e r -> p (e r)"), ident[:, :])
            last.then_inc(c["w_t"], 1)
            pe.wait_ge(*lns[3]("lo", NT))
            pe.wait_ge(c["w_lo"], 2)
            pe.wait_ge(c["a_zero"], 2)
            for h in range(2):
                for k in range(KC):
                    last = three(ps_q[h][:, :], aT_hi[:, k, :], aT_lo[:, k, :], hT_hi[:, k, h * HALF:(h + 1) * HALF],
                                 hT_lo[:, k, h * HALF:(h + 1) * HALF], k == 0, k == KC - 1)
                last.then_inc(c["mid"], 1)
            for i in range(NT):
                if i % PAIRS == 0:
                    pe.wait_ge(c["m_T"], i // PAIRS + 1)
                last = nc.tensor.transpose(ps_h[i // PAIRS][:, (i % PAIRS) * P:(i % PAIRS) * P + n], m_T[:, i * P:(i + 1) * P], ident[0:n, 0:n])
                if i % PAIRS == PAIRS - 1:
                    last.then_inc(c["mid_t"], 1)
            for i in range(NT):
                pe.wait_ge(c["gated"], i // PAIRS + 1)
                last = nc.tensor.transpose(ps_q[i // PAIRS][0:LM, (i % PAIRS) * P:(i % PAIRS + 1) * P],
                                           l_m[:, i, :, :].rearrange("p e r -> p (e r)"), ident[:, :])
                if i % PAIRS == PAIRS - 1:
                    last.then_inc(c["gated_t"], 1)
            for i in range(NT):
                pe.wait_ge(c["mT_lo"], i // PAIRS + 1)
                if i >= 4:
                    pe.wait_ge(c["x_added"], i - 3)
                three(ps_b[i % 4][:, :], mT_hi[:, i * P:(i + 1) * P], mT_lo[:, i * P:(i + 1) * P], bT_hi[:, :], bT_lo[:, :],
                      True, True).then_inc(c["delta"], 1)

        def lora_act(act):
            c = lora
            n = LM + LX
            act.wait_ge(c["w_t"], 1)
            nc.scalar.activation(aT_hi[:, :, 0:n], ps_b[0].rearrange("p (k i) -> p k i", k=KC)[:, :, 0:n], ACT.Copy).then_inc(c["w_hi"], 1)
            act.wait_ge(c["w_t"], 2)
            nc.scalar.activation(bT_hi[:, :], ps_b[1][0:LM, :], ACT.Copy, scale=LORA_SCALE).then_inc(c["w_hi"], 1)
            for h in range(2):
                act.wait_ge(c["mid"], h + 1)
                nc.scalar.activation(m_T[:, h * HALF:(h + 1) * HALF], ps_q[h][0:n, :], ACT.Copy).then_inc(c["m_T"], 1)
            act.wait_ge(c["l_lg"], 2)
            nc.scalar.activation(l_ex[:, :, :], l_lg[:, :, 0:LX], ACT.Exp, bias=zero_b[:, 0:1]).then_inc(c["l_ex"], 1)
            for h in range(2):
                act.wait_ge(c["gated_t"], h + 1)
                nc.scalar.activation(mT_hi[:, h * HALF:(h + 1) * HALF], ps_q[h][0:LM, :], ACT.Copy).then_inc(c["mT_hi"], 1)

        def lora_dve(dve):
            c = lora
            n = LM + LX
            hn = PAIRS
            dve.wait_ge(*att[1]("y_added", 2 * G * PAIRS))
            nc.vector.memset(aT_hi[:, :, n:P].bitcast(F32), 0.0).then_inc(c["a_zero"], 1)
            nc.vector.memset(aT_lo[:, :, n:P].bitcast(F32), 0.0).then_inc(c["a_zero"], 1)
            nc.vector.memset(l_lg[:, :, :], -BIG).then_inc(c["route"], 1)
            nc.vector.memset(l_top[:, :, :], NO_MATCH).then_inc(c["route"], 1)
            dve.wait_ge(c["w_hi"], 1)
            nc.vector.tensor_tensor(aT_lo[:, :, 0:n], ps_b[0].rearrange("p (k i) -> p k i", k=KC)[:, :, 0:n], aT_hi[:, :, 0:n].bitcast(F32),
                                    ALU.subtract).then_inc(c["w_lo"], 1)
            dve.wait_ge(c["w_hi"], 2)
            nc.vector.scalar_tensor_tensor(bT_lo[:, :], ps_b[1][0:LM, :], LORA_SCALE, bT_hi[:, :].bitcast(F32), ALU.mult, ALU.subtract).then_inc(c["w_lo"], 1)
            mid = [b.rearrange("p (i m) -> p i m", m=P) for b in ps_h]
            dve.wait_ge(c["route"], 2)
            for h in range(2):
                dve.wait_ge(c["mid_t"], h + 1)
                nc.vector.tensor_copy(l_lg[:, h * hn:(h + 1) * hn, 0:LX], mid[h][:, :, LM:n]).then_inc(c["route"], 1)
            dve.wait_ge(c["route"], 4)
            for i in range(NT):
                nc.vector.max(l_rep[:, i, :], l_lg[:, i, :]).then_inc(c["route"], 1)
            dve.wait_ge(c["route"], 4 + NT)
            nc.vector.tensor_copy(l_top[:, :, 0:2], l_rep[:, :, 0:2]).then_inc(c["route"], 1)
            nc.vector.tensor_copy(l_mx[:, :], l_rep[:, :, 0]).then_inc(c["route"], 1)
            dve.wait_ge(c["route"], 6 + NT)
            for i in range(NT):
                nc.vector.match_replace(l_rep[:, i, :], l_top[:, i, :], l_lg[:, i, :], TAKEN).then_inc(c["route"], 1)
            dve.wait_ge(c["route"], 6 + 2 * NT)
            nc.vector.tensor_scalar(l_rep[:, :, :], l_rep[:, :, :], TAKEN, -BIG, ALU.is_lt, ALU.mult).then_inc(c["route"], 1)
            nc.vector.tensor_tensor(l_lg[:, :, 0:LX], l_lg[:, :, 0:LX], wide(l_mx[:, :], LX), ALU.subtract).then_inc(c["l_lg"], 1)
            dve.wait_ge(c["route"], 7 + 2 * NT)
            dve.wait_ge(c["l_lg"], 1)
            nc.vector.tensor_tensor(l_lg[:, :, 0:LX], l_lg[:, :, 0:LX], l_rep[:, :, 0:LX], ALU.add).then_inc(c["l_lg"], 1)
            dve.wait_ge(c["l_ex"], 1)
            nc.vector.tensor_reduce(l_sum[:, :], l_ex[:, :, :], AX, ALU.add).then_inc(c["route"], 1)
            dve.wait_ge(c["route"], 8 + 2 * NT)
            nc.vector.reciprocal(l_rec[:, :], l_sum[:, :]).then_inc(c["route"], 1)
            dve.wait_ge(c["route"], 9 + 2 * NT)
            nc.vector.tensor_tensor(l_ex[:, :, :], l_ex[:, :, :], wide(l_rec[:, :], LX), ALU.mult).then_inc(c["route"], 1)
            dve.wait_ge(c["route"], 10 + 2 * NT)
            for h in range(2):
                own = slice(h * hn, (h + 1) * hn)
                for e in range(LX):
                    last = nc.vector.tensor_tensor(l_m[:, own, e, :], mid[h][:, :, e * LR:(e + 1) * LR], wide(l_ex[:, own, e], LR), ALU.mult)
                last.then_inc(c["gated"], 1)
            for h in range(2):
                dve.wait_ge(c["mT_hi"], h + 1)
                nc.vector.tensor_tensor(mT_lo[:, h * HALF:(h + 1) * HALF], ps_q[h][0:LM, :], mT_hi[:, h * HALF:(h + 1) * HALF].bitcast(F32),
                                        ALU.subtract).then_inc(c["mT_lo"], 1)
            for i in range(NT):
                dve.wait_ge(c["delta"], i + 1)
                nc.vector.scalar_tensor_tensor(x_sb[:, i, :], ps_b[i % 4][:, :], gates[:, 3:4], x_sb[:, i, :], ALU.mult, ALU.add).then_inc(c["x_added"], 1)

        @block.sync
        def _(sp):
            prep_sync(sp)
            kv_sync(sp)
            att_sync(sp, 0)
            moe_sync(sp)
            att_sync(sp, 1)
            lora_sync(sp)

        @block.gpsimd
        def _(pool):
            prep_pool(pool)
            kv_pool(pool)
            att_pool(pool, 0)
            moe_pool(pool)
            att_pool(pool, 1)

        @block.scalar
        def _(act):
            act.wait_ge(prep["consts"], 4)
            act.wait_ge(prep["gates_in"], 32)
            nc.scalar.activation(gates[:, :], gates_in[:, :], ACT.Tanh, bias=zero_b[:, 0:1]).then_inc(prep["gates"], 1)
            prep_act(act)
            ln_act_sd(act, lns[0])
            kv_act(act)
            ln_act(act, lns[0])
            att_act(act, 0)
            ln_act_sd(act, lns[1])
            ln_act(act, lns[1])
            moe_act(act)
            ln_act_sd(act, lns[2])
            ln_act(act, lns[2])
            att_act(act, 1)
            ln_act_sd(act, lns[3])
            ln_act(act, lns[3])
            lora_act(act)

        @block.tensor
        def _(pe):
            prep_pe(pe)
            kv_pe(pe)
            ln_pe(pe, lns[0])
            att_pe(pe, 0)
            ln_pe(pe, lns[1])
            moe_pe(pe)
            ln_pe(pe, lns[2])
            att_pe(pe, 1)
            ln_pe(pe, lns[3])
            lora_pe(pe)

        @block.vector
        def _(dve):
            prep_dve(dve)
            ln_stats_dve(dve, lns[0], lambda i: (prep["x"], 16))
            kv_dve(dve)
            ln_apply_dve(dve, lns[0])
            att_dve(dve, 0)
            ln_stats_dve(dve, lns[1], lambda i: att[0]("y_added", 2 * (G - 1) * PAIRS + i + 1))
            ln_apply_dve(dve, lns[1])
            moe_dve(dve)
            ln_stats_dve(dve, lns[2], lambda i: (moe["x_added"], i + 1))
            ln_apply_dve(dve, lns[2])
            att_dve(dve, 1)
            ln_stats_dve(dve, lns[3], lambda i: att[1]("y_added", 2 * (G - 1) * PAIRS + i + 1))
            ln_apply_dve(dve, lns[3])
            lora_dve(dve)


_INS = ["x", "ctx_4096", "pos_BxS2", "mask_BxSxS2_ik0", "mask_1x1xSxS2_ff0", "g_xattn", "g_ffn", "L0_xattn_Wq", "L0_xattn_Wk",
        "L0_xattn_Wv", "L0_xattn_Wo", "L0_ffn_gate_w", "L0_ffn_u", "L0_ffn_g", "L0_ffn_d", "L1_xattn_Wq", "L1_xattn_Wk", "L1_xattn_Wv",
        "L1_xattn_Wo", "L1_xattn_q_norm_w", "L1_xattn_k_norm_w", "L1_ffn_A", "L1_ffn_B", "L1_ffn_Wr"]


def kernel(**inputs):
    import concourse.bacc as bacc
    from concourse.bass_utils import run_bass_kernel_spmd

    nc = bacc.Bacc("TRN2", target_bir_lowering=False, num_devices=1)
    arrays, args = {}, []
    for name in _INS:
        a = np.ascontiguousarray(inputs[name])
        arrays[f"in_{name}"] = a
        args.append(nc.dram_tensor(f"in_{name}", a.shape, mybir.dt.from_np(a.dtype), kind="ExternalInput").ap())
    table = rope_constants()
    arrays["rope_constants"] = table
    args.append(nc.dram_tensor("rope_constants", table.shape, F32, kind="ExternalInput").ap())
    args.append(nc.dram_tensor("out", (B, S, E), F32, kind="ExternalOutput").ap())
    build(nc, *args)
    r = run_bass_kernel_spmd(nc, [arrays], core_ids=[0])
    return r.results[0]["out"]
```

```python
from contextlib import ExitStack

import concourse.bass as bass
import numpy as np
from concourse import mybir

P = 128
B, S, E = 16, 64, 512
T = B * S
NT = T // P
KC = E // P
H, G, D = 32, 8, 128
J = H // G
GB = 4
NB = G // GB
BW = GB * D
HALF = T // 2
PAIRS = NT // 2
JS = J * S
SC = PAIRS * JS
QB = 32
NQ = SC // QB
MAX_POS, THETA = 512, 10000.0
NX, INTER = 16, 56
FI = NX * INTER
FT = FI // P
FH = FI // 2
XH = NX // 2
LX, LR, LO = 4, 16, 512
LM = LX * LR
LORA_SCALE = 16.0 / float(np.sqrt(16.0))
EPS = 1e-5
MASKED = -1000000000.0
BIG = 3.0e38
TAKEN, NO_MATCH = 3.3e38, 3.2e38

F32 = mybir.dt.float32
FR = mybir.dt.float32r
I32 = mybir.dt.int32
ALU = mybir.AluOpType
ACT = mybir.ActivationFunctionType
AX = mybir.AxisListType.X


def rope_constants():
    inv = np.float32(1.0) / np.float32(THETA) ** (np.arange(0, D, 2, dtype=np.float32) / np.float32(D))
    ang = np.arange(MAX_POS, dtype=np.float32)[:, None] * inv.astype(np.float32)[None, :]
    c, s = np.cos(ang).astype(np.float32), np.sin(ang).astype(np.float32)
    q = np.float32(1.0 / np.sqrt(D))
    return np.concatenate([c * q, c * q, s * q, -s * q], axis=1), np.concatenate([c, s], axis=1)


def build(nc, x, ctx_in, pos, mask0, mask1, g_xattn, g_ffn, Wq0, Wk0, Wv0, Wo0, gate_w, up_w, glu_w, down_w,
          Wq1, Wk1, Wv1, Wo1, q_norm, k_norm, lora_a, lora_b, lora_r, rope_q_table, rope_k_table, out):
    stack = ExitStack()

    class Stage:

        def __init__(self, name, again=None, earlier=None):
            self.name, self.made, self.earlier = name, again.made if again else {}, earlier or {}

        def __getitem__(self, what):
            if what not in self.made:
                self.made[what] = stack.enter_context(nc.semaphore(f"{self.name}_{what}"))
            return self.made[what]

        def __call__(self, what, n):
            return self[what], n + self.earlier.get(what, 0)

    def alloc(where, *buffers):
        return [where.enter_context(nc.sbuf_tensor(n, shape, dt)) for n, shape, dt in buffers]

    with stack:
        ps_q = [stack.enter_context(nc.psum_tensor(f"ps_q{i}", [P, 512], F32)) for i in range(2)]
        ps_s = stack.enter_context(nc.psum_tensor("ps_s", [P, SC], F32))
        ps_b = [stack.enter_context(nc.psum_tensor(f"ps_b{i}", [P, 512], F32)) for i in range(4)]
        ps_h = [ps_s[:, 0:512], ps_s[:, 512:1024]]

        (x_sb, hT_hi, hT_lo, cos_q, sin_q, ident, ones, gates_in, gates, eps_ln, eps_rms, zero_b, ln_buf, ln_stats_sb, ln_mv,
         ln_sd_sb, ln_rs_sb) = alloc(
            stack, ("x_sb", [P, NT, E], F32), ("hT_hi", [P, KC, T], FR), ("hT_lo", [P, KC, T], FR),
            ("cos_q", [P, T], F32), ("sin_q", [P, T], F32), ("ident", [P, P], F32), ("ones", [P, S], F32),
            ("gates_in", [P, 4], F32), ("gates", [P, 4], F32), ("eps_ln", [P, 1], F32), ("eps_rms", [P, 1], F32),
            ("zero_b", [P, 1], F32), ("ln_buf", [P, 2, E], F32), ("ln_stats", [P, NT, 6], F32), ("ln_mv", [P, NT, 2], F32),
            ("ln_sd", [P, NT], F32), ("ln_rs", [P, NT], F32))
        mask_i, = alloc(stack, ("mask_i", [P, 2, PAIRS, 2, QB], I32))

        kT_dram = nc.dram_tensor("kT_spill", [2, G, P, T], F32, kind="Internal").ap()
        v_hi_dram = nc.dram_tensor("v_hi_spill", [2, G, P, T], F32, kind="Internal").ap()
        v_lo_dram = nc.dram_tensor("v_lo_spill", [2, G, P, T], F32, kind="Internal").ap()

        pair = lambda *parts: [f for f in zip(*parts)]
        with ExitStack() as a:
            kw_first = alloc(a, ("kw_raw0", [P, KC, BW], F32), ("kw_hi0", [P, KC, BW], FR), ("kw_lo0", [P, KC, BW], FR))
        with ExitStack() as a:
            wq_raw, wq_hi, wq_lo = alloc(a, ("wq_raw", [P, KC, J * D], F32), ("wq_hi", [P, KC, J * D], FR), ("wq_lo", [P, KC, J * D], FR))
        with ExitStack() as a:
            u_raw, r_raw, rT_hi, rT_lo = alloc(a, ("u_raw", [P, FT, E], F32), ("r_raw", [NX, E], F32), ("rT_hi", [P, KC, P], FR),
                                               ("rT_lo", [P, KC, P], FR))
        with ExitStack() as a:
            l_lg, l_top, l_rep, l_mx, l_ex, l_sum, l_rec, m_T, l_m, mT_hi, mT_lo = alloc(
                a, ("l_lg", [P, NT, 8], F32), ("l_top", [P, NT, 8], F32), ("l_rep", [P, NT, 8], F32), ("l_mx", [P, NT], F32),
                ("l_ex", [P, NT, LX], F32), ("l_sum", [P, NT], F32), ("l_rec", [P, NT], F32), ("m_T", [LM + LX, T], F32),
                ("l_m", [P, NT, LX, LR], F32), ("mT_hi", [LM, T], FR), ("mT_lo", [LM, T], FR))
        alloc(stack, ("region_first", [P, 3 * KC * BW], F32))

        with ExitStack() as here:
            pos_i, pos_f, pos_t, pos_ix = alloc(
                here, ("pos_i", [NT, P], I32), ("pos_f", [NT, P], F32), ("pos_t", [NT, P], F32), ("pos_ix", [P, NT], I32))
            (cT_hi, cT_lo, rope_k, kw_raw1, kw_hi1, kw_lo1, k_t1, k_t2, k_sq, k_ss) = alloc(
                here, ("cT_hi", [P, KC, T], FR), ("cT_lo", [P, KC, T], FR), ("rope_k", [P, NT, D], F32),
                ("kw_raw1", [P, KC, BW], F32), ("kw_hi1", [P, KC, BW], FR), ("kw_lo1", [P, KC, BW], FR),
                ("k_t1", [P, 2, BW], F32), ("k_t2", [P, 2, BW], F32), ("k_sq", [P, BW], F32), ("k_ss", [P, 3, GB], F32))
            kw_raw, kw_hi, kw_lo = pair(kw_first, (kw_raw1, kw_hi1, kw_lo1))
            with ExitStack() as a:
                c_raw, rope_q = alloc(a, ("c_raw", [P, NT, E], F32), ("rope_q", [P, NT, 2 * D], F32))
            with ExitStack() as a:
                kT_st, vs_hi, vs_lo = alloc(
                    a, ("kT_st", [P, GB, T], F32), ("vs_hi", [P, NT, BW], FR), ("vs_lo", [P, NT, BW], FR))

        with ExitStack() as a:
            g_raw, = alloc(a, ("g_raw", [P, FT, E], F32))
        with ExitStack() as a:
            d_raw, = alloc(a, ("d_raw", [P, KC, FI], F32))
        with ExitStack() as a:
            f_hi, f_lo, sg, gu, hid = alloc(
                a, ("f_hi", [P, 2, KC, P], FR), ("f_lo", [P, 2, KC, P], FR), ("sg", [P, 2, FH], F32), ("gu", [P, 2, FH], F32),
                ("hid", [P, FI], F32))
        with ExitStack() as a:
            a_raw, b_raw, aT_hi, aT_lo, bT_hi, bT_lo = alloc(
                a, ("a_raw", [LM + LX, E], F32), ("b_raw", [P, LO // P, LX, LR], F32), ("aT_hi", [P, KC, P], FR),
                ("aT_lo", [P, KC, P], FR), ("bT_hi", [LM, LO], FR), ("bT_lo", [LM, LO], FR))
        alloc(stack, ("region_second", [P, 4 * KC * P + 4 * FH + FI], F32))

        with ExitStack() as here:
            qT, kT = alloc(here, ("qT", [P, 2, J, HALF], F32), ("kT", [P, 2, HALF], F32))
            with ExitStack() as a:
                q_t1, q_t2 = alloc(a, ("q_t1", [P, 2, HALF], F32), ("q_t2", [P, 2, HALF], F32))
            q_sq, = alloc(here, ("q_sq", [P, J, HALF], F32))
            wo_raw, = alloc(here, ("wo_raw", [P, J, E], F32))
            with ExitStack() as a:
                keep0, offset0 = alloc(a, ("keep0", [P, 2, PAIRS, 2, QB], F32), ("offset0", [P, 2, PAIRS, 2, QB], F32))
            r_q, = alloc(here, ("r_q", [P, SC], F32))
            s_sb, p_sb, pT, p_hi, p_lo, v_hi, v_lo = alloc(
                here, ("s_sb", [P, SC], F32), ("p_sb", [P, SC], F32), ("pT", [P, SC], F32), ("p_hi", [P, SC], FR), ("p_lo", [P, SC], FR),
                ("v_hi", [P, NT, D], FR), ("v_lo", [P, NT, D], FR))
            o_hi, o_lo, wo_hi, wo_lo = alloc(here, ("o_hi", [P, PAIRS, J, P], FR), ("o_lo", [P, PAIRS, J, P], FR),
                                             ("wo_hi", [P, J, E], FR), ("wo_lo", [P, J, E], FR))
            mx_a, mx_b, mx_c, sm_a, sm_b, sm_c, p_rec, mask1_sb, qk_in, qk_w = alloc(
                here, ("mx_a", [P, NQ], F32), ("mx_b", [P, NQ], F32), ("mx_c", [P, NQ], F32), ("sm_a", [P, NQ], F32),
                ("sm_b", [P, NQ], F32), ("sm_c", [P, NQ], F32), ("p_rec", [P, NQ], F32), ("mask1_sb", [P, 2, QB], F32),
                ("qk_in", [P, 2], F32), ("qk_w", [P, 1], F32))
        with ExitStack() as here:
            gT_hi, gT_lo, x_lgT, uT_hi, uT_lo, dT_hi, dT_lo = alloc(
                here, ("gT_hi", [P, KC, FI], FR), ("gT_lo", [P, KC, FI], FR), ("x_lgT", [NX, T], F32), ("uT_hi", [P, KC, FI], FR),
                ("uT_lo", [P, KC, FI], FR), ("dT_hi", [P, FT, E], FR), ("dT_lo", [P, FT, E], FR))
            (hdT_hi, hdT_lo, x_lg, x_mx, x_ex, x_sum, x_rec, x_p, x_top, x_rep, x_two, x_w) = alloc(
                here, ("hdT_hi", [P, FT, P], FR), ("hdT_lo", [P, FT, P], FR), ("x_lg", [P, NT, NX], F32), ("x_mx", [P, NT], F32), ("x_ex", [P, NT, NX], F32),
                ("x_sum", [P, NT], F32), ("x_rec", [P, NT], F32), ("x_p", [P, NT, NX], F32), ("x_top", [P, NT, 8], F32),
                ("x_rep", [P, NT, NX], F32), ("x_two", [P, NT], F32), ("x_w", [P, NT, NX], F32))

        prep, kv = Stage("prep"), Stage("kv")
        units = 2 * G
        att_signals = {"wq_in": 16 * G, "wo_in": 16 * G, "k_in0": 16 * G, "k_in1": 16 * G, "v_in": 32 * G, "mask_in": 16 * 4 * 2 * 2,
                       "wq_hi": J * G, "wq_lo": J * G, "wo_hi": J * G, "wo_lo": J * G}
        for per_unit, names in ((1, "scored s_turned s_masked mx_part mx_other s_max s_shifted p_exp sm_part sm_other sm_all p_rec "
                                    "p_normed p_turned p_hi p_lo"),
                                (J, "q_done q_rot o_done o_hi o_lo y_done y_added")):
            for name in names.split():
                att_signals[name] = per_unit * units
        ln_signals = {"sd": 2, "rs": 2} | dict.fromkeys(("stats", "moments", "normed", "transposed", "hi", "lo"), NT)
        att = [Stage("att")]
        att.append(Stage("att", att[0], att_signals))
        lns = [Stage("ln")]
        for n in range(1, 4):
            lns.append(Stage("ln", lns[0], {k: n * v for k, v in ln_signals.items()}))
        moe, lora = Stage("moe"), Stage("lora")
        xt = x.flatten_outer_dims().rearrange("(i p) e -> p i e", p=P)
        ct = ctx_in.flatten_outer_dims().rearrange("(i p) e -> p i e", p=P)
        ot = out.flatten_outer_dims().rearrange("(i p) e -> p i e", p=P)
        WQ, WK, WV, WO = [Wq0, Wq1], [Wk0, Wk1], [Wv0, Wv1], [Wo0, Wo1]

        block = stack.enter_context(nc.Block())

        def wide(t, inner):
            return t.unsqueeze(2).to_broadcast([t.shape[0], t.shape[1], inner])

        def three(dst, l_hi, l_lo, r_hi, r_lo, first, last):
            nc.tensor.matmul(dst, l_hi, r_hi, start=first, stop=False)
            nc.tensor.matmul(dst, l_hi, r_lo, start=False, stop=False)
            return nc.tensor.matmul(dst, l_lo, r_hi, start=False, stop=last)

        def ln_stats(dve, c, h, done):
            for i in range(h * PAIRS, (h + 1) * PAIRS):
                dve.wait_ge(*done(i))
                nc.vector.bn_stats(ln_stats_sb[:, i, :], x_sb[:, i, :]).then_inc(c["stats"], 1)
            for i in range(h * PAIRS, (h + 1) * PAIRS):
                dve.wait_ge(*c("stats", i + 1))
                nc.vector.bn_aggr(ln_mv[:, i, :], ln_stats_sb[:, i, :]).then_inc(c["moments"], 1)

        def ln_sd(act, c, h):
            act.wait_ge(*c("moments", (h + 1) * PAIRS))
            own = slice(h * PAIRS, (h + 1) * PAIRS)
            nc.scalar.activation(ln_sd_sb[:, own], ln_mv[:, own, 1], ACT.Sqrt, bias=eps_ln[:, 0:1]).then_inc(c["sd"], 1)

        def ln_rs(dve, c, h):
            dve.wait_ge(*c("sd", h + 1))
            own = slice(h * PAIRS, (h + 1) * PAIRS)
            nc.vector.reciprocal(ln_rs_sb[:, own], ln_sd_sb[:, own]).then_inc(c["rs"], 1)

        def ln_norm(dve, c, i):
            if i % PAIRS == 0:
                dve.wait_ge(*c("rs", i // PAIRS + 1))
            if i >= 2:
                dve.wait_ge(*c("transposed", i - 1))
            nc.vector.tensor_scalar(ln_buf[:, i % 2, :], x_sb[:, i, :], ln_mv[:, i, 0:1], ln_rs_sb[:, i:i + 1],
                                    ALU.subtract, ALU.mult).then_inc(c["normed"], 1)

        def ln_turn(pe, c, i):
            pe.wait_ge(*c("normed", i + 1))
            if i >= 2:
                pe.wait_ge(*c("lo", i - 1))
            for k in range(KC):
                last = nc.tensor.transpose(ps_h[i % 2][:, k * P:(k + 1) * P], ln_buf[:, i % 2, k * P:(k + 1) * P], ident[:, :])
            last.then_inc(c["transposed"], 1)

        def ln_high(act, c, i):
            act.wait_ge(*c("transposed", i + 1))
            nc.scalar.activation(hT_hi[:, :, i * P:(i + 1) * P], ps_h[i % 2].rearrange("p (k t) -> p k t", k=KC),
                                 ACT.Copy).then_inc(c["hi"], 1)

        def ln_low(dve, c, i):
            dve.wait_ge(*c("hi", i + 1))
            nc.vector.tensor_tensor(hT_lo[:, :, i * P:(i + 1) * P], ps_h[i % 2].rearrange("p (k t) -> p k t", k=KC),
                                    hT_hi[:, :, i * P:(i + 1) * P].bitcast(F32), ALU.subtract).then_inc(c["lo"], 1)

        def ln_second(dve, c, beside):
            for i in range(PAIRS, PAIRS + 2):
                ln_norm(dve, c, i)
            for i in range(PAIRS, NT):
                beside(i)
                ln_low(dve, c, i)
                if i + 2 < NT:
                    ln_norm(dve, c, i + 2)

        def prep_sync(sp):
            c = prep
            sp.dma_start(pos_i[:, :], pos.rearrange("b s -> (b s)").rearrange("(i p) -> i p", p=P)).then_inc(c["pos"], 16)
            for n in range(NT // 2):
                sp.dma_start(c_raw[:, 2 * n:2 * n + 2, :], ct[:, 2 * n:2 * n + 2, :]).then_inc(c[f"ctx{n}"], 16)
                if n == 0:
                    kv_sync_load(sp, 0, 0)
            kv_sync_load(sp, 0, 1)
            sp.dma_start(gates_in[:, 0:2], g_xattn.partition_broadcast(P)).then_inc(c["gates_in"], 16)
            sp.dma_start(gates_in[:, 2:4], g_ffn.partition_broadcast(P)).then_inc(c["gates_in"], 16)
            sp.dma_start(x_sb[:, :, :], xt).then_inc(c["x"], 16)

        def att_load_mask(sp):
            for h in range(2):
                own = mask0[h * 2 * PAIRS:(h + 1) * 2 * PAIRS].rearrange("(t u) (a q) k -> u a q t k", u=2, q=QB)
                for par in range(2):
                    for kb in range(2):
                        q0 = par * S + kb * QB
                        for a in range(2):
                            sp.dma_start(mask_i[q0:q0 + QB, h, :, a, :], own[par, a, :, :, kb * QB:(kb + 1) * QB]).then_inc(att[0]["mask_in"], 16)

        def prep_pool(pool):
            c = prep
            nc.gpsimd.memset(ident[:, :], 0.0).then_inc(c["cleared"], 1)
            nc.gpsimd.memset(ones[:, :], 1.0).then_inc(c["consts"], 1)
            nc.gpsimd.memset(eps_ln[:, :], EPS).then_inc(c["consts"], 1)
            nc.gpsimd.memset(eps_rms[:, :], D * EPS).then_inc(c["consts"], 1)
            nc.gpsimd.memset(zero_b[:, :], 0.0).then_inc(c["consts"], 1)
            pool.wait_ge(c["cleared"], 1)
            nc.gpsimd.affine_select(out=ident[:, :], in_=ident[:, :], compare_op=ALU.not_equal, fill=1.0, base=0,
                                    pattern=[[-1, P]], channel_multiplier=1).then_inc(c["ident"], 1)
            pool.wait_ge(c["pos_ok"], 5)
            for table, rows, name in ((rope_k_table, rope_k, "rope_k"), (rope_q_table, rope_q, "rope_q")):
                for i in range(NT):
                    nc.gpsimd.indirect_dma_start(rows[:, i, :], None, table, bass.IndirectOffsetOnAxis(ap=pos_ix[:, i:i + 1], axis=0)).then_inc(c[name], 16)

        def prep_dve(dve):
            c = prep
            dve.wait_ge(c["pos"], 16)
            nc.vector.tensor_copy(pos_f[:, :], pos_i[:, :]).then_inc(c["pos_ok"], 1)
            dve.wait_ge(c["pos_ok"], 1)
            nc.vector.tensor_scalar(pos_t[:, :], pos_f[:, :], 0.0, float(MAX_POS), ALU.is_lt, ALU.mult).then_inc(c["pos_ok"], 1)
            dve.wait_ge(c["pos_ok"], 2)
            nc.vector.tensor_tensor(pos_f[:, :], pos_f[:, :], pos_t[:, :], ALU.add).then_inc(c["pos_ok"], 1)
            dve.wait_ge(c["pos_ok"], 3)
            nc.vector.tensor_scalar(pos_f[:, :], pos_f[:, :], 0.0, float(MAX_POS - 1), ALU.max, ALU.min).then_inc(c["pos_ok"], 1)
            dve.wait_ge(c["pos_turned"], 1)
            nc.vector.tensor_copy(pos_ix[:, :], ps_b[0][:, 0:NT]).then_inc(c["pos_ok"], 1)
            for i in range(NT):
                if i >= 4:
                    dve.wait_ge(kv["w0_hi"], i - 3)
                    nc.vector.tensor_tensor(kw_lo[0][:, i - 4, :], kw_raw[0][:, i - 4, :], kw_hi[0][:, i - 4, :].bitcast(F32),
                                            ALU.subtract).then_inc(kv["w0_lo"], 1)
                dve.wait_ge(c["ctx_hi"], i + 1)
                nc.vector.tensor_tensor(cT_lo[:, :, i * P:(i + 1) * P], ps_h[i % 2].rearrange("p (k t) -> p k t", k=KC),
                                        cT_hi[:, :, i * P:(i + 1) * P].bitcast(F32), ALU.subtract).then_inc(c["ctx_lo"], 1)

        def prep_pe(pe):
            c = prep
            pe.wait_ge(c["ident"], 1)
            pe.wait_ge(c["pos_ok"], 4)
            nc.tensor.transpose(ps_b[0][:, 0:NT], pos_f[:, :], ident[0:NT, 0:NT]).then_inc(c["pos_turned"], 1)
            for i in range(NT):
                if i % 2 == 0:
                    pe.wait_ge(c[f"ctx{i // 2}"], 16)
                if i >= 2:
                    pe.wait_ge(c["ctx_lo"], i - 1)
                for k in range(KC):
                    last = nc.tensor.transpose(ps_h[i % 2][:, k * P:(k + 1) * P], c_raw[:, i, k * P:(k + 1) * P], ident[:, :])
                last.then_inc(c["ctx_t"], 1)

        def prep_act(act):
            for i in range(NT):
                if i == 2:
                    kv_weights_hi(act, 0, 0)
                act.wait_ge(prep["ctx_t"], i + 1)
                nc.scalar.activation(cT_hi[:, :, i * P:(i + 1) * P], ps_h[i % 2].rearrange("p (k t) -> p k t", k=KC),
                                     ACT.Copy).then_inc(prep["ctx_hi"], 1)

        def tables_pe(pe, h):
            c = prep
            pe.wait_ge(c["rope_q"], 16 * NT)
            if h:
                pe.wait_ge(c["tables"], 2)
            for kind in range(2):
                for t in range(PAIRS):
                    last = nc.tensor.transpose(ps_b[2 + kind][:, t * P:(t + 1) * P], rope_q[:, h * PAIRS + t, kind * D:(kind + 1) * D], ident[:, :])
                last.then_inc(c["tables_t"], 1)

        def tables_act(act, h):
            for kind in range(2):
                act.wait_ge(prep["tables_t"], 2 * h + kind + 1)
                nc.scalar.activation((cos_q, sin_q)[kind][:, h * HALF:(h + 1) * HALF], ps_b[2 + kind][:, :], ACT.Copy).then_inc(prep["tables"], 1)

        def kv_sync_load(sp, cb, b):
            lay, w = divmod(b, 2)
            src = (WK, WV)[w][lay]
            if lay == 0:
                view = src[:, cb * BW:(cb + 1) * BW].rearrange("(k p) c -> p k c", p=P)
            else:
                view = src[cb * BW:(cb + 1) * BW, :].rearrange("(r p) e -> p r e", p=P)
            sp.dma_start(kw_raw[w][:, :, :], view).then_inc(kv[f"raw{w}"], 16)

        def kv_sync_spill(sp, cb, b):
            c = kv
            lay, w = divmod(b, 2)
            if w == 0:
                sp.wait_ge(c[f"k_staged{lay}"], NT * (cb + 1))
                sp.dma_start(kT_dram[lay, cb * GB:(cb + 1) * GB, :, :].rearrange("g p t -> p g t"), kT_st[:, :, :]).then_inc(c["k_spilled"], 16)
            else:
                sp.wait_ge(c["v_hi"], NT * (2 * cb + lay + 1))
                sp.wait_ge(c["v_lo"], NT * (2 * cb + lay + 1))
                for st, dr in ((vs_hi, v_hi_dram), (vs_lo, v_lo_dram)):
                    for g in range(GB):
                        sp.dma_start(dr[lay, cb * GB + g, :, :].rearrange("p (i d) -> p i d", d=D), st[:, :, g * D:(g + 1) * D].bitcast(F32)).then_inc(c["v_spilled"], 16)

        def kv_sync(sp):
            c = kv
            for cb in range(NB):
                for w in range(2):
                    sp.wait_ge(c["w0_hi"], 8 * cb + 4 * w + 4)
                    sp.wait_ge(c["w0_lo"], 8 * cb + 4 * w + 4)
                    kv_sync_load(sp, cb, 2 + w)
                    if cb == 0 and w:
                        att_load_mask(sp)
                kv_sync_spill(sp, cb, 0)
                sp.wait_ge(c["w1_t"], 8 * cb + 4)
                if cb + 1 < NB:
                    kv_sync_load(sp, cb + 1, 0)
                else:
                    att_load_wq(sp, 0, 0)
                kv_sync_spill(sp, cb, 1)
                if cb + 1 < NB:
                    sp.wait_ge(c["w1_t"], 8 * cb + 8)
                    kv_sync_load(sp, cb + 1, 1)
                kv_sync_spill(sp, cb, 2)
                if cb + 1 == NB:
                    att_wq_split(sp, 0, 1)
                    att_load_wq(sp, 0, 1)
                kv_sync_spill(sp, cb, 3)

        def kv_pe(pe):
            c = kv

            def weights_t(cb, b, k):
                w = b % 2
                if k == 0:
                    pe.wait_ge(c[f"raw{w}"], 16 * (2 * cb + 2))
                n = 8 * cb + 4 * w + k
                if n >= 2:
                    pe.wait_ge(c["w1_lo"], n - 1)
                else:
                    pe.wait_ge(prep["tables"], 4)
                for r in range(KC):
                    last = nc.tensor.transpose(ps_b[2 + k % 2][:, r * P:(r + 1) * P], kw_raw[w][:, r, k * P:(k + 1) * P], ident[:, :])
                last.then_inc(c["w1_t"], 1)

            def keys_t(cb, lay, i):
                pe.wait_ge(c[f"k_done{lay}"], NT * cb + i + 1)
                if i >= 2:
                    pe.wait_ge(c[f"k_staged{lay}"], NT * cb + i - 1)
                elif lay:
                    pe.wait_ge(c["k_staged0"], NT * (cb + 1))
                elif cb:
                    pe.wait_ge(c["k_staged1"], NT * cb)
                for g in range(GB):
                    last = nc.tensor.transpose(ps_b[i % 2][:, g * P:(g + 1) * P], k_t1[:, i % 2, g * D:(g + 1) * D], ident[:, :])
                last.then_inc(c["k_t"], 1)

            for cb in range(NB):
                for b in range(4):
                    lay, w = divmod(b, 2)
                    pe.wait_ge(c[f"w{lay}_hi"], 8 * cb + 4 * w + 4)
                    pe.wait_ge(c[f"w{lay}_lo"], 8 * cb + 4 * w + 4)
                    for i in range(NT):
                        if cb == 0 and b == 0:
                            pe.wait_ge(prep["ctx_lo"], i + 1)
                        n = NT * (4 * cb + b) + i - 2
                        if n >= 0:
                            last_cb, last_b, last_i = n // (4 * NT), n // NT % 4, n % NT
                            if last_b % 2:
                                pe.wait_ge(c["v_lo"], NT * (2 * last_cb + last_b // 2) + last_i + 1)
                            else:
                                pe.wait_ge(c[("k_read0", "k_done1")[last_b // 2]], NT * last_cb + last_i + 1)
                        for k in range(KC):
                            last = three(ps_q[i % 2][:, :], cT_hi[:, k, i * P:(i + 1) * P], cT_lo[:, k, i * P:(i + 1) * P],
                                         kw_hi[w][:, k, :], kw_lo[w][:, k, :], k == 0, k == KC - 1)
                        last.then_inc(c["tile"], 1)
                        if w == 0 and i >= 1:
                            keys_t(cb, lay, i - 1)
                        if w == 1 and i == 0:
                            keys_t(cb, lay, NT - 1)
                        if b in (1, 2) and 2 <= i < 2 + KC:
                            weights_t(cb, b + 1, i - 2)
                        if cb == 0 and b == 0 and i in (4, 7):
                            tables_pe(pe, i // 7)
                        if cb == 0 and b == 3 and i < NT // 2:
                            ln_turn(pe, lns[0], 2 * i)
                            ln_turn(pe, lns[0], 2 * i + 1)

        def kv_weights_hi(act, cb, b):
            w = b % 2
            act.wait_ge(kv[f"raw{w}"], 16 * (2 * cb + 1))
            if cb:
                act.wait_ge(kv["tile"], NT * (4 * cb - 1 + w))
            for k in range(KC):
                nc.scalar.activation(kw_hi[w][:, k, :], kw_raw[w][:, k, :], ACT.Copy).then_inc(kv["w0_hi"], 1)

        def kv_act(act):
            c = kv
            for cb in range(NB):

                def weights_hi(b, k):
                    w = b % 2
                    act.wait_ge(c["w1_t"], 8 * cb + 4 * w + k + 1)
                    nc.scalar.activation(kw_hi[w][:, k, :], ps_b[2 + k % 2][:, :], ACT.Copy).then_inc(c["w1_hi"], 1)

                def stage_keys(lay, i):
                    act.wait_ge(c["k_t"], NT * (2 * cb + lay) + i + 1)
                    if i == 0 and cb + lay:
                        act.wait_ge(c["k_spilled"], 16 * (2 * cb + lay))
                    nc.scalar.activation(kT_st[:, :, i * P:(i + 1) * P], ps_b[i % 2].rearrange("p (g t) -> p g t", g=GB),
                                         ACT.Copy).then_inc(c[f"k_staged{lay}"], 1)

                def values_hi(lay, i):
                    act.wait_ge(c["tile"], NT * (4 * cb + 2 * lay + 1) + i + 1)
                    if i == 0 and cb + lay:
                        act.wait_ge(c["v_spilled"], 16 * 2 * GB * (2 * cb + lay))
                    nc.scalar.activation(vs_hi[:, i, :], ps_q[i % 2][:, :], ACT.Copy).then_inc(c["v_hi"], 1)

                for i in range(NT - 1):
                    if i == 2:
                        kv_weights_hi(act, cb, 1)
                    stage_keys(0, i)
                    if cb == 0 and i == 3:
                        tables_act(act, 0)
                if cb == 0:
                    tables_act(act, 1)
                for i in range(NT):
                    values_hi(0, i)
                    if i == 0:
                        stage_keys(0, NT - 1)
                    if 2 <= i < 2 + KC:
                        weights_hi(2, i - 2)
                if cb == 0:
                    ln_sd(act, lns[0], 0)
                    ln_sd(act, lns[0], 1)
                for i in range(NT):
                    act.wait_ge(c["tile"], NT * (4 * cb + 2) + i + 1)
                    if cb or i:
                        act.wait_ge(c["k_ssq"], NT * cb + i)
                    nc.scalar.activation(k_sq[:, :], ps_q[i % 2][:, :], ACT.Square).then_inc(c["k_sq"], 1)
                    act.wait_ge(c["k_ssq"], NT * cb + i + 1)
                    nc.scalar.activation(k_ss[:, 1, :], k_ss[:, 0, :], ACT.Sqrt, bias=eps_ln[:, 0:1], scale=1.0 / D).then_inc(c["k_rms"], 1)
                    if i >= 1:
                        stage_keys(1, i - 1)
                    if 2 <= i < 2 + KC:
                        weights_hi(3, i - 2)
                for i in range(NT):
                    values_hi(1, i)
                    if i == 0:
                        stage_keys(1, NT - 1)
                    if cb == 0 and i < NT // 2:
                        ln_high(act, lns[0], 2 * i)
                        ln_high(act, lns[0], 2 * i + 1)
                    if i == 3 and cb + 1 < NB:
                        kv_weights_hi(act, cb + 1, 0)
                    if i == 2 and cb + 1 == NB:
                        act.wait_ge(c["tile"], NT * (4 * cb + 3))
                        for j in range(J):
                            att_wq_high(act, 0, 0, j)

        def kv_pool(pool):
            c = kv
            for cb in range(NB):

                def weights_lo(cb, w, k):
                    pool.wait_ge(c["w0_hi"], 8 * cb + 4 * w + k + 1)
                    nc.gpsimd.tensor_tensor(kw_lo[w][:, k, :], kw_raw[w][:, k, :], kw_hi[w][:, k, :].bitcast(F32),
                                            ALU.subtract).then_inc(c["w0_lo"], 1)

                for i in range(NT):
                    pool.wait_ge(c["k_read0"], NT * cb + i + 1)
                    nc.gpsimd.tensor_tensor(k_t1[:, i % 2, :], k_t1[:, i % 2, :], k_t2[:, i % 2, :], ALU.add).then_inc(c["k_done0"], 1)
                    if 2 <= i < 2 + KC:
                        weights_lo(cb, 1, i - 2)
                for k in range(KC):
                    if cb + 1 < NB:
                        weights_lo(cb + 1, 0, k)
                    else:
                        att_wq_low(pool, 0, 0, k)

        def kv_dve(dve):
            c = kv
            h = D // 2
            dve.wait_ge(prep["rope_k"], 16 * NT)
            for cb in range(NB):

                def weights_lo(b, k):
                    w = b % 2
                    dve.wait_ge(c["w1_hi"], 8 * cb + 4 * w + k + 1)
                    nc.vector.tensor_tensor(kw_lo[w][:, k, :], ps_b[2 + k % 2][:, :], kw_hi[w][:, k, :].bitcast(F32),
                                            ALU.subtract).then_inc(c["w1_lo"], 1)

                def values_lo(lay, i):
                    dve.wait_ge(c["v_hi"], NT * (2 * cb + lay) + i + 1)
                    nc.vector.tensor_tensor(vs_lo[:, i, :], ps_q[i % 2][:, :], vs_hi[:, i, :].bitcast(F32),
                                            ALU.subtract).then_inc(c["v_lo"], 1)

                for i in range(NT):
                    dve.wait_ge(c["tile"], NT * 4 * cb + i + 1)
                    if cb or i >= 2:
                        dve.wait_ge(c["k_t"], NT * 2 * cb + max(i - 1, 0))
                    key = ps_q[i % 2].rearrange("p (g u d) -> p g u d", g=GB, u=2)
                    t1 = k_t1[:, i % 2, :].rearrange("p (g u d) -> p g u d", g=GB, u=2)
                    t2 = k_t2[:, i % 2, :].rearrange("p (g u d) -> p g u d", g=GB, u=2)
                    cos = rope_k[:, i, 0:h].unsqueeze(1).to_broadcast([P, GB, h])
                    sin = rope_k[:, i, h:D].unsqueeze(1).to_broadcast([P, GB, h])
                    for u in range(2):
                        nc.vector.tensor_tensor(t1[:, :, u, :], key[:, :, u, :], cos, ALU.mult).then_inc(c["k_cos"], 1)
                    nc.vector.scalar_tensor_tensor(t2[:, :, 0, :], key[:, :, 1, :], -1.0, sin, ALU.mult, ALU.mult).then_inc(c["k_cos"], 1)
                    nc.vector.tensor_tensor(t2[:, :, 1, :], key[:, :, 0, :], sin, ALU.mult).then_inc(c["k_read0"], 1)
                for i in range(NT):
                    values_lo(0, i)
                    if 2 <= i < 2 + KC:
                        weights_lo(2, i - 2)
                    if cb == 0 and i in (3, 5):
                        ln_stats(dve, lns[0], i // 5, lambda i: (prep["x"], 16))
                for i in range(NT):
                    dve.wait_ge(c["k_sq"], NT * cb + i + 1)
                    nc.vector.tensor_reduce(k_ss[:, 0, :], k_sq[:, :].rearrange("p (g d) -> p g d", g=GB), AX, ALU.add).then_inc(c["k_ssq"], 1)
                    dve.wait_ge(c["k_rms"], NT * cb + i + 1)
                    nc.vector.reciprocal(k_ss[:, 2, :], k_ss[:, 1, :]).then_inc(c["k_rrms"], 1)
                    dve.wait_ge(c["k_rrms"], NT * cb + i + 1)
                    dve.wait_ge(c["k_t"], NT * (2 * cb + 1) + max(i - 1, 0))
                    nc.vector.tensor_tensor(k_t1[:, i % 2, :].rearrange("p (g d) -> p g d", g=GB), ps_q[i % 2].rearrange("p (g d) -> p g d", g=GB),
                                            wide(k_ss[:, 2, :], D), ALU.mult).then_inc(c["k_done1"], 1)
                    if 2 <= i < 2 + KC:
                        weights_lo(3, i - 2)
                    if cb == 0 and i in (2, 5):
                        ln_rs(dve, lns[0], i // 5)
                        if i == 5:
                            ln_norm(dve, lns[0], 0)
                            ln_norm(dve, lns[0], 1)
                for i in range(NT):
                    values_lo(1, i)
                    if cb == 0 and i < NT // 2:
                        ln_low(dve, lns[0], 2 * i)
                        ln_low(dve, lns[0], 2 * i + 1)
                        if i + 1 < NT // 2:
                            ln_norm(dve, lns[0], 2 * i + 2)
                            ln_norm(dve, lns[0], 2 * i + 3)

        def att_load_wq(sp, lay, g):
            if lay == 0:
                view = Wq0.rearrange("(k p) (g n) -> g p k n", p=P, g=G)[g]
            else:
                view = Wq1.rearrange("(g j p) e -> g p j e", p=P, g=G)[g]
            sp.dma_start(wq_raw[:, :, :], view).then_inc(att[lay]["wq_in"], 16)

        def att_wq_turn(pe, g, j):
            c = att[1]
            if j == 0:
                pe.wait_ge(*c("wq_in", 16 * (g + 1)))
            if j < 2 and isinstance(g, int) and g == 0:
                pe.wait_ge(moe["gu"], 2 * NT)
            elif j < 2:
                pe.wait_ge(*c("q_rot", 8 * g - 1 + j))
            if j >= 2:
                pe.wait_ge(*c("wq_lo", 4 * g + j - 1))
            for k in range(KC):
                last = nc.tensor.transpose(ps_q[j % 2][:, k * P:(k + 1) * P], wq_raw[:, j, k * P:(k + 1) * P], ident[:, :])
            last.then_inc(c["wq_t"], 1)

        def att_wq_high(act, lay, g, j):
            c = att[lay]
            if lay:
                act.wait_ge(*c("wq_t", 4 * g + j + 1))
                src = ps_q[j % 2].rearrange("p (k d) -> p k d", k=KC)
            else:
                act.wait_ge(*c("wq_in", 16 * (g + 1)))
                if not (isinstance(g, int) and g == 0):
                    act.wait_ge(*c("q_done", 8 * g - J + j + 1))
                src = wq_raw[:, :, j * D:(j + 1) * D]
            nc.scalar.activation(wq_hi[:, :, j * D:(j + 1) * D], src, ACT.Copy).then_inc(c["wq_hi"], 1)

        def att_wq_low(pool, lay, g, j):
            c = att[lay]
            pool.wait_ge(*c("wq_hi", 4 * g + j + 1))
            nc.gpsimd.tensor_tensor(wq_lo[:, :, j * D:(j + 1) * D], wq_raw[:, :, j * D:(j + 1) * D],
                                    wq_hi[:, :, j * D:(j + 1) * D].bitcast(F32), ALU.subtract).then_inc(c["wq_lo"], 1)

        def att_wq_low_turned(dve, g, j):
            c = att[1]
            dve.wait_ge(*c("wq_hi", 4 * g + j + 1))
            nc.vector.tensor_tensor(wq_lo[:, :, j * D:(j + 1) * D], ps_q[j % 2].rearrange("p (k d) -> p k d", k=KC),
                                    wq_hi[:, :, j * D:(j + 1) * D].bitcast(F32), ALU.subtract).then_inc(c["wq_lo"], 1)

        def att_wq_split(sp, lay, n):
            sp.wait_ge(*att[lay]("wq_hi", 4 * n))
            sp.wait_ge(*att[lay]("wq_lo", 4 * n))

        def att_sync(sp, lay):
            c = att[lay]

            def load_wo(g):
                if lay == 0:
                    view = Wo0.rearrange("(g j p) e -> g p j e", p=P, g=G)[g]
                else:
                    view = Wo1.rearrange("(k p) (g n) -> g p k n", p=P, g=G)[g]
                sp.dma_start(wo_raw[:, :, :], view).then_inc(c["wo_in"], 16)

            def load_k(g, h):
                sp.dma_start(kT[:, h, :], kT_dram[lay, g, :, h * HALF:(h + 1) * HALF]).then_inc(c[f"k_in{h}"], 16)

            def load_v(g):
                sp.dma_start(v_hi[:, :, :].bitcast(F32), v_hi_dram[lay, g].rearrange("p (i d) -> p i d", d=D)).then_inc(c["v_in"], 16)
                sp.dma_start(v_lo[:, :, :].bitcast(F32), v_lo_dram[lay, g].rearrange("p (i d) -> p i d", d=D)).then_inc(c["v_in"], 16)

            def wo_split(n):
                sp.wait_ge(*c("wo_hi", 4 * n))
                sp.wait_ge(*c("wo_lo", 4 * n))

            if lay == 0:
                sp.wait_ge(kv["k_spilled"], 16 * 2 * NB)
                sp.wait_ge(kv["v_spilled"], 16 * 2 * GB * 2 * NB)
            else:
                sp.wait_ge(moe["u_done"], 2 * NT)
            load_k(0, 0)
            load_k(0, 1)
            if lay:
                for par in range(2):
                    for kb in range(2):
                        q0 = par * S + kb * QB
                        sp.dma_start(mask1_sb[q0:q0 + QB, :, :],
                                     mask1[0, 0, :, kb * QB:(kb + 1) * QB].rearrange("(a q) k -> q a k", q=QB)).then_inc(c["mask_in"], 16)
                sp.dma_start(qk_in[:, 0:1], q_norm.unsqueeze(1)).then_inc(c["qk_in"], 16)
                sp.dma_start(qk_in[:, 1:2], k_norm.unsqueeze(1)).then_inc(c["qk_in"], 16)
            load_wo(0)
            if lay:
                sp.wait_ge(moe["down"], NT)
            load_v(0)
            if lay == 0:
                moe_load_g(sp)
            else:
                lora_load(sp)
            if lay:
                att_wq_split(sp, lay, 1)
                att_load_wq(sp, lay, 1)
            sp.wait_ge(*c("scored", 1))
            load_k(1, 0)
            att_wq_split(sp, lay, 2)
            att_load_wq(sp, lay, 2)

            def steady(g, wq, k):
                wo_split(g)
                load_wo(g)
                sp.wait_ge(*c("scored", 2 * g))
                load_k(g, 1)
                if k:
                    sp.wait_ge(*c("scored", 2 * g + 1))
                    load_k(g + 1, 0)
                sp.wait_ge(*c("o_done", 8 * g))
                load_v(g)
                if wq:
                    att_wq_split(sp, lay, g + 2)
                    att_load_wq(sp, lay, g + 2)

            for g in range(1, G - 2):
                steady(g, True, True)
            steady(G - 2, False, True)
            steady(G - 1, False, False)

        def att_steps(eng, step):
            step(0, 0, True, False, False, False)
            step(0, 1, True, True, False, True)
            step(1, 0, True, True, True, False)
            step(1, 1, True, True, True, True)
            with eng.Fori(2, G - 1) as g:
                step(g, 0, True, True, True, False)
                step(g, 1, True, True, True, True)
            step(G - 1, 0, True, True, True, False)
            step(G - 1, 1, True, True, True, False)

        def att_pe(pe, lay, beside):
            c = att[lay]

            def project(g, h, j):
                n = 4 * (2 * g + h) + j
                if h == 0:
                    ready = 4 * g + ((3, 4, 4, 4)[j] if lay else j + 1)
                    pe.wait_ge(*c("wq_hi", ready))
                    pe.wait_ge(*c("wq_lo", ready))
                if not (isinstance(g, int) and n < 2):
                    pe.wait_ge(*c("q_rot" if lay else "q_read", n - 1))
                for k in range(KC):
                    last = three(ps_q[j % 2][:, :], wq_hi[:, k, j * D:(j + 1) * D], wq_lo[:, k, j * D:(j + 1) * D],
                                 hT_hi[:, k, h * HALF:(h + 1) * HALF], hT_lo[:, k, h * HALF:(h + 1) * HALF], k == 0, k == KC - 1)
                last.then_inc(c["q_done"], 1)

            def square_sums(u, h):
                pe.wait_ge(*c("q_sq", 4 * u + 4))
                if isinstance(u, int) and u == 0:
                    pe.wait_ge(*lns[2]("lo", NT))
                else:
                    pe.wait_ge(*c("s_scaled", u))
                for t in range(PAIRS):
                    for par in range(2):
                        b = (2 * t + par) * S
                        last = nc.tensor.matmul(ps_s[par * S:(par + 1) * S, t * JS:(t + 1) * JS], ones[:, :], q_sq[:, :, b:b + S],
                                                start=True, stop=True)
                last.then_inc(c["ssq"], 1)

            def score(u, h, g):
                pe.wait_ge(*c("q_rot", 4 * u + 4))
                pe.wait_ge(*c(f"k_in{h}", 16 * (g + 1)))
                if lay:
                    pe.wait_ge(*c("r_ln", u + 1))
                elif not (isinstance(u, int) and u == 0):
                    pe.wait_ge(*c("s_turned", u))
                for t in range(PAIRS):
                    for par in range(2):
                        b = (2 * t + par) * S
                        last = nc.tensor.matmul(ps_s[par * S:(par + 1) * S, t * JS:(t + 1) * JS], kT[:, h, b:b + S], qT[:, h, :, b:b + S],
                                                start=True, stop=True)
                last.then_inc(c["scored"], 1)

            def values(u, h, g):
                pe.wait_ge(*c("p_hi", u + 1))
                pe.wait_ge(*c("p_lo", u + 1))
                pe.wait_ge(*c("v_in", 32 * (g + 1)))
                if not (isinstance(u, int) and u == 0):
                    pe.wait_ge(*c("y_added", 4 * u))
                if lay and h == 0:
                    pe.wait_ge(*c("wo_hi", 4 * g + 4))
                    pe.wait_ge(*c("wo_lo", 4 * g + 4))
                for half in range(2):
                    for tt in range(2):
                        t = 2 * half + tt
                        cols = slice(t * JS, (t + 1) * JS)
                        for n, (v_part, p_part) in enumerate(((v_hi, p_hi), (v_hi, p_lo), (v_lo, p_hi))):
                            for par in range(2):
                                rows = slice(par * S, (par + 1) * S)
                                last = nc.tensor.matmul(ps_b[2 * half + par][:, tt * JS:(tt + 1) * JS], v_part[rows, h * PAIRS + t, :],
                                                        p_part[rows, cols], start=n == 0, stop=n == 2)
                                if tt == 1 and n == 2:
                                    last.then_inc(c["o_done"], 1)

            def project_out(u, h, g, t):
                if t % 2 == 0:
                    pe.wait_ge(*c("o_hi", 4 * u + t + 2))
                    pe.wait_ge(*c("o_lo", 4 * u + t + 2))
                if t == 0 and h == 0:
                    pe.wait_ge(*c("wo_hi", 4 * g + 4))
                    pe.wait_ge(*c("wo_lo", 4 * g + 4))
                for j in range(J):
                    last = three(ps_b[t][:, :], o_hi[:, t, j, :], o_lo[:, t, j, :], wo_hi[:, j, :], wo_lo[:, j, :], j == 0, j == J - 1)
                last.then_inc(c["y_done"], 1)

            def wo_turn(g):
                pe.wait_ge(*c("wo_in", 16 * (g + 1)))
                if not (isinstance(g, int) and g == 0):
                    pe.wait_ge(*c("y_added", 8 * g))
                for j in range(J):
                    for k in range(KC):
                        last = nc.tensor.transpose(ps_b[j][:, k * P:(k + 1) * P], wo_raw[:, k, j * D:(j + 1) * D], ident[:, :])
                    last.then_inc(c["wo_t"], 1)

            def step(g, h, do_project, do_score, do_finish, next_wq):
                us, up = 2 * g + h - 1, 2 * g + h - 2
                if do_score and lay:
                    square_sums(us, 1 - h)
                at_first = lay and isinstance(g, int) and (g, h) == (0, 0)
                if do_project:
                    project(g, h, 0)
                if at_first:
                    ln_turn(pe, lns[2], PAIRS)
                    ln_turn(pe, lns[2], PAIRS + 1)
                if do_score:
                    score(us, 1 - h, g if h else g - 1)
                if lay and do_finish and h == 0:
                    wo_turn(g - 1)
                if do_project:
                    project(g, h, 1)
                    if at_first:
                        ln_turn(pe, lns[2], PAIRS + 2)
                        ln_turn(pe, lns[2], PAIRS + 3)
                    project(g, h, 2)
                if do_finish:
                    values(up, h, g - 1)
                if do_project:
                    project(g, h, 3)
                for t in range(PAIRS):
                    if lay and next_wq:
                        att_wq_turn(pe, g + 1, t)
                    if do_finish:
                        project_out(up, h, g - 1, t)

            if lay == 0:
                pe.wait_ge(*lns[0]("lo", NT))
                pe.wait_ge(kv["v_lo"], 2 * NT * NB)
            else:
                pe.wait_ge(*lns[2]("lo", PAIRS))
            att_steps(pe, step)
            last = 2 * G - 1
            if lay:
                square_sums(last, 1)
            score(last, 1, G - 1)
            if lay:
                wo_turn(G - 1)
            beside(0, -1)
            for h in range(2):
                values(last - 1 + h, h, G - 1)
                for t in range(PAIRS):
                    project_out(last - 1 + h, h, G - 1, t)
                    beside(h, t)

        def att_act(act, lay, beside):
            c = att[lay]

            def wo_high(g, j):
                if lay:
                    act.wait_ge(*c("wo_t", 4 * g + j + 1))
                    src = ps_b[j][:, :]
                else:
                    act.wait_ge(*c("wo_in", 16 * (g + 1)))
                    if not (isinstance(g, int) and g == 0):
                        act.wait_ge(*c("y_done", 8 * g))
                    src = wo_raw[:, j, :]
                nc.scalar.activation(wo_hi[:, j, :], src, ACT.Copy).then_inc(c["wo_hi"], 1)

            def queries(u, h, j):
                act.wait_ge(*c("q_done", 4 * u + j + 1))
                if j == 0 and not (isinstance(u, int) and u == 0):
                    act.wait_ge(*c("ssq", u))
                nc.scalar.activation(q_sq[:, j, :], ps_q[j % 2][:, :], ACT.Square).then_inc(c["q_sq"], 1)
                nc.scalar.activation(qT[:, h, j, :], ps_q[j % 2][:, :], ACT.Copy, scale=qk_w[:, 0:1]).then_inc(c["q_rot"], 1)

            def norms(u):
                act.wait_ge(*c("ssq", u + 1))
                if not (isinstance(u, int) and u == 0):
                    act.wait_ge(*c("s_scaled", u))
                nc.scalar.activation(r_q[:, :], ps_s[:, :], ACT.Ln, bias=eps_rms[:, 0:1]).then_inc(c["r_ln"], 1)
                act.wait_ge(*c("r_ln", u + 1))
                nc.scalar.activation(r_q[:, :], r_q[:, :], ACT.Exp, bias=zero_b[:, 0:1], scale=-0.5).then_inc(c["r_q"], 1)

            def exponentials(u):
                act.wait_ge(*c("s_shifted", u + 1))
                nc.scalar.activation(p_sb[:, :], s_sb[:, :], ACT.Exp, bias=zero_b[:, 0:1]).then_inc(c["p_exp"], 1)

            def probs_high(u):
                act.wait_ge(*c("p_turned", u + 1))
                if not (isinstance(u, int) and u == 0):
                    act.wait_ge(*c("o_done", 4 * u))
                nc.scalar.activation(p_hi[:, :], pT[:, :], ACT.Copy).then_inc(c["p_hi"], 1)

            def out_high(u, n):
                half, par = divmod(n, 2)
                act.wait_ge(*c("o_done", 4 * u + n + 1))
                nc.scalar.activation(o_hi[:, 2 * half:2 * half + 2, :, par * S:(par + 1) * S],
                                     ps_b[n].rearrange("p (t j q) -> p t j q", t=2, j=J), ACT.Copy).then_inc(c["o_hi"], 1)

            def step(g, h, do_project, do_score, do_finish, next_wq):
                uq, us, up = 2 * g + h, 2 * g + h - 1, 2 * g + h - 2
                if do_score and lay:
                    norms(us)
                if do_finish and h == 0 and lay == 0:
                    for j in range(J):
                        wo_high(g - 1, j)
                for j in range(J):
                    if j == 3 and do_finish:
                        for n in range(4):
                            out_high(up, n)
                    if do_project and lay:
                        queries(uq, h, j)
                        if isinstance(g, int) and (g, h) == (0, 0) and j < 2:
                            ln_high(act, lns[2], PAIRS + 2 * j)
                            ln_high(act, lns[2], PAIRS + 2 * j + 1)
                    if next_wq and lay == 0 and j < 3:
                        att_wq_high(act, lay, g + 1, j)
                    if j == 0 and do_finish and h == 0 and lay:
                        for jj in range(J):
                            wo_high(g - 1, jj)
                if next_wq and lay:
                    att_wq_high(act, lay, g + 1, 0)
                if do_score:
                    exponentials(us)
                if next_wq:
                    for j in (1, 2) if lay else (3,):
                        att_wq_high(act, lay, g + 1, j)
                if do_score:
                    probs_high(us)
                if next_wq and lay:
                    att_wq_high(act, lay, g + 1, 3)

            if lay:
                act.wait_ge(*c("qk_w", 1))
            att_steps(act, step)
            last = 2 * G - 1
            if lay:
                norms(last)
            for j in range(J):
                wo_high(G - 1, j)
            beside(0, -1)
            for n in range(4):
                out_high(last - 1, n)
            beside(0, 0)
            exponentials(last)
            beside(0, 1)
            beside(0, 2)
            probs_high(last)
            beside(0, 3)
            for n in range(4):
                out_high(last, n)
            ln_sd(act, lns[2 * lay + 1], 0)
            for t in range(PAIRS):
                ln_high(act, lns[2 * lay + 1], t)
                beside(1, t)

        def att_pool(pool, lay):
            c = att[lay]

            def wo_low(g, j):
                pool.wait_ge(*c("wo_hi", 4 * g + j + 1))
                nc.gpsimd.tensor_tensor(wo_lo[:, j, :], wo_raw[:, j, :], wo_hi[:, j, :].bitcast(F32), ALU.subtract).then_inc(c["wo_lo"], 1)

            def rotate(u, h, j):
                pool.wait_ge(*c("q_read", 4 * u + j + 1))
                nc.gpsimd.tensor_tensor(qT[:, h, j, :], q_t1[:, j % 2, :], q_t2[:, j % 2, :], ALU.add).then_inc(c["q_rot"], 1)

            def mask(u, h):
                sc = s_sb.rearrange("p (t j n) -> p t j n", t=PAIRS, j=J)
                if lay == 0:
                    if isinstance(u, int) and u == 0:
                        pool.wait_ge(*c("masks", 2))
                    pool.wait_ge(*c("s_kept", u + 1))
                    m = offset0[:, h, :, :, :].rearrange("p t a k -> p t (a k)").unsqueeze(2).to_broadcast([P, PAIRS, J, S])
                    last = nc.gpsimd.tensor_tensor(sc, sc, m, ALU.add)
                else:
                    pool.wait_ge(*c("s_turned", u + 1))
                    m = mask1_sb.rearrange("p a k -> p (a k)").unsqueeze(1).to_broadcast([P, PAIRS * J, S])
                    sc = s_sb.rearrange("p (n k) -> p n k", k=S)
                    last = nc.gpsimd.tensor_tensor(sc, sc, m, ALU.add)
                last.then_inc(c["s_masked"], 1)

            def shift(u):
                pool.wait_ge(*c("s_max", u + 1))
                sc = s_sb.rearrange("p (n k) -> p n k", k=QB)
                nc.gpsimd.tensor_tensor(sc, sc, wide(mx_c[:, :], QB), ALU.subtract).then_inc(c["s_shifted"], 1)

            def normalise(u):
                pool.wait_ge(*c("p_rec", u + 1))
                pr = p_sb.rearrange("p (n k) -> p n k", k=QB)
                nc.gpsimd.tensor_tensor(pr, pr, wide(p_rec[:, :], QB), ALU.mult).then_inc(c["p_normed"], 1)

            def probs_low(u):
                pool.wait_ge(*c("p_hi", u + 1))
                nc.gpsimd.tensor_tensor(p_lo[:, :], pT[:, :], p_hi[:, :].bitcast(F32), ALU.subtract).then_inc(c["p_lo"], 1)

            def step(g, h, do_project, do_score, do_finish, next_wq):
                uq, us = 2 * g + h, 2 * g + h - 1

                def added(j):
                    if do_project and lay == 0:
                        rotate(uq, h, j)

                def split(wo, wq):
                    if lay == 0:
                        for j in wo if do_finish and h == 0 else ():
                            wo_low(g - 1, j)
                        for j in wq if next_wq else ():
                            att_wq_low(pool, lay, g + 1, j)

                split((0, 1), ())
                added(0)
                split((2,), (0,))
                if do_score:
                    mask(us, 1 - h)
                added(1)
                added(2)
                split((3,), (1,))
                if do_score:
                    shift(us)
                added(3)
                split((), (2,))
                if do_score:
                    normalise(us)
                split((), (3,))
                if do_score:
                    probs_low(us)

            if lay:
                pool.wait_ge(*c("mask_in", 16 * 4))
            att_steps(pool, step)
            step(G, 0, False, True, True, False)

        def att_dve(dve, lay, beside):
            c = att[lay]

            def wo_low(g, j):
                dve.wait_ge(*c("wo_hi", 4 * g + j + 1))
                nc.vector.tensor_tensor(wo_lo[:, j, :], ps_b[j][:, :], wo_hi[:, j, :].bitcast(F32), ALU.subtract).then_inc(c["wo_lo"], 1)

            def rotate(u, h, j):
                n = 4 * u + j
                dve.wait_ge(*c("q_done", n + 1))
                if not (isinstance(u, int) and n < 2):
                    dve.wait_ge(*c("q_rot", n - 1))
                tok = slice(h * HALF, (h + 1) * HALF)
                half = D // 2
                nc.vector.tensor_tensor(q_t1[:, j % 2, :], ps_q[j % 2][:, :], cos_q[:, tok], ALU.mult).then_inc(c["q_cos"], 1)
                nc.vector.tensor_tensor(q_t2[0:half, j % 2, :], ps_q[j % 2][half:D, :], sin_q[half:D, tok], ALU.mult).then_inc(c["q_cos"], 1)
                nc.vector.tensor_tensor(q_t2[half:D, j % 2, :], ps_q[j % 2][0:half, :], sin_q[0:half, tok], ALU.mult).then_inc(c["q_read"], 1)

            def masks():
                dve.wait_ge(*c("mask_in", 16 * 4 * 2 * 2))
                nc.vector.tensor_scalar(keep0[:, :], mask_i[:, :], 0.0, None, ALU.not_equal).then_inc(c["masks"], 1)
                nc.vector.tensor_scalar(offset0[:, :], mask_i[:, :], 0.0, MASKED, ALU.is_equal, ALU.mult).then_inc(c["masks"], 1)
                dve.wait_ge(*c("masks", 2))

            def turn_scores(u, h):
                dve.wait_ge(*c("scored", u + 1))
                src = ps_s[:, :]
                if lay:
                    dve.wait_ge(*c("r_q", u + 1))
                    nc.vector.tensor_tensor(p_sb[:, :], ps_s[:, :], r_q[:, :], ALU.mult).then_inc(c["s_scaled"], 1)
                    dve.wait_ge(*c("s_scaled", u + 1))
                    src = p_sb[:, :]
                nc.vector.transpose(s_sb[:, :], src).then_inc(c["s_turned"], 1)
                if lay == 0:
                    dve.wait_ge(*c("s_turned", u + 1))
                    sc = s_sb.rearrange("p (t j n) -> p t j n", t=PAIRS, j=J)
                    m = keep0[:, h, :, :, :].rearrange("p t a k -> p t (a k)").unsqueeze(2).to_broadcast([P, PAIRS, J, S])
                    nc.vector.tensor_tensor(sc, sc, m, ALU.mult).then_inc(c["s_kept"], 1)

            def across(dst, src):
                for k in range(4):
                    last = nc.vector.tensor_copy(dst[k * QB:(k + 1) * QB, :], src[(k ^ 1) * QB:((k ^ 1) + 1) * QB, :])
                return last

            def maxima(u):
                dve.wait_ge(*c("s_masked", u + 1))
                nc.vector.tensor_reduce(mx_a[:, :], s_sb.rearrange("p (n k) -> p n k", k=QB), AX, ALU.max).then_inc(c["mx_part"], 1)
                dve.wait_ge(*c("mx_part", u + 1))
                across(mx_b, mx_a).then_inc(c["mx_other"], 1)
                dve.wait_ge(*c("mx_other", u + 1))
                nc.vector.tensor_tensor(mx_c[:, :], mx_a[:, :], mx_b[:, :], ALU.max).then_inc(c["s_max"], 1)

            def sums(u):
                dve.wait_ge(*c("p_exp", u + 1))
                nc.vector.tensor_reduce(sm_a[:, :], p_sb.rearrange("p (n k) -> p n k", k=QB), AX, ALU.add).then_inc(c["sm_part"], 1)
                dve.wait_ge(*c("sm_part", u + 1))
                across(sm_b, sm_a).then_inc(c["sm_other"], 1)
                dve.wait_ge(*c("sm_other", u + 1))
                nc.vector.tensor_tensor(sm_c[:, :], sm_a[:, :], sm_b[:, :], ALU.add).then_inc(c["sm_all"], 1)
                dve.wait_ge(*c("sm_all", u + 1))
                nc.vector.reciprocal(p_rec[:, :], sm_c[:, :]).then_inc(c["p_rec"], 1)

            def turn_probs(u):
                dve.wait_ge(*c("p_normed", u + 1))
                nc.vector.transpose(pT[:, :], p_sb[:, :]).then_inc(c["p_turned"], 1)

            def out_low(u, n):
                half, par = divmod(n, 2)
                dve.wait_ge(*c("o_hi", 4 * u + n + 1))
                part = (slice(None), slice(2 * half, 2 * half + 2), slice(None), slice(par * S, (par + 1) * S))
                nc.vector.tensor_tensor(o_lo[part], ps_b[n].rearrange("p (t j q) -> p t j q", t=2, j=J),
                                        o_hi[part].bitcast(F32), ALU.subtract).then_inc(c["o_lo"], 1)

            def add_output(u, h, t):
                n = 4 * u + t
                dve.wait_ge(*c("y_done", n + 1))
                if not (isinstance(u, int) and u == 0):
                    dve.wait_ge(*c("y_added", 4 * u))
                i = h * PAIRS + t
                nc.vector.scalar_tensor_tensor(x_sb[:, i, :], ps_b[t][:, :], gates[:, lay:lay + 1], x_sb[:, i, :],
                                               ALU.mult, ALU.add).then_inc(c["y_added"], 1)

            def step(g, h, do_project, do_score, do_finish, next_wq):
                uq, us, up = 2 * g + h, 2 * g + h - 1, 2 * g + h - 2

                def rotated(j):
                    if do_project and lay == 0:
                        rotate(uq, h, j)

                def end(t):
                    if next_wq and lay:
                        att_wq_low_turned(dve, g + 1, t)
                    if do_finish:
                        add_output(up, h, t)

                rotated(0)
                if lay == 0 and isinstance(g, int) and (g, h) == (0, 0):
                    masks()
                if do_score:
                    turn_scores(us, 1 - h)
                if do_finish and lay and h == 0:
                    for j in range(J):
                        wo_low(g - 1, j)
                rotated(1)
                rotated(2)
                if do_finish:
                    out_low(up, 0)
                    out_low(up, 1)
                if do_score:
                    maxima(us)
                if do_finish:
                    out_low(up, 2)
                    out_low(up, 3)
                rotated(3)
                end(0)
                if do_score:
                    sums(us)
                end(1)
                end(2)
                if do_score:
                    turn_probs(us)
                end(3)

            if lay:
                dve.wait_ge(*c("qk_in", 32))
                nc.vector.tensor_tensor(qk_w[:, :], qk_in[:, 0:1], qk_in[:, 1:2], ALU.mult).then_inc(c["qk_w"], 1)
                ln_stats(dve, lns[2], 1, lambda i: (moe["x_added"], i + 1))
                ln_rs(dve, lns[2], 1)
                ln_second(dve, lns[2], lambda i: None)
            att_steps(dve, step)
            last, ln = 2 * G - 1, lns[2 * lay + 1]
            turn_scores(last, 1)
            if lay:
                for j in range(J):
                    wo_low(G - 1, j)
            beside(0, -1)
            out_low(last - 1, 0)
            out_low(last - 1, 1)
            maxima(last)
            out_low(last - 1, 2)
            out_low(last - 1, 3)
            add_output(last - 1, 0, 0)
            beside(0, 0)
            sums(last)
            add_output(last - 1, 0, 1)
            beside(0, 1)
            add_output(last - 1, 0, 2)
            turn_probs(last)
            beside(0, 2)
            add_output(last - 1, 0, 3)
            beside(0, 3)
            ln_stats(dve, ln, 0, lambda i: c("y_added", 2 * (G - 1) * PAIRS + i + 1))
            for n in range(4):
                out_low(last, n)
            ln_rs(dve, ln, 0)
            ln_norm(dve, ln, 0)
            ln_norm(dve, ln, 1)
            for t in range(PAIRS):
                add_output(last, 1, t)
                ln_low(dve, ln, t)
                if t + 2 < PAIRS:
                    ln_norm(dve, ln, t + 2)
                beside(1, t)
            ln_stats(dve, ln, 1, lambda i: c("y_added", 2 * (G - 1) * PAIRS + i + 1))


        def moe_load_g(sp):
            sp.dma_start(g_raw[:, :, :], glu_w.rearrange("(n p) e -> p n e", p=P)).then_inc(moe["g_in"], 16)

        def moe_sync(sp):
            c = moe
            sp.wait_ge(*att[0]("q_done", J * 2 * G))
            sp.dma_start(r_raw[:, :], gate_w).then_inc(c["r_in"], 16)
            sp.dma_start(u_raw[:, :, :], up_w.rearrange("(n p) e -> p n e", p=P)).then_inc(c["u_in"], 16)
            sp.wait_ge(c["w_t"], 1 + FT)
            sp.dma_start(d_raw[:, :, :], down_w.rearrange("(k p) n -> p k n", p=P)).then_inc(c["d_in"], 16)
            sp.wait_ge(c["w_t"], 1 + 2 * FT)
            sp.wait_ge(c["logits"], 2)
            att_load_wq(sp, 1, 0)

        turns = [("r", 0)] + [(w, n) for w in "gud" for n in range(FT)]
        TURNS = {(0, -1): (0, 1), (0, 0): (2,), (0, 1): (3, 4), (0, 2): (5,), (0, 3): (6, 7),
                 (1, 0): (8,), (1, 1): (9, 10), (1, 2): (11, 12), (1, 3): (13, 14)}
        LATE_TURNS = {PAIRS: (15, 16, 17), PAIRS + 1: (18,), PAIRS + 2: (19,), PAIRS + 3: (20, 21)}

        def turned(m):
            w, n = turns[m]
            bank = ps_q[m % 2]
            view = bank.rearrange("p (k i) -> p k i", k=KC)
            if w == "r":
                return rT_hi[:, :, 0:NX], rT_lo[:, :, 0:NX], view[:, :, 0:NX]
            if w == "d":
                return dT_hi[:, n, :], dT_lo[:, n, :], bank[:, :]
            hi, lo = {"g": (gT_hi, gT_lo), "u": (uT_hi, uT_lo)}[w]
            return hi[:, :, n * P:(n + 1) * P], lo[:, :, n * P:(n + 1) * P], view

        def turn_pe(pe, m):
            c = moe
            w, n = turns[m]
            if m == 0:
                pe.wait_ge(*att[0]("q_rot", J * 2 * G))
            if n == 0:
                pe.wait_ge(c[f"{w}_in"], 16)
            if m >= 2:
                pe.wait_ge(c["w_lo"], m - 1)
            for k in range(KC):
                if w == "r":
                    last = nc.tensor.transpose(ps_q[m % 2][:, k * P:k * P + NX], r_raw[:, k * P:(k + 1) * P], ident[0:NX, 0:NX])
                elif w == "d":
                    last = nc.tensor.transpose(ps_q[m % 2][:, k * P:(k + 1) * P], d_raw[:, k, n * P:(n + 1) * P], ident[:, :])
                else:
                    raw = {"g": g_raw, "u": u_raw}[w]
                    last = nc.tensor.transpose(ps_q[m % 2][:, k * P:(k + 1) * P], raw[:, n, k * P:(k + 1) * P], ident[:, :])
            last.then_inc(c["w_t"], 1)

        def turn_act(act, m):
            act.wait_ge(moe["w_t"], m + 1)
            hi, lo, src = turned(m)
            nc.scalar.activation(hi, src, ACT.Copy).then_inc(moe["w_hi"], 1)

        def turn_dve(dve, m):
            dve.wait_ge(moe["w_hi"], m + 1)
            hi, lo, src = turned(m)
            nc.vector.tensor_tensor(lo, src, hi.bitcast(F32), ALU.subtract).then_inc(moe["w_lo"], 1)

        def moe_beside_pe(h, t):
            if h:
                ln_turn(nc.tensor, lns[1], t)
            for m in TURNS[h, t]:
                turn_pe(nc.tensor, m)

        def moe_beside_act(h, t):
            for m in TURNS[h, t]:
                turn_act(nc.scalar, m)

        def moe_beside_dve(h, t):
            if (h, t) == (0, -1):
                nc.vector.wait_ge(*att[0]("q_done", J * 2 * G))
                nc.vector.memset(rT_hi[:, :, NX:P].bitcast(F32), 0.0).then_inc(moe["r_zero"], 1)
                nc.vector.memset(rT_lo[:, :, NX:P].bitcast(F32), 0.0).then_inc(moe["r_zero"], 1)
            for m in TURNS[h, t]:
                turn_dve(nc.vector, m)

        def moe_pe(pe):
            c = moe

            def logits(h):
                pe.wait_ge(*lns[1]("lo", (h + 1) * PAIRS))
                for k in range(KC):
                    last = three(ps_b[2 + h][:, :], rT_hi[:, k, :], rT_lo[:, k, :], hT_hi[:, k, h * HALF:(h + 1) * HALF],
                                 hT_lo[:, k, h * HALF:(h + 1) * HALF], k == 0, k == KC - 1)
                last.then_inc(c["logits"], 1)

            def logits_t():
                pe.wait_ge(c["lgT"], 2)
                for i in range(NT):
                    last = nc.tensor.transpose(ps_h[0][:, i * NX:(i + 1) * NX], x_lgT[:, i * P:(i + 1) * P], ident[0:NX, 0:NX])
                last.then_inc(c["lg_t"], 1)

            def up(i, r, half):
                if half == 0:
                    pe.wait_ge(c["f_hi"], i + 1)
                    pe.wait_ge(c["f_lo"], i + 1)
                if not (isinstance(i, int) and i == 0):
                    pe.wait_ge(c["gu"], 2 * i + half - 1)
                for bank, hi, lo, name in ((ps_q[half], gT_hi, gT_lo, "g_done"), (ps_b[half], uT_hi, uT_lo, "u_done")):
                    for k in range(KC):
                        last = three(bank[:, 0:FH], f_hi[:, r, k, :], f_lo[:, r, k, :], hi[:, k, half * FH:(half + 1) * FH],
                                     lo[:, k, half * FH:(half + 1) * FH], k == 0, k == KC - 1)
                    last.then_inc(c[name], 1)

            def hidden_t(i):
                pe.wait_ge(c["hid"], 2 * i + 2)
                if not (isinstance(i, int) and i == 0):
                    pe.wait_ge(c["hdT_lo"], 2 * i)
                for n in range(FT):
                    last = nc.tensor.transpose(ps_h[n // 4][:, (n % 4) * P:(n % 4 + 1) * P], hid[:, n * P:(n + 1) * P], ident[:, :])
                last.then_inc(c["hid_t"], 1)

            def down(i, r):
                pe.wait_ge(c["hdT_lo"], 2 * i + 2)
                if not (isinstance(i, int) and i < 2):
                    pe.wait_ge(c["x_added"], i - 1)
                for n in range(FT):
                    last = three(ps_b[2 + r][:, :], hdT_hi[:, n, :], hdT_lo[:, n, :], dT_hi[:, n, :], dT_lo[:, n, :], n == 0, n == FT - 1)
                last.then_inc(c["down"], 1)

            def tile(i, r):
                up(i, r, 0)
                hidden_t(i - 1)
                up(i, r, 1)
                down(i - 1, 1 - r)

            pe.wait_ge(*att[0]("y_added", 2 * G * PAIRS))
            pe.wait_ge(c["r_zero"], 2)
            logits(0)
            for i in range(PAIRS, NT):
                for m in LATE_TURNS[i]:
                    turn_pe(pe, m)
                ln_turn(pe, lns[1], i)
            logits(1)
            pe.wait_ge(c["w_lo"], len(turns))
            up(0, 0, 0)
            logits_t()
            up(0, 0, 1)
            pe.wait_ge(c["x_lg"], 1)
            tile(1, 1)
            tile(2, 0)
            with pe.Fori(1, NT // 2 - 1) as m:
                tile(2 * m + 1, 1)
                tile(2 * m + 2, 0)
            up(NT - 1, 1, 0)
            hidden_t(NT - 2)
            up(NT - 1, 1, 1)
            pe.wait_ge(c["hdT_lo"], 2 * (NT - 1))
            ln_turn(pe, lns[2], 0)
            ln_turn(pe, lns[2], 1)
            down(NT - 2, 0)
            ln_turn(pe, lns[2], 2)
            ln_turn(pe, lns[2], 3)
            att_wq_turn(pe, 0, 0)
            att_wq_turn(pe, 0, 1)
            pe.wait_ge(*lns[2]("lo", PAIRS))
            hidden_t(NT - 1)
            att_wq_turn(pe, 0, 2)
            att_wq_turn(pe, 0, 3)
            down(NT - 1, 1)

        def moe_act(act):
            c = moe

            def logits(h):
                act.wait_ge(c["logits"], h + 1)
                nc.scalar.activation(x_lgT[:, h * HALF:(h + 1) * HALF], ps_b[2 + h][0:NX, :], ACT.Copy).then_inc(c["lgT"], 1)

            def silu(i, half):
                act.wait_ge(c["g_done"], 2 * i + half + 1)
                if not (isinstance(i, int) and i == 0):
                    act.wait_ge(c["gu"], 2 * i + half - 1)
                nc.scalar.activation(sg[:, half, :], ps_q[half][:, 0:FH], ACT.Silu, bias=zero_b[:, 0:1]).then_inc(c["silu"], 1)

            def tokens(i, r):
                if not (isinstance(i, int) and i < 2):
                    act.wait_ge(c["u_done"], 2 * i - 2)
                nc.scalar.activation(f_hi[:, r, :, :], hT_hi[:, :, bass.ts(i, P)].bitcast(F32), ACT.Copy).then_inc(c["f_hi"], 1)

            def hidden_hi(i):
                for b, (n0, n1) in enumerate(((0, 4), (4, FT))):
                    act.wait_ge(c["hid_t"], i + 1)
                    if not (isinstance(i, int) and i == 0):
                        act.wait_ge(c["down"], i)
                    nc.scalar.activation(hdT_hi[:, n0:n1, :], ps_h[b][:, 0:(n1 - n0) * P].rearrange("p (n t) -> p n t", t=P),
                                         ACT.Copy).then_inc(c["hdT_hi"], 1)

            def tile(i, r):
                tokens(i + 1, 1 - r)
                silu(i, 0)
                hidden_hi(i - 1)
                silu(i, 1)

            ln_sd(act, lns[1], 1)
            logits(0)
            for i in range(PAIRS, NT):
                for m in LATE_TURNS[i]:
                    turn_act(act, m)
                ln_high(act, lns[1], i)
            tokens(0, 0)
            logits(1)
            tokens(1, 1)
            silu(0, 0)
            act.wait_ge(c["x_lg"], 1)
            nc.scalar.activation(x_ex[:, :, :], x_lg[:, :, :], ACT.Exp, bias=zero_b[:, 0:1]).then_inc(c["x_ex"], 1)
            silu(0, 1)
            tile(1, 1)
            tile(2, 0)
            with act.Fori(1, NT // 2 - 1) as m:
                tile(2 * m + 1, 1)
                tile(2 * m + 2, 0)
            silu(NT - 1, 0)
            hidden_hi(NT - 2)
            silu(NT - 1, 1)
            ln_sd(act, lns[2], 0)
            for i in range(PAIRS):
                ln_high(act, lns[2], i)
            for j in range(2):
                att_wq_high(act, 1, 0, j)
            hidden_hi(NT - 1)
            for j in range(2, J):
                att_wq_high(act, 1, 0, j)
            ln_sd(act, lns[2], 1)

        def moe_pool(pool):
            c = moe
            pool.wait_ge(*att[0]("y_added", 2 * G * PAIRS))
            nc.gpsimd.memset(x_top[:, :, :], -1.0).then_inc(c["top_clear"], 1)

            def tokens(i, r):
                if not (isinstance(i, int) and i < 2):
                    pool.wait_ge(c["u_done"], 2 * i - 2)
                nc.gpsimd.tensor_copy(f_lo[:, r, :, :], hT_lo[:, :, bass.ts(i, P)].bitcast(F32)).then_inc(c["f_lo"], 1)

            def weigh(i, half):
                pool.wait_ge(c["gu"], 2 * i + half + 1)
                if not (isinstance(i, int) and i == 0):
                    pool.wait_ge(c["hid_t"], i)
                w = x_w[:, bass.ds(i, 1), half * XH:(half + 1) * XH].rearrange("p o e -> p (o e)")
                nc.gpsimd.tensor_tensor(hid[:, half * FH:(half + 1) * FH].rearrange("p (e n) -> p e n", e=XH),
                                        gu[:, half, :].rearrange("p (e n) -> p e n", e=XH), wide(w, INTER), ALU.mult).then_inc(c["hid"], 1)

            def tile(i, r, after):
                if after:
                    tokens(i + 1, 1 - r)
                weigh(i, 0)
                weigh(i, 1)

            pool.wait_ge(c["w_t"], len(turns))
            pool.wait_ge(*lns[1]("lo", NT))
            tokens(0, 0)
            pool.wait_ge(c["x_w"], 1)
            tile(0, 0, True)
            tile(1, 1, True)
            tile(2, 0, True)
            with pool.Fori(1, NT // 2 - 1) as m:
                tile(2 * m + 1, 1, True)
                tile(2 * m + 2, 0, True)
            tile(NT - 1, 1, False)

        def moe_dve(dve):
            c = moe

            def gated(i, half):
                dve.wait_ge(c["silu"], 2 * i + half + 1)
                dve.wait_ge(c["u_done"], 2 * i + half + 1)
                if not (isinstance(i, int) and i == 0):
                    dve.wait_ge(c["hid"], 2 * i + half - 1)
                nc.vector.tensor_tensor(gu[:, half, :], ps_b[half][:, 0:FH], sg[:, half, :], ALU.mult).then_inc(c["gu"], 1)

            def hidden_lo(i):
                for b, (n0, n1) in enumerate(((0, 4), (4, FT))):
                    dve.wait_ge(c["hdT_hi"], 2 * i + b + 1)
                    nc.vector.tensor_tensor(hdT_lo[:, n0:n1, :], ps_h[b][:, 0:(n1 - n0) * P].rearrange("p (n t) -> p n t", t=P),
                                            hdT_hi[:, n0:n1, :].bitcast(F32), ALU.subtract).then_inc(c["hdT_lo"], 1)

            def add_output(i, r):
                dve.wait_ge(c["down"], i + 1)
                xi = x_sb[:, bass.ds(i, 1), :].rearrange("p o e -> p (o e)")
                nc.vector.scalar_tensor_tensor(xi, ps_b[2 + r][:, :], gates[:, 2:3], xi, ALU.mult, ALU.add).then_inc(c["x_added"], 1)

            def tile(i, r):
                gated(i, 0)
                hidden_lo(i - 1)
                gated(i, 1)
                add_output(i - 1, 1 - r)

            def late_turns(i):
                for m in LATE_TURNS[i]:
                    turn_dve(dve, m)

            ln_rs(dve, lns[1], 1)
            ln_second(dve, lns[1], late_turns)
            gated(0, 0)
            lg = ps_h[0][:, 0:NT * NX].rearrange("p (i e) -> p i e", e=NX)
            dve.wait_ge(c["lg_t"], 1)
            nc.vector.tensor_reduce(x_mx[:, :], lg, AX, ALU.max).then_inc(c["route"], 1)
            dve.wait_ge(c["route"], 1)
            nc.vector.tensor_tensor(x_lg[:, :, :], lg, wide(x_mx[:, :], NX), ALU.subtract).then_inc(c["x_lg"], 1)
            gated(0, 1)
            dve.wait_ge(c["x_ex"], 1)
            nc.vector.tensor_reduce(x_sum[:, :], x_ex[:, :, :], AX, ALU.add).then_inc(c["route"], 1)
            dve.wait_ge(c["route"], 2)
            nc.vector.reciprocal(x_rec[:, :], x_sum[:, :]).then_inc(c["route"], 1)
            dve.wait_ge(c["route"], 3)
            nc.vector.tensor_tensor(x_p[:, :, :], x_ex[:, :, :], wide(x_rec[:, :], NX), ALU.mult).then_inc(c["route"], 1)
            dve.wait_ge(c["route"], 4)
            for i in range(NT):
                nc.vector.max(x_rep[:, i, 0:8], x_p[:, i, :]).then_inc(c["route"], 1)
            dve.wait_ge(c["route"], 4 + NT)
            dve.wait_ge(c["top_clear"], 1)
            nc.vector.tensor_copy(x_top[:, :, 0:2], x_rep[:, :, 0:2]).then_inc(c["route"], 1)
            nc.vector.tensor_tensor(x_two[:, :], x_rep[:, :, 0], x_rep[:, :, 1], ALU.add).then_inc(c["route"], 1)
            dve.wait_ge(c["route"], 6 + NT)
            nc.vector.reciprocal(x_rec[:, :], x_two[:, :]).then_inc(c["route"], 1)
            for i in range(NT):
                nc.vector.match_replace(x_rep[:, i, :], x_top[:, i, :], x_p[:, i, :], -1.0).then_inc(c["route"], 1)
            dve.wait_ge(c["route"], 7 + 2 * NT)
            nc.vector.tensor_scalar(x_rep[:, :, :], x_rep[:, :, :], 0.0, None, ALU.max).then_inc(c["route"], 1)
            dve.wait_ge(c["route"], 8 + 2 * NT)
            nc.vector.tensor_tensor(x_p[:, :, :], x_p[:, :, :], x_rep[:, :, :], ALU.subtract).then_inc(c["route"], 1)
            dve.wait_ge(c["route"], 9 + 2 * NT)
            nc.vector.tensor_tensor(x_w[:, :, :], x_p[:, :, :], wide(x_rec[:, :], NX), ALU.mult).then_inc(c["x_w"], 1)

            tile(1, 1)
            tile(2, 0)
            with dve.Fori(1, NT // 2 - 1) as m:
                tile(2 * m + 1, 1)
                tile(2 * m + 2, 0)
            gated(NT - 1, 0)
            hidden_lo(NT - 2)
            ln_stats(dve, lns[2], 0, lambda i: (c["x_added"], i + 1))
            gated(NT - 1, 1)
            ln_rs(dve, lns[2], 0)
            ln_norm(dve, lns[2], 0)
            ln_norm(dve, lns[2], 1)
            ln_low(dve, lns[2], 0)
            ln_norm(dve, lns[2], 2)
            ln_low(dve, lns[2], 1)
            ln_norm(dve, lns[2], 3)
            add_output(NT - 2, 0)
            ln_low(dve, lns[2], 2)
            ln_low(dve, lns[2], 3)
            for j in range(2):
                att_wq_low_turned(dve, 0, j)
            hidden_lo(NT - 1)
            for j in range(2, J):
                att_wq_low_turned(dve, 0, j)
            add_output(NT - 1, 1)

        def lora_load(sp):
            c = lora
            sp.dma_start(a_raw[0:LM, :], lora_a.rearrange("e r f -> (e r) f")).then_inc(c["a_in"], 16)
            sp.dma_start(a_raw[LM:LM + LX, :], lora_r).then_inc(c["a_in"], 16)
            for e in range(LX):
                sp.dma_start(b_raw[:, :, e, :], lora_b[e].rearrange("(n p) r -> p n r", p=P)).then_inc(c["b_in"], 16)

        def lora_sync(sp):
            c = lora
            for i in range(NT):
                sp.wait_ge(c["x_added"], i + 1)
                sp.dma_start(ot[:, i, :], x_sb[:, i, :]).then_inc(c["out"], 16)
            sp.wait_ge(c["out"], 16 * NT)

        LN = LM + LX
        delta_banks = [ps_b[2], ps_b[3]] + ps_h

        def lora_beside_pe(h, t):
            if h:
                ln_turn(nc.tensor, lns[3], t)
            if (h, t) == (0, -1):
                nc.tensor.wait_ge(*att[1]("q_rot", J * 2 * G))
                nc.tensor.wait_ge(lora["a_in"], 32)
                for k in range(KC):
                    last = nc.tensor.transpose(ps_q[0][:, k * P:k * P + LN], a_raw[:, k * P:(k + 1) * P], ident[0:LN, 0:LN])
                last.then_inc(lora["w_t"], 1)
                nc.tensor.wait_ge(lora["b_in"], 16 * LX)
                for k in range(LO // P):
                    last = nc.tensor.transpose(ps_q[1][0:LM, k * P:(k + 1) * P], b_raw[:, k, :, :].rearrange("p e r -> p (e r)"), ident[:, :])
                last.then_inc(lora["w_t"], 1)

        def lora_beside_act(h, t):
            if (h, t) == (0, -1):
                nc.scalar.wait_ge(lora["w_t"], 1)
                nc.scalar.activation(aT_hi[:, :, 0:LN], ps_q[0].rearrange("p (k i) -> p k i", k=KC)[:, :, 0:LN], ACT.Copy).then_inc(lora["w_hi"], 1)
                nc.scalar.wait_ge(lora["w_t"], 2)
                nc.scalar.activation(bT_hi[:, :], ps_q[1][0:LM, :], ACT.Copy, scale=LORA_SCALE).then_inc(lora["w_hi"], 1)

        def lora_beside_dve(h, t):
            if (h, t) == (0, -1):
                nc.vector.memset(aT_hi[:, :, LN:P].bitcast(F32), 0.0).then_inc(lora["a_zero"], 1)
                nc.vector.memset(aT_lo[:, :, LN:P].bitcast(F32), 0.0).then_inc(lora["a_zero"], 1)
                nc.vector.wait_ge(*att[1]("q_done", J * 2 * G))
                nc.vector.memset(l_lg[:, :, :], -BIG).then_inc(lora["l_clear"], 1)
                nc.vector.memset(l_top[:, :, :], NO_MATCH).then_inc(lora["l_clear"], 1)
                nc.vector.wait_ge(lora["w_hi"], 1)
                nc.vector.tensor_tensor(aT_lo[:, :, 0:LN], ps_q[0].rearrange("p (k i) -> p k i", k=KC)[:, :, 0:LN],
                                        aT_hi[:, :, 0:LN].bitcast(F32), ALU.subtract).then_inc(lora["w_lo"], 1)
                nc.vector.wait_ge(lora["w_hi"], 2)
                nc.vector.scalar_tensor_tensor(bT_lo[:, :], ps_q[1][0:LM, :], LORA_SCALE, bT_hi[:, :].bitcast(F32), ALU.mult,
                                               ALU.subtract).then_inc(lora["w_lo"], 1)

        def lora_pe(pe):
            c = lora

            def mid(h):
                pe.wait_ge(*lns[3]("lo", (h + 1) * PAIRS))
                for k in range(KC):
                    last = three(ps_q[h][:, :], aT_hi[:, k, :], aT_lo[:, k, :], hT_hi[:, k, h * HALF:(h + 1) * HALF],
                                 hT_lo[:, k, h * HALF:(h + 1) * HALF], k == 0, k == KC - 1)
                last.then_inc(c["mid"], 1)

            def mid_t(h):
                pe.wait_ge(c["m_T"], h + 1)
                for t in range(PAIRS):
                    i = h * PAIRS + t
                    last = nc.tensor.transpose(ps_b[h][:, t * P:t * P + LN], m_T[:, i * P:(i + 1) * P], ident[0:LN, 0:LN])
                last.then_inc(c["mid_t"], 1)

            def gated_t(h):
                pe.wait_ge(c["gated"], h + 1)
                for t in range(PAIRS):
                    last = nc.tensor.transpose(ps_q[h][0:LM, t * P:(t + 1) * P], l_m[:, h * PAIRS + t, :, :].rearrange("p e r -> p (e r)"),
                                               ident[:, :])
                last.then_inc(c["gated_t"], 1)

            def delta(i):
                if i % PAIRS == 0:
                    pe.wait_ge(c["mT_lo"], i // PAIRS + 1)
                if i >= 4:
                    pe.wait_ge(c["x_added"], i - 3)
                three(delta_banks[i % 4][:, :], mT_hi[:, i * P:(i + 1) * P], mT_lo[:, i * P:(i + 1) * P], bT_hi[:, :], bT_lo[:, :],
                      True, True).then_inc(c["delta"], 1)

            pe.wait_ge(c["w_lo"], 2)
            pe.wait_ge(c["a_zero"], 2)
            pe.wait_ge(*att[1]("y_added", 2 * G * PAIRS))
            mid(0)
            ln_turn(pe, lns[3], PAIRS)
            ln_turn(pe, lns[3], PAIRS + 1)
            mid_t(0)
            ln_turn(pe, lns[3], PAIRS + 2)
            ln_turn(pe, lns[3], PAIRS + 3)
            mid(1)
            mid_t(1)
            for h in range(2):
                gated_t(h)
                for t in range(PAIRS):
                    delta(h * PAIRS + t)

        def lora_act(act):
            c = lora

            def mid(h):
                act.wait_ge(c["mid"], h + 1)
                nc.scalar.activation(m_T[:, h * HALF:(h + 1) * HALF], ps_q[h][0:LN, :], ACT.Copy).then_inc(c["m_T"], 1)

            mid(0)
            ln_sd(act, lns[3], 1)
            for i in range(PAIRS, NT):
                ln_high(act, lns[3], i)
            mid(1)
            for h in range(2):
                act.wait_ge(c["l_lg"], 2 * h + 2)
                own = slice(h * PAIRS, (h + 1) * PAIRS)
                nc.scalar.activation(l_ex[:, own, :], l_lg[:, own, 0:LX], ACT.Exp, bias=zero_b[:, 0:1]).then_inc(c["l_ex"], 1)
                act.wait_ge(c["gated_t"], h + 1)
                nc.scalar.activation(mT_hi[:, h * HALF:(h + 1) * HALF], ps_q[h][0:LM, :], ACT.Copy).then_inc(c["mT_hi"], 1)

        def lora_dve(dve):
            c = lora
            steps = 7 + 2 * PAIRS

            def route(h):
                own = slice(h * PAIRS, (h + 1) * PAIRS)
                tiles = range(h * PAIRS, (h + 1) * PAIRS)
                mid = ps_b[h].rearrange("p (i m) -> p i m", m=P)
                done = steps * h
                dve.wait_ge(c["l_clear"], 2)
                dve.wait_ge(c["mid_t"], h + 1)
                nc.vector.tensor_copy(l_lg[:, own, 0:LX], mid[:, :, LM:LN]).then_inc(c["route"], 1)
                dve.wait_ge(c["route"], done + 1)
                for i in tiles:
                    nc.vector.max(l_rep[:, i, :], l_lg[:, i, :]).then_inc(c["route"], 1)
                dve.wait_ge(c["route"], done + 1 + PAIRS)
                nc.vector.tensor_copy(l_top[:, own, 0:2], l_rep[:, own, 0:2]).then_inc(c["route"], 1)
                nc.vector.tensor_copy(l_mx[:, own], l_rep[:, own, 0]).then_inc(c["route"], 1)
                dve.wait_ge(c["route"], done + 3 + PAIRS)
                for i in tiles:
                    nc.vector.match_replace(l_rep[:, i, :], l_top[:, i, :], l_lg[:, i, :], TAKEN).then_inc(c["route"], 1)
                dve.wait_ge(c["route"], done + 3 + 2 * PAIRS)
                nc.vector.tensor_scalar(l_rep[:, own, :], l_rep[:, own, :], TAKEN, -BIG, ALU.is_lt, ALU.mult).then_inc(c["route"], 1)
                nc.vector.tensor_tensor(l_lg[:, own, 0:LX], l_lg[:, own, 0:LX], wide(l_mx[:, own], LX), ALU.subtract).then_inc(c["l_lg"], 1)
                dve.wait_ge(c["route"], done + 4 + 2 * PAIRS)
                dve.wait_ge(c["l_lg"], 2 * h + 1)
                nc.vector.tensor_tensor(l_lg[:, own, 0:LX], l_lg[:, own, 0:LX], l_rep[:, own, 0:LX], ALU.add).then_inc(c["l_lg"], 1)

            def gate(h):
                own = slice(h * PAIRS, (h + 1) * PAIRS)
                mid = ps_b[h].rearrange("p (i m) -> p i m", m=P)
                done = steps * h + 4 + 2 * PAIRS
                dve.wait_ge(c["l_ex"], h + 1)
                nc.vector.tensor_reduce(l_sum[:, own], l_ex[:, own, :], AX, ALU.add).then_inc(c["route"], 1)
                dve.wait_ge(c["route"], done + 1)
                nc.vector.reciprocal(l_rec[:, own], l_sum[:, own]).then_inc(c["route"], 1)
                dve.wait_ge(c["route"], done + 2)
                nc.vector.tensor_tensor(l_ex[:, own, :], l_ex[:, own, :], wide(l_rec[:, own], LX), ALU.mult).then_inc(c["route"], 1)
                dve.wait_ge(c["route"], done + 3)
                for e in range(LX):
                    last = nc.vector.tensor_tensor(l_m[:, own, e, :], mid[:, :, e * LR:(e + 1) * LR], wide(l_ex[:, own, e], LR), ALU.mult)
                    last.then_inc(c["gated" if e == LX - 1 else "gating"], 1)

            def mid_low(h):
                dve.wait_ge(c["mT_hi"], h + 1)
                nc.vector.tensor_tensor(mT_lo[:, h * HALF:(h + 1) * HALF], ps_q[h][0:LM, :], mT_hi[:, h * HALF:(h + 1) * HALF].bitcast(F32),
                                        ALU.subtract).then_inc(c["mT_lo"], 1)

            def add_output(i):
                dve.wait_ge(c["delta"], i + 1)
                nc.vector.scalar_tensor_tensor(x_sb[:, i, :], delta_banks[i % 4][:, :], gates[:, 3:4], x_sb[:, i, :],
                                               ALU.mult, ALU.add).then_inc(c["x_added"], 1)

            ln_rs(dve, lns[3], 1)
            ln_second(dve, lns[3], lambda i: None)
            route(0)
            gate(0)
            mid_low(0)
            route(1)
            for t in range(PAIRS):
                add_output(t)
            gate(1)
            mid_low(1)
            for t in range(PAIRS):
                add_output(PAIRS + t)

        @block.sync
        def _(sp):
            prep_sync(sp)
            kv_sync(sp)
            att_sync(sp, 0)
            moe_sync(sp)
            att_sync(sp, 1)
            lora_sync(sp)

        @block.gpsimd
        def _(pool):
            prep_pool(pool)
            kv_pool(pool)
            att_pool(pool, 0)
            moe_pool(pool)
            att_pool(pool, 1)

        @block.scalar
        def _(act):
            act.wait_ge(prep["consts"], 4)
            prep_act(act)
            kv_act(act)
            act.wait_ge(prep["gates_in"], 32)
            nc.scalar.activation(gates[:, :], gates_in[:, :], ACT.Tanh, bias=zero_b[:, 0:1]).then_inc(prep["gates"], 1)
            att_act(act, 0, moe_beside_act)
            moe_act(act)
            att_act(act, 1, lora_beside_act)
            lora_act(act)

        @block.tensor
        def _(pe):
            prep_pe(pe)
            kv_pe(pe)
            att_pe(pe, 0, moe_beside_pe)
            moe_pe(pe)
            att_pe(pe, 1, lora_beside_pe)
            lora_pe(pe)

        @block.vector
        def _(dve):
            prep_dve(dve)
            kv_dve(dve)
            att_dve(dve, 0, moe_beside_dve)
            moe_dve(dve)
            att_dve(dve, 1, lora_beside_dve)
            lora_dve(dve)


_INS = ["x", "ctx_4096", "pos_BxS2", "mask_BxSxS2_ik0", "mask_1x1xSxS2_ff0", "g_xattn", "g_ffn", "L0_xattn_Wq", "L0_xattn_Wk",
        "L0_xattn_Wv", "L0_xattn_Wo", "L0_ffn_gate_w", "L0_ffn_u", "L0_ffn_g", "L0_ffn_d", "L1_xattn_Wq", "L1_xattn_Wk", "L1_xattn_Wv",
        "L1_xattn_Wo", "L1_xattn_q_norm_w", "L1_xattn_k_norm_w", "L1_ffn_A", "L1_ffn_B", "L1_ffn_Wr"]


def kernel(**inputs):
    import concourse.bacc as bacc
    from concourse.bass_utils import run_bass_kernel_spmd

    nc = bacc.Bacc("TRN2", target_bir_lowering=False, num_devices=1)
    arrays, args = {}, []
    for name in _INS:
        a = np.ascontiguousarray(inputs[name])
        arrays[f"in_{name}"] = a
        args.append(nc.dram_tensor(f"in_{name}", a.shape, mybir.dt.from_np(a.dtype), kind="ExternalInput").ap())
    for name, table in zip(("rope_q_table", "rope_k_table"), rope_constants()):
        arrays[name] = table
        args.append(nc.dram_tensor(name, table.shape, F32, kind="ExternalInput").ap())
    args.append(nc.dram_tensor("out", (B, S, E), F32, kind="ExternalOutput").ap())
    build(nc, *args)
    r = run_bass_kernel_spmd(nc, [arrays], core_ids=[0])
    return r.results[0]["out"]
```

```python
from contextlib import ExitStack

import concourse.bass as bass
import numpy as np
from concourse import mybir

P = 128
B, S, E = 16, 64, 512
T = B * S
NT = T // P
KC = E // P
H, G, D = 32, 8, 128
J = H // G
GB = 4
NB = G // GB
BW = GB * D
HALF = T // 2
PAIRS = NT // 2
JS = J * S
SC = PAIRS * JS
QB = 32
NQ = SC // QB
MAX_POS, THETA = 512, 10000.0
NX, INTER = 16, 56
FI = NX * INTER
FT = FI // P
FH = FI // 2
XH = NX // 2
LX, LR, LO = 4, 16, 512
LM = LX * LR
LORA_SCALE = 16.0 / float(np.sqrt(16.0))
EPS = 1e-5
MASKED = -1000000000.0
BIG = 3.0e38
TAKEN, NO_MATCH = 3.3e38, 3.2e38

F32 = mybir.dt.float32
FR = mybir.dt.float32r
I32 = mybir.dt.int32
ALU = mybir.AluOpType
ACT = mybir.ActivationFunctionType
AX = mybir.AxisListType.X


def rope_constants():
    inv = np.float32(1.0) / np.float32(THETA) ** (np.arange(0, D, 2, dtype=np.float32) / np.float32(D))
    ang = np.arange(MAX_POS, dtype=np.float32)[:, None] * inv.astype(np.float32)[None, :]
    c, s = np.cos(ang).astype(np.float32), np.sin(ang).astype(np.float32)
    q = np.float32(1.0 / np.sqrt(D))
    return np.concatenate([c * q, c * q, s * q, -s * q], axis=1), np.concatenate([c, s], axis=1)


def build(nc, x, ctx_in, pos, mask0, mask1, g_xattn, g_ffn, Wq0, Wk0, Wv0, Wo0, gate_w, up_w, glu_w, down_w,
          Wq1, Wk1, Wv1, Wo1, q_norm, k_norm, lora_a, lora_b, lora_r, rope_q_table, rope_k_table, out):
    stack = ExitStack()

    class Stage:

        def __init__(self, name, again=None, earlier=None):
            self.name, self.made, self.earlier = name, again.made if again else {}, earlier or {}

        def __getitem__(self, what):
            if what not in self.made:
                self.made[what] = stack.enter_context(nc.semaphore(f"{self.name}_{what}"))
            return self.made[what]

        def __call__(self, what, n):
            return self[what], n + self.earlier.get(what, 0)

    def alloc(where, *buffers):
        return [where.enter_context(nc.sbuf_tensor(n, shape, dt)) for n, shape, dt in buffers]

    with stack:
        ps_q = [stack.enter_context(nc.psum_tensor(f"ps_q{i}", [P, 512], F32)) for i in range(2)]
        ps_s = stack.enter_context(nc.psum_tensor("ps_s", [P, SC], F32))
        ps_b = [stack.enter_context(nc.psum_tensor(f"ps_b{i}", [P, 512], F32)) for i in range(4)]
        ps_h = [ps_s[:, 0:512], ps_s[:, 512:1024]]

        (x_sb, hT_hi, hT_lo, cos_q, sin_q, ident, ones, gates_in, gates, eps_ln, eps_rms, zero_b, ln_buf, ln_stats_sb, ln_mv,
         ln_sd_sb, ln_rs_sb) = alloc(
            stack, ("x_sb", [P, NT, E], F32), ("hT_hi", [P, KC, T], FR), ("hT_lo", [P, KC, T], FR),
            ("cos_q", [P, T], F32), ("sin_q", [P, T], F32), ("ident", [P, P], F32), ("ones", [P, S], F32),
            ("gates_in", [P, 4], F32), ("gates", [P, 4], F32), ("eps_ln", [P, 1], F32), ("eps_rms", [P, 1], F32),
            ("zero_b", [P, 1], F32), ("ln_buf", [P, 2, E], F32), ("ln_stats", [P, NT, 6], F32), ("ln_mv", [P, NT, 2], F32),
            ("ln_sd", [P, NT], F32), ("ln_rs", [P, NT], F32))
        mask_i, = alloc(stack, ("mask_i", [P, 2, PAIRS, 2, QB], I32))

        kT_dram = nc.dram_tensor("kT_spill", [2, G, P, T], F32, kind="Internal").ap()
        v_hi_dram = nc.dram_tensor("v_hi_spill", [2, G, P, T], F32, kind="Internal").ap()
        v_lo_dram = nc.dram_tensor("v_lo_spill", [2, G, P, T], F32, kind="Internal").ap()

        pair = lambda *parts: [f for f in zip(*parts)]
        with ExitStack() as a:
            kw_first = alloc(a, ("kw_raw0", [P, KC, BW], F32), ("kw_hi0", [P, KC, BW], FR), ("kw_lo0", [P, KC, BW], FR))
        with ExitStack() as a:
            wq_raw, wq_hi, wq_lo = alloc(a, ("wq_raw", [P, KC, J * D], F32), ("wq_hi", [P, KC, J * D], FR), ("wq_lo", [P, KC, J * D], FR))
        with ExitStack() as a:
            u_raw, r_raw, rT_hi, rT_lo, gu1 = alloc(a, ("u_raw", [P, FT, E], F32), ("r_raw", [NX, E], F32), ("rT_hi", [P, KC, P], FR),
                                                    ("rT_lo", [P, KC, P], FR), ("gu1", [P, 2, FH], F32))
        with ExitStack() as a:
            d_raw, = alloc(a, ("d_raw", [P, KC, FI], F32))
        with ExitStack() as a:
            l_lg, l_top, l_rep, l_mx, l_ex, l_sum, l_rec, m_T, l_m, mT_hi, mT_lo = alloc(
                a, ("l_lg", [P, NT, 8], F32), ("l_top", [P, NT, 8], F32), ("l_rep", [P, NT, 8], F32), ("l_mx", [P, NT], F32),
                ("l_ex", [P, NT, LX], F32), ("l_sum", [P, NT], F32), ("l_rec", [P, NT], F32), ("m_T", [LM + LX, T], F32),
                ("l_m", [P, NT, LX, LR], F32), ("mT_hi", [LM, T], FR), ("mT_lo", [LM, T], FR))
        alloc(stack, ("region_first", [P, 3 * KC * BW], F32))

        with ExitStack() as here:
            pos_i, pos_f, pos_t, pos_ix = alloc(
                here, ("pos_i", [NT, P], I32), ("pos_f", [NT, P], F32), ("pos_t", [NT, P], F32), ("pos_ix", [P, NT], I32))
            (cT_hi, cT_lo, rope_k, kw_raw1, kw_hi1, kw_lo1, k_t1, k_t2, k_sq, k_ss) = alloc(
                here, ("cT_hi", [P, KC, T], FR), ("cT_lo", [P, KC, T], FR), ("rope_k", [P, NT, D], F32),
                ("kw_raw1", [P, KC, BW], F32), ("kw_hi1", [P, KC, BW], FR), ("kw_lo1", [P, KC, BW], FR),
                ("k_t1", [P, 2, BW], F32), ("k_t2", [P, 2, BW], F32), ("k_sq", [P, BW], F32), ("k_ss", [P, 3, GB], F32))
            kw_raw, kw_hi, kw_lo = pair(kw_first, (kw_raw1, kw_hi1, kw_lo1))
            with ExitStack() as a:
                c_raw, rope_q = alloc(a, ("c_raw", [P, NT, E], F32), ("rope_q", [P, NT, 2 * D], F32))
            with ExitStack() as a:
                kT_st, vs_hi, vs_lo = alloc(
                    a, ("kT_st", [P, GB, T], F32), ("vs_hi", [P, NT, BW], FR), ("vs_lo", [P, NT, BW], FR))

        with ExitStack() as a:
            g_raw, = alloc(a, ("g_raw", [P, FT, E], F32))
        with ExitStack() as a:
            f_hi, f_lo, sg, gu, hid = alloc(
                a, ("f_hi", [P, 2, KC, P], FR), ("f_lo", [P, 2, KC, P], FR), ("sg", [P, 2, FH], F32), ("gu", [P, 2, FH], F32),
                ("hid", [P, FI], F32))
        with ExitStack() as a:
            a_raw, b_raw, aT_hi, aT_lo, bT_hi, bT_lo = alloc(
                a, ("a_raw", [LM + LX, E], F32), ("b_raw", [P, LO // P, LX, LR], F32), ("aT_hi", [P, KC, P], FR),
                ("aT_lo", [P, KC, P], FR), ("bT_hi", [LM, LO], FR), ("bT_lo", [LM, LO], FR))
        alloc(stack, ("region_second", [P, 4 * KC * P + 4 * FH + FI], F32))

        with ExitStack() as here:
            qT, kT = alloc(here, ("qT", [P, 2, J, HALF], F32), ("kT", [P, 2, HALF], F32))
            with ExitStack() as a:
                q_t1, q_t2 = alloc(a, ("q_t1", [P, 2, HALF], F32), ("q_t2", [P, 2, HALF], F32))
            q_sq, = alloc(here, ("q_sq", [P, J, HALF], F32))
            wo_raw, = alloc(here, ("wo_raw", [P, J, E], F32))
            with ExitStack() as a:
                keep0, offset0 = alloc(a, ("keep0", [P, 2, PAIRS, 2, QB], F32), ("offset0", [P, 2, PAIRS, 2, QB], F32))
            r_q, = alloc(here, ("r_q", [P, SC], F32))
            s_sb, p_sb, pT, p_hi, p_lo, v_hi, v_lo = alloc(
                here, ("s_sb", [P, SC], F32), ("p_sb", [P, SC], F32), ("pT", [P, SC], F32), ("p_hi", [P, SC], FR), ("p_lo", [P, SC], FR),
                ("v_hi", [P, NT, D], FR), ("v_lo", [P, NT, D], FR))
            o_hi, o_lo, wo_hi, wo_lo = alloc(here, ("o_hi", [P, PAIRS, J, P], FR), ("o_lo", [P, PAIRS, J, P], FR),
                                             ("wo_hi", [P, J, E], FR), ("wo_lo", [P, J, E], FR))
            mx_a, mx_b, mx_c, sm_a, sm_b, sm_c, p_rec, mask1_sb, qk_in, qk_w = alloc(
                here, ("mx_a", [P, NQ], F32), ("mx_b", [P, NQ], F32), ("mx_c", [P, NQ], F32), ("sm_a", [P, NQ], F32),
                ("sm_b", [P, NQ], F32), ("sm_c", [P, NQ], F32), ("p_rec", [P, NQ], F32), ("mask1_sb", [P, 2, QB], F32),
                ("qk_in", [P, 2], F32), ("qk_w", [P, 1], F32))
        with ExitStack() as here:
            gT_hi, gT_lo, x_lgT, uT_hi, uT_lo, dT_hi, dT_lo = alloc(
                here, ("gT_hi", [P, KC, FI], FR), ("gT_lo", [P, KC, FI], FR), ("x_lgT", [NX, T], F32), ("uT_hi", [P, KC, FI], FR),
                ("uT_lo", [P, KC, FI], FR), ("dT_hi", [P, FT, E], FR), ("dT_lo", [P, FT, E], FR))
            (hdT_hi, hdT_lo, x_lg, x_mx, x_ex, x_sum, x_rec, x_p, x_top, x_rep, x_two, x_w) = alloc(
                here, ("hdT_hi", [P, FT, P], FR), ("hdT_lo", [P, FT, P], FR), ("x_lg", [P, NT, NX], F32), ("x_mx", [P, NT], F32), ("x_ex", [P, NT, NX], F32),
                ("x_sum", [P, NT], F32), ("x_rec", [P, NT], F32), ("x_p", [P, NT, NX], F32), ("x_top", [P, NT, 8], F32),
                ("x_rep", [P, NT, NX], F32), ("x_two", [P, NT], F32), ("x_w", [P, NT, NX], F32))

        prep, kv = Stage("prep"), Stage("kv")
        units = 2 * G
        att_signals = {"wq_in": 16 * G, "wo_in": 16 * G, "k_in0": 16 * G, "k_in1": 16 * G, "v_in": 32 * G, "mask_in": 16 * 4 * 2 * 2,
                       "wq_hi": J * G, "wq_lo": J * G, "wo_hi": J * G, "wo_lo": J * G}
        for per_unit, names in ((1, "scored s_turned s_masked mx_part mx_other s_max s_shifted p_exp sm_part sm_other sm_all p_rec "
                                    "p_normed p_turned p_hi p_lo"),
                                (J, "q_done q_rot o_done o_hi o_lo y_done y_added")):
            for name in names.split():
                att_signals[name] = per_unit * units
        ln_signals = {"sd": 2, "rs": 2} | dict.fromkeys(("stats", "moments", "normed", "transposed", "hi", "lo"), NT)
        att = [Stage("att")]
        att.append(Stage("att", att[0], att_signals))
        lns = [Stage("ln")]
        for n in range(1, 4):
            lns.append(Stage("ln", lns[0], {k: n * v for k, v in ln_signals.items()}))
        moe, lora = Stage("moe"), Stage("lora")
        xt = x.flatten_outer_dims().rearrange("(i p) e -> p i e", p=P)
        ct = ctx_in.flatten_outer_dims().rearrange("(i p) e -> p i e", p=P)
        ot = out.flatten_outer_dims().rearrange("(i p) e -> p i e", p=P)
        WQ, WK, WV, WO = [Wq0, Wq1], [Wk0, Wk1], [Wv0, Wv1], [Wo0, Wo1]

        block = stack.enter_context(nc.Block())

        def wide(t, inner):
            return t.unsqueeze(2).to_broadcast([t.shape[0], t.shape[1], inner])

        def three(dst, l_hi, l_lo, r_hi, r_lo, first, last):
            nc.tensor.matmul(dst, l_hi, r_hi, start=first, stop=False)
            nc.tensor.matmul(dst, l_hi, r_lo, start=False, stop=False)
            return nc.tensor.matmul(dst, l_lo, r_hi, start=False, stop=last)

        def ln_stat(dve, c, i, done):
            dve.wait_ge(*done(i))
            nc.vector.bn_stats(ln_stats_sb[:, i, :], x_sb[:, i, :]).then_inc(c["stats"], 1)
            dve.wait_ge(*c("stats", i + 1))
            nc.vector.bn_aggr(ln_mv[:, i, :], ln_stats_sb[:, i, :]).then_inc(c["moments"], 1)

        def ln_stats(dve, c, h, done):
            for i in range(h * PAIRS, (h + 1) * PAIRS):
                ln_stat(dve, c, i, done)

        HALVES = ((0, PAIRS), (PAIRS, NT))
        PARTS = ((0, PAIRS), (PAIRS, NT - 1), (NT - 1, NT))

        def ln_sd(act, c, h, parts=HALVES):
            act.wait_ge(*c("moments", parts[h][1]))
            own = slice(*parts[h])
            nc.scalar.activation(ln_sd_sb[:, own], ln_mv[:, own, 1], ACT.Sqrt, bias=eps_ln[:, 0:1]).then_inc(c["sd"], 1)

        def ln_rs(dve, c, h, parts=HALVES):
            dve.wait_ge(*c("sd", h + 1))
            own = slice(*parts[h])
            nc.vector.reciprocal(ln_rs_sb[:, own], ln_sd_sb[:, own]).then_inc(c["rs"], 1)

        def ln_norm(dve, c, i):
            if i % PAIRS == 0:
                dve.wait_ge(*c("rs", i // PAIRS + 1))
            if i >= 2:
                dve.wait_ge(*c("transposed", i - 1))
            nc.vector.tensor_scalar(ln_buf[:, i % 2, :], x_sb[:, i, :], ln_mv[:, i, 0:1], ln_rs_sb[:, i:i + 1],
                                    ALU.subtract, ALU.mult).then_inc(c["normed"], 1)

        def ln_turn(pe, c, i):
            pe.wait_ge(*c("normed", i + 1))
            if i >= 2:
                pe.wait_ge(*c("lo", i - 1))
            for k in range(KC):
                last = nc.tensor.transpose(ps_h[i % 2][:, k * P:(k + 1) * P], ln_buf[:, i % 2, k * P:(k + 1) * P], ident[:, :])
            last.then_inc(c["transposed"], 1)

        def ln_high(act, c, i):
            act.wait_ge(*c("transposed", i + 1))
            nc.scalar.activation(hT_hi[:, :, i * P:(i + 1) * P], ps_h[i % 2].rearrange("p (k t) -> p k t", k=KC),
                                 ACT.Copy).then_inc(c["hi"], 1)

        def ln_low(dve, c, i):
            dve.wait_ge(*c("hi", i + 1))
            nc.vector.tensor_tensor(hT_lo[:, :, i * P:(i + 1) * P], ps_h[i % 2].rearrange("p (k t) -> p k t", k=KC),
                                    hT_hi[:, :, i * P:(i + 1) * P].bitcast(F32), ALU.subtract).then_inc(c["lo"], 1)

        def ln_second(dve, c, beside):
            for i in range(PAIRS, PAIRS + 2):
                ln_norm(dve, c, i)
            for i in range(PAIRS, NT):
                beside(i)
                ln_low(dve, c, i)
                if i + 2 < NT:
                    ln_norm(dve, c, i + 2)

        def prep_sync(sp):
            c = prep
            sp.dma_start(pos_i[:, :], pos.rearrange("b s -> (b s)").rearrange("(i p) -> i p", p=P)).then_inc(c["pos"], 16)
            for n in range(NT // 2):
                sp.dma_start(c_raw[:, 2 * n:2 * n + 2, :], ct[:, 2 * n:2 * n + 2, :]).then_inc(c[f"ctx{n}"], 16)
                if n == 0:
                    kv_sync_load(sp, 0, 0)
            kv_sync_load(sp, 0, 1)
            sp.dma_start(gates_in[:, 0:2], g_xattn.partition_broadcast(P)).then_inc(c["gates_in"], 16)
            sp.dma_start(gates_in[:, 2:4], g_ffn.partition_broadcast(P)).then_inc(c["gates_in"], 16)
            sp.dma_start(x_sb[:, :, :], xt).then_inc(c["x"], 16)

        def att_load_mask(sp):
            for h in range(2):
                own = mask0[h * 2 * PAIRS:(h + 1) * 2 * PAIRS].rearrange("(t u) (a q) k -> u a q t k", u=2, q=QB)
                for par in range(2):
                    for kb in range(2):
                        q0 = par * S + kb * QB
                        for a in range(2):
                            sp.dma_start(mask_i[q0:q0 + QB, h, :, a, :], own[par, a, :, :, kb * QB:(kb + 1) * QB]).then_inc(att[0]["mask_in"], 16)

        def prep_pool(pool):
            c = prep
            nc.gpsimd.memset(ident[:, :], 0.0).then_inc(c["cleared"], 1)
            nc.gpsimd.memset(ones[:, :], 1.0).then_inc(c["consts"], 1)
            nc.gpsimd.memset(eps_ln[:, :], EPS).then_inc(c["consts"], 1)
            nc.gpsimd.memset(eps_rms[:, :], D * EPS).then_inc(c["consts"], 1)
            nc.gpsimd.memset(zero_b[:, :], 0.0).then_inc(c["consts"], 1)
            pool.wait_ge(c["cleared"], 1)
            nc.gpsimd.affine_select(out=ident[:, :], in_=ident[:, :], compare_op=ALU.not_equal, fill=1.0, base=0,
                                    pattern=[[-1, P]], channel_multiplier=1).then_inc(c["ident"], 1)
            pool.wait_ge(c["pos_ok"], 5)
            for table, rows, name in ((rope_k_table, rope_k, "rope_k"), (rope_q_table, rope_q, "rope_q")):
                for i in range(NT):
                    nc.gpsimd.indirect_dma_start(rows[:, i, :], None, table, bass.IndirectOffsetOnAxis(ap=pos_ix[:, i:i + 1], axis=0)).then_inc(c[name], 16)

        def prep_dve(dve):
            c = prep
            dve.wait_ge(c["pos"], 16)
            nc.vector.tensor_copy(pos_f[:, :], pos_i[:, :]).then_inc(c["pos_ok"], 1)
            dve.wait_ge(c["pos_ok"], 1)
            nc.vector.tensor_scalar(pos_t[:, :], pos_f[:, :], 0.0, float(MAX_POS), ALU.is_lt, ALU.mult).then_inc(c["pos_ok"], 1)
            dve.wait_ge(c["pos_ok"], 2)
            nc.vector.tensor_tensor(pos_f[:, :], pos_f[:, :], pos_t[:, :], ALU.add).then_inc(c["pos_ok"], 1)
            dve.wait_ge(c["pos_ok"], 3)
            nc.vector.tensor_scalar(pos_f[:, :], pos_f[:, :], 0.0, float(MAX_POS - 1), ALU.max, ALU.min).then_inc(c["pos_ok"], 1)
            dve.wait_ge(c["pos_turned"], 1)
            nc.vector.tensor_copy(pos_ix[:, :], ps_b[0][:, 0:NT]).then_inc(c["pos_ok"], 1)
            for i in range(NT):
                if i >= 4:
                    dve.wait_ge(kv["w0_hi"], i - 3)
                    nc.vector.tensor_tensor(kw_lo[0][:, i - 4, :], kw_raw[0][:, i - 4, :], kw_hi[0][:, i - 4, :].bitcast(F32),
                                            ALU.subtract).then_inc(kv["w0_lo"], 1)
                dve.wait_ge(c["ctx_hi"], i + 1)
                nc.vector.tensor_tensor(cT_lo[:, :, i * P:(i + 1) * P], ps_h[i % 2].rearrange("p (k t) -> p k t", k=KC),
                                        cT_hi[:, :, i * P:(i + 1) * P].bitcast(F32), ALU.subtract).then_inc(c["ctx_lo"], 1)

        def prep_pe(pe):
            c = prep
            pe.wait_ge(c["ident"], 1)
            pe.wait_ge(c["pos_ok"], 4)
            nc.tensor.transpose(ps_b[0][:, 0:NT], pos_f[:, :], ident[0:NT, 0:NT]).then_inc(c["pos_turned"], 1)
            for i in range(NT):
                if i % 2 == 0:
                    pe.wait_ge(c[f"ctx{i // 2}"], 16)
                if i >= 2:
                    pe.wait_ge(c["ctx_lo"], i - 1)
                for k in range(KC):
                    last = nc.tensor.transpose(ps_h[i % 2][:, k * P:(k + 1) * P], c_raw[:, i, k * P:(k + 1) * P], ident[:, :])
                last.then_inc(c["ctx_t"], 1)

        def prep_act(act):
            for i in range(NT):
                if i == 2:
                    kv_weights_hi(act, 0, 0)
                act.wait_ge(prep["ctx_t"], i + 1)
                nc.scalar.activation(cT_hi[:, :, i * P:(i + 1) * P], ps_h[i % 2].rearrange("p (k t) -> p k t", k=KC),
                                     ACT.Copy).then_inc(prep["ctx_hi"], 1)

        def tables_pe(pe, h):
            c = prep
            pe.wait_ge(c["rope_q"], 16 * NT)
            if h:
                pe.wait_ge(c["tables"], 2)
            for kind in range(2):
                for t in range(PAIRS):
                    last = nc.tensor.transpose(ps_b[2 + kind][:, t * P:(t + 1) * P], rope_q[:, h * PAIRS + t, kind * D:(kind + 1) * D], ident[:, :])
                last.then_inc(c["tables_t"], 1)

        def tables_act(act, h):
            for kind in range(2):
                act.wait_ge(prep["tables_t"], 2 * h + kind + 1)
                nc.scalar.activation((cos_q, sin_q)[kind][:, h * HALF:(h + 1) * HALF], ps_b[2 + kind][:, :], ACT.Copy).then_inc(prep["tables"], 1)

        def kv_sync_load(sp, cb, b):
            lay, w = divmod(b, 2)
            src = (WK, WV)[w][lay]
            if lay == 0:
                view = src[:, cb * BW:(cb + 1) * BW].rearrange("(k p) c -> p k c", p=P)
            else:
                view = src[cb * BW:(cb + 1) * BW, :].rearrange("(r p) e -> p r e", p=P)
            sp.dma_start(kw_raw[w][:, :, :], view).then_inc(kv[f"raw{w}"], 16)

        def kv_sync_spill(sp, cb, b):
            c = kv
            lay, w = divmod(b, 2)
            if w == 0:
                sp.wait_ge(c[f"k_staged{lay}"], NT * (cb + 1))
                sp.dma_start(kT_dram[lay, cb * GB:(cb + 1) * GB, :, :].rearrange("g p t -> p g t"), kT_st[:, :, :]).then_inc(c["k_spilled"], 16)
            else:
                sp.wait_ge(c["v_hi"], NT * (2 * cb + lay + 1))
                sp.wait_ge(c["v_lo"], NT * (2 * cb + lay + 1))
                for st, dr in ((vs_hi, v_hi_dram), (vs_lo, v_lo_dram)):
                    for g in range(GB):
                        sp.dma_start(dr[lay, cb * GB + g, :, :].rearrange("p (i d) -> p i d", d=D), st[:, :, g * D:(g + 1) * D].bitcast(F32)).then_inc(c["v_spilled"], 16)

        def kv_sync(sp):
            c = kv
            for cb in range(NB):
                for w in range(2):
                    sp.wait_ge(c["w0_hi"], 8 * cb + 4 * w + 4)
                    sp.wait_ge(c["w0_lo"], 8 * cb + 4 * w + 4)
                    kv_sync_load(sp, cb, 2 + w)
                    if cb == 0 and w:
                        att_load_mask(sp)
                kv_sync_spill(sp, cb, 0)
                sp.wait_ge(c["w1_t"], 8 * cb + 4)
                if cb + 1 < NB:
                    kv_sync_load(sp, cb + 1, 0)
                else:
                    att_load_wq(sp, 0, 0)
                kv_sync_spill(sp, cb, 1)
                if cb + 1 < NB:
                    sp.wait_ge(c["w1_t"], 8 * cb + 8)
                    kv_sync_load(sp, cb + 1, 1)
                kv_sync_spill(sp, cb, 2)
                if cb + 1 == NB:
                    att_wq_split(sp, 0, 1)
                    att_load_wq(sp, 0, 1)
                kv_sync_spill(sp, cb, 3)

        def kv_pe(pe):
            c = kv

            def weights_t(cb, b, k):
                w = b % 2
                if k == 0:
                    pe.wait_ge(c[f"raw{w}"], 16 * (2 * cb + 2))
                n = 8 * cb + 4 * w + k
                if n >= 2:
                    pe.wait_ge(c["w1_lo"], n - 1)
                else:
                    pe.wait_ge(prep["tables"], 4)
                for r in range(KC):
                    last = nc.tensor.transpose(ps_b[2 + k % 2][:, r * P:(r + 1) * P], kw_raw[w][:, r, k * P:(k + 1) * P], ident[:, :])
                last.then_inc(c["w1_t"], 1)

            def keys_t(cb, lay, i):
                pe.wait_ge(c[f"k_done{lay}"], NT * cb + i + 1)
                if i >= 2:
                    pe.wait_ge(c[f"k_staged{lay}"], NT * cb + i - 1)
                elif lay:
                    pe.wait_ge(c["k_staged0"], NT * (cb + 1))
                elif cb:
                    pe.wait_ge(c["k_staged1"], NT * cb)
                for g in range(GB):
                    last = nc.tensor.transpose(ps_b[i % 2][:, g * P:(g + 1) * P], k_t1[:, i % 2, g * D:(g + 1) * D], ident[:, :])
                last.then_inc(c["k_t"], 1)

            for cb in range(NB):
                for b in range(4):
                    lay, w = divmod(b, 2)
                    pe.wait_ge(c[f"w{lay}_hi"], 8 * cb + 4 * w + 4)
                    pe.wait_ge(c[f"w{lay}_lo"], 8 * cb + 4 * w + 4)
                    for i in range(NT):
                        if cb == 0 and b == 0:
                            pe.wait_ge(prep["ctx_lo"], i + 1)
                        n = NT * (4 * cb + b) + i - 2
                        if n >= 0:
                            last_cb, last_b, last_i = n // (4 * NT), n // NT % 4, n % NT
                            if last_b % 2:
                                pe.wait_ge(c["v_lo"], NT * (2 * last_cb + last_b // 2) + last_i + 1)
                            else:
                                pe.wait_ge(c[("k_read0", "k_done1")[last_b // 2]], NT * last_cb + last_i + 1)
                        for k in range(KC):
                            last = three(ps_q[i % 2][:, :], cT_hi[:, k, i * P:(i + 1) * P], cT_lo[:, k, i * P:(i + 1) * P],
                                         kw_hi[w][:, k, :], kw_lo[w][:, k, :], k == 0, k == KC - 1)
                        last.then_inc(c["tile"], 1)
                        if w == 0 and i >= 1:
                            keys_t(cb, lay, i - 1)
                        if w == 1 and i == 0:
                            keys_t(cb, lay, NT - 1)
                        if b in (1, 2) and 2 <= i < 2 + KC:
                            weights_t(cb, b + 1, i - 2)
                        if cb == 0 and b == 0 and i in (4, 7):
                            tables_pe(pe, i // 7)
                        if cb == 0 and b == 3 and i < NT // 2:
                            ln_turn(pe, lns[0], 2 * i)
                            ln_turn(pe, lns[0], 2 * i + 1)

        def kv_weights_hi(act, cb, b):
            w = b % 2
            act.wait_ge(kv[f"raw{w}"], 16 * (2 * cb + 1))
            if cb:
                act.wait_ge(kv["tile"], NT * (4 * cb - 1 + w))
            for k in range(KC):
                nc.scalar.activation(kw_hi[w][:, k, :], kw_raw[w][:, k, :], ACT.Copy).then_inc(kv["w0_hi"], 1)

        def kv_act(act):
            c = kv
            for cb in range(NB):

                def weights_hi(b, k):
                    w = b % 2
                    act.wait_ge(c["w1_t"], 8 * cb + 4 * w + k + 1)
                    nc.scalar.activation(kw_hi[w][:, k, :], ps_b[2 + k % 2][:, :], ACT.Copy).then_inc(c["w1_hi"], 1)

                def stage_keys(lay, i):
                    act.wait_ge(c["k_t"], NT * (2 * cb + lay) + i + 1)
                    if i == 0 and cb + lay:
                        act.wait_ge(c["k_spilled"], 16 * (2 * cb + lay))
                    nc.scalar.activation(kT_st[:, :, i * P:(i + 1) * P], ps_b[i % 2].rearrange("p (g t) -> p g t", g=GB),
                                         ACT.Copy).then_inc(c[f"k_staged{lay}"], 1)

                def values_hi(lay, i):
                    act.wait_ge(c["tile"], NT * (4 * cb + 2 * lay + 1) + i + 1)
                    if i == 0 and cb + lay:
                        act.wait_ge(c["v_spilled"], 16 * 2 * GB * (2 * cb + lay))
                    nc.scalar.activation(vs_hi[:, i, :], ps_q[i % 2][:, :], ACT.Copy).then_inc(c["v_hi"], 1)

                for i in range(NT - 1):
                    if i == 2:
                        kv_weights_hi(act, cb, 1)
                    stage_keys(0, i)
                    if cb == 0 and i == 3:
                        tables_act(act, 0)
                if cb == 0:
                    tables_act(act, 1)
                for i in range(NT):
                    values_hi(0, i)
                    if i == 0:
                        stage_keys(0, NT - 1)
                    if 2 <= i < 2 + KC:
                        weights_hi(2, i - 2)
                if cb == 0:
                    ln_sd(act, lns[0], 0)
                    ln_sd(act, lns[0], 1)
                for i in range(NT):
                    act.wait_ge(c["tile"], NT * (4 * cb + 2) + i + 1)
                    if cb or i:
                        act.wait_ge(c["k_ssq"], NT * cb + i)
                    nc.scalar.activation(k_sq[:, :], ps_q[i % 2][:, :], ACT.Square).then_inc(c["k_sq"], 1)
                    act.wait_ge(c["k_ssq"], NT * cb + i + 1)
                    nc.scalar.activation(k_ss[:, 1, :], k_ss[:, 0, :], ACT.Sqrt, bias=eps_ln[:, 0:1], scale=1.0 / D).then_inc(c["k_rms"], 1)
                    if i >= 1:
                        stage_keys(1, i - 1)
                    if 2 <= i < 2 + KC:
                        weights_hi(3, i - 2)
                for i in range(NT):
                    values_hi(1, i)
                    if i == 0:
                        stage_keys(1, NT - 1)
                    if cb == 0 and i < NT // 2:
                        ln_high(act, lns[0], 2 * i)
                        ln_high(act, lns[0], 2 * i + 1)
                    if i == 3 and cb + 1 < NB:
                        kv_weights_hi(act, cb + 1, 0)
                    if i == 2 and cb + 1 == NB:
                        act.wait_ge(c["tile"], NT * (4 * cb + 3))
                        for j in range(J):
                            att_wq_high(act, 0, 0, j)

        def kv_pool(pool):
            c = kv
            for cb in range(NB):

                def weights_lo(cb, w, k):
                    pool.wait_ge(c["w0_hi"], 8 * cb + 4 * w + k + 1)
                    nc.gpsimd.tensor_tensor(kw_lo[w][:, k, :], kw_raw[w][:, k, :], kw_hi[w][:, k, :].bitcast(F32),
                                            ALU.subtract).then_inc(c["w0_lo"], 1)

                for i in range(NT):
                    pool.wait_ge(c["k_read0"], NT * cb + i + 1)
                    nc.gpsimd.tensor_tensor(k_t1[:, i % 2, :], k_t1[:, i % 2, :], k_t2[:, i % 2, :], ALU.add).then_inc(c["k_done0"], 1)
                    if 2 <= i < 2 + KC:
                        weights_lo(cb, 1, i - 2)
                for k in range(KC):
                    if cb + 1 < NB:
                        weights_lo(cb + 1, 0, k)
                    else:
                        att_wq_low(pool, 0, 0, k)

        def kv_dve(dve):
            c = kv
            h = D // 2
            dve.wait_ge(prep["rope_k"], 16 * NT)
            for cb in range(NB):

                def weights_lo(b, k):
                    w = b % 2
                    dve.wait_ge(c["w1_hi"], 8 * cb + 4 * w + k + 1)
                    nc.vector.tensor_tensor(kw_lo[w][:, k, :], ps_b[2 + k % 2][:, :], kw_hi[w][:, k, :].bitcast(F32),
                                            ALU.subtract).then_inc(c["w1_lo"], 1)

                def values_lo(lay, i):
                    dve.wait_ge(c["v_hi"], NT * (2 * cb + lay) + i + 1)
                    nc.vector.tensor_tensor(vs_lo[:, i, :], ps_q[i % 2][:, :], vs_hi[:, i, :].bitcast(F32),
                                            ALU.subtract).then_inc(c["v_lo"], 1)

                for i in range(NT):
                    dve.wait_ge(c["tile"], NT * 4 * cb + i + 1)
                    if cb or i >= 2:
                        dve.wait_ge(c["k_t"], NT * 2 * cb + max(i - 1, 0))
                    key = ps_q[i % 2].rearrange("p (g u d) -> p g u d", g=GB, u=2)
                    t1 = k_t1[:, i % 2, :].rearrange("p (g u d) -> p g u d", g=GB, u=2)
                    t2 = k_t2[:, i % 2, :].rearrange("p (g u d) -> p g u d", g=GB, u=2)
                    cos = rope_k[:, i, 0:h].unsqueeze(1).to_broadcast([P, GB, h])
                    sin = rope_k[:, i, h:D].unsqueeze(1).to_broadcast([P, GB, h])
                    for u in range(2):
                        nc.vector.tensor_tensor(t1[:, :, u, :], key[:, :, u, :], cos, ALU.mult).then_inc(c["k_cos"], 1)
                    nc.vector.scalar_tensor_tensor(t2[:, :, 0, :], key[:, :, 1, :], -1.0, sin, ALU.mult, ALU.mult).then_inc(c["k_cos"], 1)
                    nc.vector.tensor_tensor(t2[:, :, 1, :], key[:, :, 0, :], sin, ALU.mult).then_inc(c["k_read0"], 1)
                for i in range(NT):
                    values_lo(0, i)
                    if 2 <= i < 2 + KC:
                        weights_lo(2, i - 2)
                    if cb == 0 and i in (3, 5):
                        ln_stats(dve, lns[0], i // 5, lambda i: (prep["x"], 16))
                for i in range(NT):
                    dve.wait_ge(c["k_sq"], NT * cb + i + 1)
                    nc.vector.tensor_reduce(k_ss[:, 0, :], k_sq[:, :].rearrange("p (g d) -> p g d", g=GB), AX, ALU.add).then_inc(c["k_ssq"], 1)
                    dve.wait_ge(c["k_rms"], NT * cb + i + 1)
                    nc.vector.reciprocal(k_ss[:, 2, :], k_ss[:, 1, :]).then_inc(c["k_rrms"], 1)
                    dve.wait_ge(c["k_rrms"], NT * cb + i + 1)
                    dve.wait_ge(c["k_t"], NT * (2 * cb + 1) + max(i - 1, 0))
                    nc.vector.tensor_tensor(k_t1[:, i % 2, :].rearrange("p (g d) -> p g d", g=GB), ps_q[i % 2].rearrange("p (g d) -> p g d", g=GB),
                                            wide(k_ss[:, 2, :], D), ALU.mult).then_inc(c["k_done1"], 1)
                    if 2 <= i < 2 + KC:
                        weights_lo(3, i - 2)
                    if cb == 0 and i in (2, 5):
                        ln_rs(dve, lns[0], i // 5)
                        if i == 5:
                            ln_norm(dve, lns[0], 0)
                            ln_norm(dve, lns[0], 1)
                for i in range(NT):
                    values_lo(1, i)
                    if cb == 0 and i < NT // 2:
                        ln_low(dve, lns[0], 2 * i)
                        ln_low(dve, lns[0], 2 * i + 1)
                        if i + 1 < NT // 2:
                            ln_norm(dve, lns[0], 2 * i + 2)
                            ln_norm(dve, lns[0], 2 * i + 3)

        def att_load_wq(sp, lay, g):
            if lay == 0:
                view = Wq0.rearrange("(k p) (g n) -> g p k n", p=P, g=G)[g]
            else:
                view = Wq1.rearrange("(g j p) e -> g p j e", p=P, g=G)[g]
            sp.dma_start(wq_raw[:, :, :], view).then_inc(att[lay]["wq_in"], 16)

        def att_wq_turn(pe, g, j):
            c = att[1]
            if j == 0:
                pe.wait_ge(*c("wq_in", 16 * (g + 1)))
            if j < 2 and isinstance(g, int) and g == 0:
                pe.wait_ge(moe["gu"], 2 * NT)
            elif j < 2:
                pe.wait_ge(*c("q_rot", 8 * g - 1 + j))
            if j >= 2:
                pe.wait_ge(*c("wq_lo", 4 * g + j - 1))
            for k in range(KC):
                last = nc.tensor.transpose(ps_q[j % 2][:, k * P:(k + 1) * P], wq_raw[:, j, k * P:(k + 1) * P], ident[:, :])
            last.then_inc(c["wq_t"], 1)

        def att_wq_high(act, lay, g, j):
            c = att[lay]
            if lay:
                act.wait_ge(*c("wq_t", 4 * g + j + 1))
                src = ps_q[j % 2].rearrange("p (k d) -> p k d", k=KC)
            else:
                act.wait_ge(*c("wq_in", 16 * (g + 1)))
                if not (isinstance(g, int) and g == 0):
                    act.wait_ge(*c("q_done", 8 * g - J + j + 1))
                src = wq_raw[:, :, j * D:(j + 1) * D]
            nc.scalar.activation(wq_hi[:, :, j * D:(j + 1) * D], src, ACT.Copy).then_inc(c["wq_hi"], 1)

        def att_wq_low(pool, lay, g, j):
            c = att[lay]
            pool.wait_ge(*c("wq_hi", 4 * g + j + 1))
            nc.gpsimd.tensor_tensor(wq_lo[:, :, j * D:(j + 1) * D], wq_raw[:, :, j * D:(j + 1) * D],
                                    wq_hi[:, :, j * D:(j + 1) * D].bitcast(F32), ALU.subtract).then_inc(c["wq_lo"], 1)

        def att_wq_low_turned(dve, g, j):
            c = att[1]
            dve.wait_ge(*c("wq_hi", 4 * g + j + 1))
            nc.vector.tensor_tensor(wq_lo[:, :, j * D:(j + 1) * D], ps_q[j % 2].rearrange("p (k d) -> p k d", k=KC),
                                    wq_hi[:, :, j * D:(j + 1) * D].bitcast(F32), ALU.subtract).then_inc(c["wq_lo"], 1)

        def att_wq_split(sp, lay, n):
            sp.wait_ge(*att[lay]("wq_hi", 4 * n))
            sp.wait_ge(*att[lay]("wq_lo", 4 * n))

        def first_scores(lay, g, h):
            return lay == 0 and isinstance(g, int) and (g, h) == (0, 1)

        def second_first_scores(lay, g, h):
            return lay == 1 and isinstance(g, int) and (g, h) == (0, 1)

        def last_step(lay, g, h):
            return lay == 1 and isinstance(g, int) and (g, h) == (G - 1, 1)

        def att_mask(eng, lay, u, h):
            c = att[lay]
            if lay == 0:
                if isinstance(u, int) and u == 0:
                    eng.wait_ge(*c("masks", 2))
                eng.wait_ge(*c("s_kept", u + 1))
                sc = s_sb.rearrange("p (t j n) -> p t j n", t=PAIRS, j=J)
                m = offset0[:, h, :, :, :].rearrange("p t a k -> p t (a k)").unsqueeze(2).to_broadcast([P, PAIRS, J, S])
            else:
                eng.wait_ge(*c("s_turned", u + 1))
                sc = s_sb.rearrange("p (n k) -> p n k", k=S)
                m = mask1_sb.rearrange("p a k -> p (a k)").unsqueeze(1).to_broadcast([P, PAIRS * J, S])
            eng.tensor_tensor(sc, sc, m, ALU.add).then_inc(c["s_masked"], 1)

        def att_shift(eng, lay, u):
            c = att[lay]
            eng.wait_ge(*c("s_max", u + 1))
            sc = s_sb.rearrange("p (n k) -> p n k", k=QB)
            eng.tensor_tensor(sc, sc, wide(mx_c[:, :], QB), ALU.subtract).then_inc(c["s_shifted"], 1)

        def att_normalise(eng, lay, u):
            c = att[lay]
            eng.wait_ge(*c("p_rec", u + 1))
            pr = p_sb.rearrange("p (n k) -> p n k", k=QB)
            eng.tensor_tensor(pr, pr, wide(p_rec[:, :], QB), ALU.mult).then_inc(c["p_normed"], 1)

        def att_probs_low(eng, lay, u):
            c = att[lay]
            eng.wait_ge(*c("p_hi", u + 1))
            eng.tensor_tensor(p_lo[:, :], pT[:, :], p_hi[:, :].bitcast(F32), ALU.subtract).then_inc(c["p_lo"], 1)

        def att_sync(sp, lay):
            c = att[lay]

            def load_wo(g):
                if lay == 0:
                    view = Wo0.rearrange("(g j p) e -> g p j e", p=P, g=G)[g]
                else:
                    view = Wo1.rearrange("(k p) (g n) -> g p k n", p=P, g=G)[g]
                sp.dma_start(wo_raw[:, :, :], view).then_inc(c["wo_in"], 16)

            def load_k(g, h):
                sp.dma_start(kT[:, h, :], kT_dram[lay, g, :, h * HALF:(h + 1) * HALF]).then_inc(c[f"k_in{h}"], 16)

            def load_v(g):
                sp.dma_start(v_hi[:, :, :].bitcast(F32), v_hi_dram[lay, g].rearrange("p (i d) -> p i d", d=D)).then_inc(c["v_in"], 16)
                sp.dma_start(v_lo[:, :, :].bitcast(F32), v_lo_dram[lay, g].rearrange("p (i d) -> p i d", d=D)).then_inc(c["v_in"], 16)

            def wo_split(n):
                sp.wait_ge(*c("wo_hi", 4 * n))
                sp.wait_ge(*c("wo_lo", 4 * n))

            if lay == 0:
                sp.wait_ge(kv["k_spilled"], 16 * 2 * NB)
                sp.wait_ge(kv["v_spilled"], 16 * 2 * GB * 2 * NB)
            else:
                sp.wait_ge(moe["u_done"], 2 * NT)
            load_k(0, 0)
            load_k(0, 1)
            if lay:
                for par in range(2):
                    for kb in range(2):
                        q0 = par * S + kb * QB
                        sp.dma_start(mask1_sb[q0:q0 + QB, :, :],
                                     mask1[0, 0, :, kb * QB:(kb + 1) * QB].rearrange("(a q) k -> q a k", q=QB)).then_inc(c["mask_in"], 16)
                sp.dma_start(qk_in[:, 0:1], q_norm.unsqueeze(1)).then_inc(c["qk_in"], 16)
                sp.dma_start(qk_in[:, 1:2], k_norm.unsqueeze(1)).then_inc(c["qk_in"], 16)
            load_wo(0)
            if lay:
                sp.wait_ge(moe["down"], NT)
            load_v(0)
            if lay == 0:
                moe_load_g(sp)
            else:
                lora_load(sp)
            if lay:
                att_wq_split(sp, lay, 1)
                att_load_wq(sp, lay, 1)
            sp.wait_ge(*c("scored", 1))
            load_k(1, 0)
            att_wq_split(sp, lay, 2)
            att_load_wq(sp, lay, 2)

            def steady(g, wq, k):
                wo_split(g)
                load_wo(g)
                sp.wait_ge(*c("scored", 2 * g))
                load_k(g, 1)
                if k:
                    sp.wait_ge(*c("scored", 2 * g + 1))
                    load_k(g + 1, 0)
                sp.wait_ge(*c("o_done", 8 * g))
                load_v(g)
                if wq:
                    att_wq_split(sp, lay, g + 2)
                    att_load_wq(sp, lay, g + 2)

            for g in range(1, G - 2):
                steady(g, True, True)
            steady(G - 2, False, True)
            steady(G - 1, False, False)

        LN_BESIDE = {0: (0, 1), 1: (2, 3), 2: (), 3: ()}

        def att_steps(eng, step):
            step(0, 0, True, False, False, False)
            step(0, 1, True, True, False, True)
            step(1, 0, True, True, True, False)
            step(1, 1, True, True, True, True)
            with eng.Fori(2, G - 1) as g:
                step(g, 0, True, True, True, False)
                step(g, 1, True, True, True, True)
            step(G - 1, 0, True, True, True, False)
            step(G - 1, 1, True, True, True, False)

        def att_pe(pe, lay, beside):
            c = att[lay]

            def project(g, h, j):
                n = 4 * (2 * g + h) + j
                if h == 0:
                    ready = 4 * g + ((3, 4, 4, 4)[j] if lay else j + 1)
                    pe.wait_ge(*c("wq_hi", ready))
                    pe.wait_ge(*c("wq_lo", ready))
                if not (isinstance(g, int) and n < 2):
                    pe.wait_ge(*c("q_rot" if lay else "q_read", n - 1))
                for k in range(KC):
                    last = three(ps_q[j % 2][:, :], wq_hi[:, k, j * D:(j + 1) * D], wq_lo[:, k, j * D:(j + 1) * D],
                                 hT_hi[:, k, h * HALF:(h + 1) * HALF], hT_lo[:, k, h * HALF:(h + 1) * HALF], k == 0, k == KC - 1)
                last.then_inc(c["q_done"], 1)

            def square_sums(u, h):
                pe.wait_ge(*c("q_sq", 4 * u + 4))
                if isinstance(u, int) and u == 0:
                    pe.wait_ge(*lns[2]("lo", NT))
                else:
                    pe.wait_ge(*c("s_scaled", u))
                for t in range(PAIRS):
                    for par in range(2):
                        b = (2 * t + par) * S
                        last = nc.tensor.matmul(ps_s[par * S:(par + 1) * S, t * JS:(t + 1) * JS], ones[:, :], q_sq[:, :, b:b + S],
                                                start=True, stop=True)
                last.then_inc(c["ssq"], 1)

            def score(u, h, g):
                pe.wait_ge(*c("q_rot", 4 * u + 4))
                pe.wait_ge(*c(f"k_in{h}", 16 * (g + 1)))
                if lay:
                    pe.wait_ge(*c("r_ln", u + 1))
                elif not (isinstance(u, int) and u == 0):
                    pe.wait_ge(*c("s_turned", u))
                for t in range(PAIRS):
                    for par in range(2):
                        b = (2 * t + par) * S
                        last = nc.tensor.matmul(ps_s[par * S:(par + 1) * S, t * JS:(t + 1) * JS], kT[:, h, b:b + S], qT[:, h, :, b:b + S],
                                                start=True, stop=True)
                last.then_inc(c["scored"], 1)

            def values(u, h, g):
                pe.wait_ge(*c("p_hi", u + 1))
                pe.wait_ge(*c("p_lo", u + 1))
                pe.wait_ge(*c("v_in", 32 * (g + 1)))
                if not (isinstance(u, int) and u == 0):
                    pe.wait_ge(*c("y_added", 4 * u))
                if lay and h == 0:
                    pe.wait_ge(*c("wo_hi", 4 * g + 4))
                    pe.wait_ge(*c("wo_lo", 4 * g + 4))
                for half in range(2):
                    for tt in range(2):
                        t = 2 * half + tt
                        cols = slice(t * JS, (t + 1) * JS)
                        for n, (v_part, p_part) in enumerate(((v_hi, p_hi), (v_hi, p_lo), (v_lo, p_hi))):
                            for par in range(2):
                                rows = slice(par * S, (par + 1) * S)
                                last = nc.tensor.matmul(ps_b[2 * half + par][:, tt * JS:(tt + 1) * JS], v_part[rows, h * PAIRS + t, :],
                                                        p_part[rows, cols], start=n == 0, stop=n == 2)
                                if tt == 1 and n == 2:
                                    last.then_inc(c["o_done"], 1)

            def project_out(u, h, g, t):
                if t % 2 == 0:
                    pe.wait_ge(*c("o_hi", 4 * u + t + 2))
                    pe.wait_ge(*c("o_lo", 4 * u + t + 2))
                if t == 0 and h == 0:
                    pe.wait_ge(*c("wo_hi", 4 * g + 4))
                    pe.wait_ge(*c("wo_lo", 4 * g + 4))
                for j in range(J):
                    last = three(ps_b[t][:, :], o_hi[:, t, j, :], o_lo[:, t, j, :], wo_hi[:, j, :], wo_lo[:, j, :], j == 0, j == J - 1)
                last.then_inc(c["y_done"], 1)

            def wo_turn(g):
                pe.wait_ge(*c("wo_in", 16 * (g + 1)))
                if not (isinstance(g, int) and g == 0):
                    pe.wait_ge(*c("y_added", 8 * g))
                for j in range(J):
                    for k in range(KC):
                        last = nc.tensor.transpose(ps_b[j][:, k * P:(k + 1) * P], wo_raw[:, k, j * D:(j + 1) * D], ident[:, :])
                    last.then_inc(c["wo_t"], 1)

            def step(g, h, do_project, do_score, do_finish, next_wq):
                us, up = 2 * g + h - 1, 2 * g + h - 2
                if do_score and lay and not (isinstance(g, int) and (g, h) == (1, 0)):
                    square_sums(us, 1 - h)
                at_first = lay and isinstance(g, int) and (g, h) == (0, 0)
                if do_project:
                    project(g, h, 0)
                if first_scores(lay, g, h):
                    project(g, h, 1)
                if do_score:
                    score(us, 1 - h, g if h else g - 1)
                if lay and do_finish and h == 0:
                    wo_turn(g - 1)
                if do_project:
                    if not first_scores(lay, g, h):
                        project(g, h, 1)
                    if at_first:
                        ln_turn(pe, lns[2], PAIRS)
                        ln_turn(pe, lns[2], PAIRS + 1)
                    project(g, h, 2)
                    if at_first:
                        ln_turn(pe, lns[2], PAIRS + 2)
                        ln_turn(pe, lns[2], PAIRS + 3)
                if do_finish:
                    values(up, h, g - 1)
                if do_project:
                    project(g, h, 3)
                for t in range(PAIRS):
                    if lay and next_wq:
                        att_wq_turn(pe, g + 1, t)
                    if second_first_scores(lay, g, h) and t == 1:
                        square_sums(us + 1, 1)
                    if do_finish:
                        project_out(up, h, g - 1, t)
                    if last_step(lay, g, h) and t == 0:
                        square_sums(us + 1, 1)

            if lay == 0:
                pe.wait_ge(*lns[0]("lo", NT))
                pe.wait_ge(kv["v_lo"], 2 * NT * NB)
            else:
                pe.wait_ge(*lns[2]("lo", PAIRS))
            att_steps(pe, step)
            last = 2 * G - 1
            score(last, 1, G - 1)
            if lay:
                wo_turn(G - 1)
            beside(0, -1)
            for h in range(2):
                values(last - 1 + h, h, G - 1)
                for t in range(PAIRS):
                    project_out(last - 1 + h, h, G - 1, t)
                    for i in LN_BESIDE[t] if h else ():
                        ln_turn(pe, lns[2 * lay + 1], i)
                    beside(h, t)

        def att_act(act, lay, beside):
            c = att[lay]

            def wo_high(g, j):
                if lay:
                    act.wait_ge(*c("wo_t", 4 * g + j + 1))
                    src = ps_b[j][:, :]
                else:
                    act.wait_ge(*c("wo_in", 16 * (g + 1)))
                    if not (isinstance(g, int) and g == 0):
                        act.wait_ge(*c("y_done", 8 * g))
                    src = wo_raw[:, j, :]
                nc.scalar.activation(wo_hi[:, j, :], src, ACT.Copy).then_inc(c["wo_hi"], 1)

            def queries(u, h, j):
                act.wait_ge(*c("q_done", 4 * u + j + 1))
                if j == 0 and not (isinstance(u, int) and u == 0):
                    act.wait_ge(*c("ssq", u))
                nc.scalar.activation(q_sq[:, j, :], ps_q[j % 2][:, :], ACT.Square).then_inc(c["q_sq"], 1)
                nc.scalar.activation(qT[:, h, j, :], ps_q[j % 2][:, :], ACT.Copy, scale=qk_w[:, 0:1]).then_inc(c["q_rot"], 1)

            def norms(u):
                act.wait_ge(*c("ssq", u + 1))
                if not (isinstance(u, int) and u == 0):
                    act.wait_ge(*c("s_scaled", u))
                nc.scalar.activation(r_q[:, :], ps_s[:, :], ACT.Ln, bias=eps_rms[:, 0:1]).then_inc(c["r_ln"], 1)
                act.wait_ge(*c("r_ln", u + 1))
                nc.scalar.activation(r_q[:, :], r_q[:, :], ACT.Exp, bias=zero_b[:, 0:1], scale=-0.5).then_inc(c["r_q"], 1)

            def exponentials(u):
                act.wait_ge(*c("s_shifted", u + 1))
                nc.scalar.activation(p_sb[:, :], s_sb[:, :], ACT.Exp, bias=zero_b[:, 0:1]).then_inc(c["p_exp"], 1)

            def probs_high(u):
                act.wait_ge(*c("p_turned", u + 1))
                if not (isinstance(u, int) and u == 0):
                    act.wait_ge(*c("o_done", 4 * u))
                nc.scalar.activation(p_hi[:, :], pT[:, :], ACT.Copy).then_inc(c["p_hi"], 1)

            def out_high(u, n):
                half, par = divmod(n, 2)
                act.wait_ge(*c("o_done", 4 * u + n + 1))
                nc.scalar.activation(o_hi[:, 2 * half:2 * half + 2, :, par * S:(par + 1) * S],
                                     ps_b[n].rearrange("p (t j q) -> p t j q", t=2, j=J), ACT.Copy).then_inc(c["o_hi"], 1)

            def step(g, h, do_project, do_score, do_finish, next_wq):
                uq, us, up = 2 * g + h, 2 * g + h - 1, 2 * g + h - 2
                if do_score and lay:
                    norms(us)
                if do_finish and h == 0 and lay == 0 and not (isinstance(g, int) and g == 1):
                    for j in range(J):
                        wo_high(g - 1, j)
                for j in range(J):
                    if first_scores(lay, g, h):
                        wo_high(0, j)
                    if j == 3 and do_finish:
                        for n in range(4):
                            out_high(up, n)
                    if second_first_scores(lay, g, h) and j == 3:
                        exponentials(us)
                    if do_project and lay:
                        queries(uq, h, j)
                        if isinstance(g, int) and (g, h) == (0, 0) and j in (1, 2):
                            ln_high(act, lns[2], PAIRS + 2 * j - 2)
                            ln_high(act, lns[2], PAIRS + 2 * j - 1)
                    if next_wq and lay == 0 and j < 3:
                        att_wq_high(act, lay, g + 1, j)
                    if j == 0 and do_finish and h == 0 and lay:
                        for jj in range(J):
                            wo_high(g - 1, jj)
                if next_wq and lay:
                    att_wq_high(act, lay, g + 1, 0)
                if do_score and not second_first_scores(lay, g, h):
                    exponentials(us)
                if last_step(lay, g, h):
                    norms(us + 1)
                if next_wq:
                    for j in (1, 2) if lay else (3,):
                        att_wq_high(act, lay, g + 1, j)
                if do_score:
                    probs_high(us)
                if next_wq and lay:
                    att_wq_high(act, lay, g + 1, 3)

            if lay:
                act.wait_ge(*c("qk_w", 1))
            att_steps(act, step)
            last = 2 * G - 1
            for j in range(J):
                wo_high(G - 1, j)
            beside(0, -1)
            for n in range(4):
                out_high(last - 1, n)
            exponentials(last)
            beside(0, 0)
            probs_high(last)
            beside(0, 1)
            beside(0, 2)
            beside(0, 3)
            for n in range(4):
                out_high(last, n)
            ln_sd(act, lns[2 * lay + 1], 0)
            for t in range(PAIRS):
                for i in LN_BESIDE[t]:
                    ln_high(act, lns[2 * lay + 1], i)
                beside(1, t)

        def att_pool(pool, lay):
            c = att[lay]

            def wo_low(g, j):
                pool.wait_ge(*c("wo_hi", 4 * g + j + 1))
                nc.gpsimd.tensor_tensor(wo_lo[:, j, :], wo_raw[:, j, :], wo_hi[:, j, :].bitcast(F32), ALU.subtract).then_inc(c["wo_lo"], 1)

            def rotate(u, h, j):
                pool.wait_ge(*c("q_read", 4 * u + j + 1))
                nc.gpsimd.tensor_tensor(qT[:, h, j, :], q_t1[:, j % 2, :], q_t2[:, j % 2, :], ALU.add).then_inc(c["q_rot"], 1)

            def step(g, h, do_project, do_score, do_finish, next_wq):
                uq, us = 2 * g + h, 2 * g + h - 1

                def added(j):
                    if do_project and lay == 0:
                        rotate(uq, h, j)

                def split(wo, wq):
                    if lay == 0:
                        for j in wo if do_finish and h == 0 and not (isinstance(g, int) and g == 1) else ():
                            wo_low(g - 1, j)
                        for j in wq if next_wq else ():
                            att_wq_low(pool, lay, g + 1, j)

                if first_scores(lay, g, h):
                    added(0)
                    added(1)
                    split((), (0,))
                    added(2)
                    split((), (1,))
                    added(3)
                    split((), (2, 3))
                    for j in range(J):
                        wo_low(0, j)
                    return
                if second_first_scores(lay, g, h):
                    return
                split((0, 1), ())
                added(0)
                split((2,), (0,))
                if do_score:
                    att_mask(pool, lay, us, 1 - h)
                added(1)
                added(2)
                split((3,), (1,))
                if do_score:
                    att_shift(pool, lay, us)
                added(3)
                split((), (2,))
                if do_score:
                    att_normalise(pool, lay, us)
                split((), (3,))
                if do_score:
                    att_probs_low(pool, lay, us)

            if lay:
                pool.wait_ge(*c("mask_in", 16 * 4))
            att_steps(pool, step)
            if lay == 0:
                step(G, 0, False, False, True, False)
                att_normalise(pool, lay, 2 * G - 1)
                att_probs_low(pool, lay, 2 * G - 1)
            else:
                att_mask(pool, lay, 2 * G - 1, 1)

        def att_dve(dve, lay, beside):
            c = att[lay]

            def wo_low(g, j):
                dve.wait_ge(*c("wo_hi", 4 * g + j + 1))
                nc.vector.tensor_tensor(wo_lo[:, j, :], ps_b[j][:, :], wo_hi[:, j, :].bitcast(F32), ALU.subtract).then_inc(c["wo_lo"], 1)

            def rotate(u, h, j):
                n = 4 * u + j
                dve.wait_ge(*c("q_done", n + 1))
                if not (isinstance(u, int) and n < 2):
                    dve.wait_ge(*c("q_rot", n - 1))
                tok = slice(h * HALF, (h + 1) * HALF)
                half = D // 2
                nc.vector.tensor_tensor(q_t1[:, j % 2, :], ps_q[j % 2][:, :], cos_q[:, tok], ALU.mult).then_inc(c["q_cos"], 1)
                nc.vector.tensor_tensor(q_t2[0:half, j % 2, :], ps_q[j % 2][half:D, :], sin_q[half:D, tok], ALU.mult).then_inc(c["q_cos"], 1)
                nc.vector.tensor_tensor(q_t2[half:D, j % 2, :], ps_q[j % 2][0:half, :], sin_q[0:half, tok], ALU.mult).then_inc(c["q_read"], 1)

            def masks():
                dve.wait_ge(*c("mask_in", 16 * 4 * 2 * 2))
                nc.vector.tensor_scalar(keep0[:, :], mask_i[:, :], 0.0, None, ALU.not_equal).then_inc(c["masks"], 1)
                nc.vector.tensor_scalar(offset0[:, :], mask_i[:, :], 0.0, MASKED, ALU.is_equal, ALU.mult).then_inc(c["masks"], 1)
                dve.wait_ge(*c("masks", 2))

            def scale_scores(u):
                dve.wait_ge(*c("scored", u + 1))
                dve.wait_ge(*c("r_q", u + 1))
                if isinstance(u, int) and u == 2 * G - 1:
                    dve.wait_ge(*c("p_turned", u))
                nc.vector.tensor_tensor(p_sb[:, :], ps_s[:, :], r_q[:, :], ALU.mult).then_inc(c["s_scaled"], 1)

            def turn_scores(u, h):
                src = ps_s[:, :]
                if lay == 0:
                    dve.wait_ge(*c("scored", u + 1))
                else:
                    if not (isinstance(u, int) and u == 2 * G - 1):
                        scale_scores(u)
                    dve.wait_ge(*c("s_scaled", u + 1))
                    src = p_sb[:, :]
                nc.vector.transpose(s_sb[:, :], src).then_inc(c["s_turned"], 1)
                if lay == 0:
                    dve.wait_ge(*c("s_turned", u + 1))
                    sc = s_sb.rearrange("p (t j n) -> p t j n", t=PAIRS, j=J)
                    m = keep0[:, h, :, :, :].rearrange("p t a k -> p t (a k)").unsqueeze(2).to_broadcast([P, PAIRS, J, S])
                    nc.vector.tensor_tensor(sc, sc, m, ALU.mult).then_inc(c["s_kept"], 1)

            def across(dst, src):
                for k in range(4):
                    last = nc.vector.tensor_copy(dst[k * QB:(k + 1) * QB, :], src[(k ^ 1) * QB:((k ^ 1) + 1) * QB, :])
                return last

            def maxima(u):
                dve.wait_ge(*c("s_masked", u + 1))
                nc.vector.tensor_reduce(mx_a[:, :], s_sb.rearrange("p (n k) -> p n k", k=QB), AX, ALU.max).then_inc(c["mx_part"], 1)
                dve.wait_ge(*c("mx_part", u + 1))
                across(mx_b, mx_a).then_inc(c["mx_other"], 1)
                dve.wait_ge(*c("mx_other", u + 1))
                nc.vector.tensor_tensor(mx_c[:, :], mx_a[:, :], mx_b[:, :], ALU.max).then_inc(c["s_max"], 1)

            def sums(u):
                dve.wait_ge(*c("p_exp", u + 1))
                nc.vector.tensor_reduce(sm_a[:, :], p_sb.rearrange("p (n k) -> p n k", k=QB), AX, ALU.add).then_inc(c["sm_part"], 1)
                dve.wait_ge(*c("sm_part", u + 1))
                across(sm_b, sm_a).then_inc(c["sm_other"], 1)
                dve.wait_ge(*c("sm_other", u + 1))
                nc.vector.tensor_tensor(sm_c[:, :], sm_a[:, :], sm_b[:, :], ALU.add).then_inc(c["sm_all"], 1)
                dve.wait_ge(*c("sm_all", u + 1))
                nc.vector.reciprocal(p_rec[:, :], sm_c[:, :]).then_inc(c["p_rec"], 1)

            def turn_probs(u):
                dve.wait_ge(*c("p_normed", u + 1))
                nc.vector.transpose(pT[:, :], p_sb[:, :]).then_inc(c["p_turned"], 1)

            def out_low(u, n):
                half, par = divmod(n, 2)
                dve.wait_ge(*c("o_hi", 4 * u + n + 1))
                part = (slice(None), slice(2 * half, 2 * half + 2), slice(None), slice(par * S, (par + 1) * S))
                nc.vector.tensor_tensor(o_lo[part], ps_b[n].rearrange("p (t j q) -> p t j q", t=2, j=J),
                                        o_hi[part].bitcast(F32), ALU.subtract).then_inc(c["o_lo"], 1)

            def add_output(u, h, t):
                n = 4 * u + t
                dve.wait_ge(*c("y_done", n + 1))
                if not (isinstance(u, int) and u == 0):
                    dve.wait_ge(*c("y_added", 4 * u))
                i = h * PAIRS + t
                nc.vector.scalar_tensor_tensor(x_sb[:, i, :], ps_b[t][:, :], gates[:, lay:lay + 1], x_sb[:, i, :],
                                               ALU.mult, ALU.add).then_inc(c["y_added"], 1)

            def step(g, h, do_project, do_score, do_finish, next_wq):
                uq, us, up = 2 * g + h, 2 * g + h - 1, 2 * g + h - 2

                def rotated(j):
                    if do_project and lay == 0:
                        rotate(uq, h, j)

                def end(t):
                    if next_wq and lay:
                        att_wq_low_turned(dve, g + 1, t)
                    if do_finish:
                        add_output(up, h, t)


                if first_scores(lay, g, h):
                    rotated(0)
                    rotated(1)
                    turn_scores(us, 1 - h)
                    att_mask(dve, lay, us, 1 - h)
                    rotated(2)
                    maxima(us)
                    rotated(3)
                    att_shift(dve, lay, us)
                    rotate(uq + 1, 0, 0)
                    sums(us)
                    att_normalise(dve, lay, us)
                    turn_probs(us)
                    att_probs_low(dve, lay, us)
                    return
                if second_first_scores(lay, g, h):
                    turn_scores(us, 1 - h)
                    dve.wait_ge(*c("mask_in", 16 * 4))
                    att_mask(dve, lay, us, 1 - h)
                    maxima(us)
                    att_shift(dve, lay, us)
                    sums(us)
                    end(0)
                    att_normalise(dve, lay, us)
                    end(1)
                    turn_probs(us)
                    end(2)
                    att_probs_low(dve, lay, us)
                    end(3)
                    return
                if not (isinstance(g, int) and (g, h) == (1, 0)):
                    rotated(0)
                if lay == 0 and isinstance(g, int) and (g, h) == (0, 0):
                    masks()
                if do_score:
                    turn_scores(us, 1 - h)
                if do_finish and lay and h == 0:
                    for j in range(J):
                        wo_low(g - 1, j)
                rotated(1)
                rotated(2)
                if do_finish:
                    out_low(up, 0)
                    out_low(up, 1)
                if do_score:
                    maxima(us)
                if do_finish:
                    out_low(up, 2)
                    out_low(up, 3)
                rotated(3)
                end(0)
                if do_score:
                    sums(us)
                end(1)
                end(2)
                if do_score:
                    turn_probs(us)
                end(3)

            if lay:
                dve.wait_ge(*c("qk_in", 32))
                nc.vector.tensor_tensor(qk_w[:, :], qk_in[:, 0:1], qk_in[:, 1:2], ALU.mult).then_inc(c["qk_w"], 1)
                ln_stat(dve, lns[2], NT - 1, lambda i: (moe["x_added"], i + 1))
                ln_rs(dve, lns[2], 1)
                ln_second(dve, lns[2], lambda i: None)
            att_steps(dve, step)
            last, ln = 2 * G - 1, lns[2 * lay + 1]
            added = lambda i: c("y_added", 2 * (G - 1) * PAIRS + i + 1)
            if lay == 0:
                beside(0, -2)
            else:
                scale_scores(last)
                for j in range(J):
                    wo_low(G - 1, j)
            turn_scores(last, 1)
            out_low(last - 1, 0)
            out_low(last - 1, 1)
            if lay == 0:
                att_mask(dve, lay, last, 1)
            maxima(last)
            out_low(last - 1, 2)
            out_low(last - 1, 3)
            att_shift(dve, lay, last)
            if lay:
                add_output(last - 1, 0, 0)
                sums(last)
                att_normalise(dve, lay, last)
                turn_probs(last)
                add_output(last - 1, 0, 1)
                add_output(last - 1, 0, 2)
                att_probs_low(dve, lay, last)
                add_output(last - 1, 0, 3)
                beside(0, -2)
                beside(0, -1)
                ln_stat(dve, ln, 0, added)
                ln_stat(dve, ln, 1, added)
            else:
                beside(0, -1)
                sums(last)
                beside(0, 0)
                add_output(last - 1, 0, 0)
                turn_probs(last)
                add_output(last - 1, 0, 1)
                beside(0, 1)
                ln_stat(dve, ln, 0, added)
                add_output(last - 1, 0, 2)
                beside(0, 2)
                add_output(last - 1, 0, 3)
                beside(0, 3)
                ln_stat(dve, ln, 1, added)
            out_low(last, 0)
            out_low(last, 1)
            ln_stat(dve, ln, 2, added)
            ln_stat(dve, ln, 3, added)
            out_low(last, 2)
            out_low(last, 3)
            ln_rs(dve, ln, 0)
            ln_norm(dve, ln, 0)
            ln_norm(dve, ln, 1)
            for t in range(PAIRS):
                add_output(last, 1, t)
                ln_stat(dve, ln, PAIRS + t, added)
                for i in LN_BESIDE[t]:
                    ln_low(dve, ln, i)
                    if i + 2 < PAIRS:
                        ln_norm(dve, ln, i + 2)
                beside(1, t)

        def moe_load_g(sp):
            sp.dma_start(g_raw[:, :, :], glu_w.rearrange("(n p) e -> p n e", p=P)).then_inc(moe["g_in"], 16)

        def moe_sync(sp):
            c = moe
            sp.wait_ge(*att[0]("q_done", J * 2 * G))
            sp.dma_start(r_raw[:, :], gate_w).then_inc(c["r_in"], 16)
            sp.dma_start(u_raw[:, :, :], up_w.rearrange("(n p) e -> p n e", p=P)).then_inc(c["u_in"], 16)
            sp.wait_ge(c["w_t"], 1 + 2 * FT)
            sp.dma_start(d_raw[:, :, :], down_w.rearrange("(k p) n -> p k n", p=P)).then_inc(c["d_in"], 16)
            sp.wait_ge(c["w_t"], len(turns))
            sp.wait_ge(c["logits"], 2)
            att_load_wq(sp, 1, 0)

        turns = [("r", 0)] + [(w, n) for w in "gud" for n in range(FT)]
        TURNS = {(0, -1): (0, 1), (0, 0): (2, 3), (0, 1): (4,), (0, 2): (5,), (0, 3): (6, 7),
                 (1, 0): (8,), (1, 1): (9, 10), (1, 2): (11, 12), (1, 3): (13, 14)}

        def turn_bank(m):
            return ps_b[2 + m % 2] if turns[m][0] == "d" else ps_q[m % 2]

        def turned(m):
            w, n = turns[m]
            bank = turn_bank(m)
            view = bank.rearrange("p (k i) -> p k i", k=KC)
            if w == "r":
                return rT_hi[:, :, 0:NX], rT_lo[:, :, 0:NX], view[:, :, 0:NX]
            if w == "d":
                return dT_hi[:, n, :], dT_lo[:, n, :], bank[:, :]
            hi, lo = {"g": (gT_hi, gT_lo), "u": (uT_hi, uT_lo)}[w]
            return hi[:, :, n * P:(n + 1) * P], lo[:, :, n * P:(n + 1) * P], view

        def turn_pe(pe, m):
            c = moe
            w, n = turns[m]
            if m == 0:
                pe.wait_ge(*att[0]("q_rot", J * 2 * G))
            if n == 0:
                pe.wait_ge(c[f"{w}_in"], 16)
            if m >= 2:
                pe.wait_ge(c["w_lo"], m - 1)
            bank = turn_bank(m)
            for k in range(KC):
                if w == "r":
                    last = nc.tensor.transpose(bank[:, k * P:k * P + NX], r_raw[:, k * P:(k + 1) * P], ident[0:NX, 0:NX])
                elif w == "d":
                    last = nc.tensor.transpose(bank[:, k * P:(k + 1) * P], d_raw[:, k, n * P:(n + 1) * P], ident[:, :])
                else:
                    raw = {"g": g_raw, "u": u_raw}[w]
                    last = nc.tensor.transpose(bank[:, k * P:(k + 1) * P], raw[:, n, k * P:(k + 1) * P], ident[:, :])
            last.then_inc(c["w_t"], 1)

        def turn_act(act, m):
            act.wait_ge(moe["w_t"], m + 1)
            hi, lo, src = turned(m)
            nc.scalar.activation(hi, src, ACT.Copy).then_inc(moe["w_hi"], 1)

        def turn_dve(dve, m):
            dve.wait_ge(moe["w_hi"], m + 1)
            hi, lo, src = turned(m)
            nc.vector.tensor_tensor(lo, src, hi.bitcast(F32), ALU.subtract).then_inc(moe["w_lo"], 1)

        def moe_beside_pe(h, t):
            for m in TURNS[h, t]:
                turn_pe(nc.tensor, m)

        def moe_beside_act(h, t):
            for m in TURNS[h, t]:
                turn_act(nc.scalar, m)

        def moe_beside_dve(h, t):
            if t == -2:
                nc.vector.wait_ge(*att[0]("q_done", J * 2 * G))
                nc.vector.memset(rT_hi[:, :, NX:P].bitcast(F32), 0.0).then_inc(moe["r_zero"], 1)
                nc.vector.memset(rT_lo[:, :, NX:P].bitcast(F32), 0.0).then_inc(moe["r_zero"], 1)
                return
            for m in TURNS[h, t]:
                turn_dve(nc.vector, m)

        def gated_values(i):
            return gu1 if isinstance(i, int) and i == 1 else gu

        def moe_pe(pe):
            c = moe

            def logits(h):
                pe.wait_ge(*lns[1]("lo", (h + 1) * PAIRS))
                for k in range(KC):
                    last = three(ps_b[2][:, :], rT_hi[:, k, :], rT_lo[:, k, :], hT_hi[:, k, h * HALF:(h + 1) * HALF],
                                 hT_lo[:, k, h * HALF:(h + 1) * HALF], k == 0, k == KC - 1)
                last.then_inc(c["logits"], 1)

            def logits_t():
                pe.wait_ge(c["lgT"], 2)
                for i in range(NT):
                    last = nc.tensor.transpose(ps_h[0][:, i * NX:(i + 1) * NX], x_lgT[:, i * P:(i + 1) * P], ident[0:NX, 0:NX])
                last.then_inc(c["lg_t"], 1)

            def up(i, r, half, between=None):
                if half == 0:
                    pe.wait_ge(c["f_hi"], i + 1)
                    pe.wait_ge(c["f_lo"], i + 1)
                if not (isinstance(i, int) and i == 0):
                    pe.wait_ge(c["gu"], 2 * i + half - 1)
                for bank, hi, lo, name in ((ps_q[half], gT_hi, gT_lo, "g_done"), (ps_b[half], uT_hi, uT_lo, "u_done")):
                    for k in range(KC):
                        last = three(bank[:, 0:FH], f_hi[:, r, k, :], f_lo[:, r, k, :], hi[:, k, half * FH:(half + 1) * FH],
                                     lo[:, k, half * FH:(half + 1) * FH], k == 0, k == KC - 1)
                    last.then_inc(c[name], 1)
                    if between and name == "g_done":
                        between()

            def hidden_t(i):
                pe.wait_ge(c["hid"], 2 * i + 2)
                if not (isinstance(i, int) and i == 0):
                    pe.wait_ge(c["hdT_lo"], 2 * i)
                for n in range(FT):
                    last = nc.tensor.transpose(ps_h[n // 4][:, (n % 4) * P:(n % 4 + 1) * P], hid[:, n * P:(n + 1) * P], ident[:, :])
                last.then_inc(c["hid_t"], 1)

            def down(i, r, between=None):
                pe.wait_ge(c["hdT_lo"], 2 * i + 2)
                if not (isinstance(i, int) and i < 2):
                    pe.wait_ge(c["x_added"], i - 1)
                for n in range(FT):
                    last = three(ps_b[2 + r][:, :], hdT_hi[:, n, :], hdT_lo[:, n, :], dT_hi[:, n, :], dT_lo[:, n, :], n == 0, n == FT - 1)
                    if between and n == FT // 2:
                        between()
                last.then_inc(c["down"], 1)

            def tile(i, r):
                up(i, r, 0)
                hidden_t(i - 1)
                up(i, r, 1)
                down(i - 1, 1 - r)

            pe.wait_ge(*att[0]("y_added", 2 * G * PAIRS - 1))
            pe.wait_ge(c["r_zero"], 2)
            pe.wait_ge(c["w_lo"], 1)
            logits(0)
            pe.wait_ge(*att[0]("y_added", 2 * G * PAIRS))
            pe.wait_ge(c["w_lo"], 1 + 2 * FT)
            up(0, 0, 0)
            ln_turn(pe, lns[1], PAIRS)
            ln_turn(pe, lns[1], PAIRS + 1)
            up(0, 0, 1)
            ln_turn(pe, lns[1], PAIRS + 2)
            ln_turn(pe, lns[1], PAIRS + 3)
            turn_pe(pe, 15)
            turn_pe(pe, 16)

            def turns_17_18():
                turn_pe(pe, 17)
                turn_pe(pe, 18)

            up(1, 1, 0, turns_17_18)
            turn_pe(pe, 19)
            pe.wait_ge(c["w_lo"], 19)
            logits(1)
            up(1, 1, 1, logits_t)
            turn_pe(pe, 20)
            turn_pe(pe, 21)
            up(2, 0, 0)
            hidden_t(0)

            def finish():
                pe.wait_ge(c["w_lo"], len(turns))
                down(0, 0)
                hidden_t(1)

            up(2, 0, 1, finish)
            down(1, 1)
            with pe.Fori(1, NT // 2 - 1) as m:
                tile(2 * m + 1, 1)
                tile(2 * m + 2, 0)
            up(NT - 1, 1, 0)
            hidden_t(NT - 2)

            def first_turns():
                pe.wait_ge(c["hdT_lo"], 2 * (NT - 1))
                ln_turn(pe, lns[2], 0)
                ln_turn(pe, lns[2], 1)

            def last_hidden_t():
                pe.wait_ge(*lns[2]("lo", PAIRS))
                hidden_t(NT - 1)

            def wq_turns():
                att_wq_turn(pe, 0, 2)
                att_wq_turn(pe, 0, 3)

            up(NT - 1, 1, 1, first_turns)
            ln_turn(pe, lns[2], 2)
            ln_turn(pe, lns[2], 3)
            down(NT - 2, 0, last_hidden_t)
            att_wq_turn(pe, 0, 0)
            att_wq_turn(pe, 0, 1)
            down(NT - 1, 1, wq_turns)

        def moe_act(act):
            c = moe

            def logits(h):
                act.wait_ge(c["logits"], h + 1)
                nc.scalar.activation(x_lgT[:, h * HALF:(h + 1) * HALF], ps_b[2][0:NX, :], ACT.Copy).then_inc(c["lgT"], 1)

            def silu(i, half):
                act.wait_ge(c["g_done"], 2 * i + half + 1)
                if not (isinstance(i, int) and i == 0):
                    act.wait_ge(c["gu"], 2 * i + half - 1)
                nc.scalar.activation(sg[:, half, :], ps_q[half][:, 0:FH], ACT.Silu, bias=zero_b[:, 0:1]).then_inc(c["silu"], 1)

            def tokens(i, r):
                if not (isinstance(i, int) and i < 2):
                    act.wait_ge(c["u_done"], 2 * i - 2)
                nc.scalar.activation(f_hi[:, r, :, :], hT_hi[:, :, bass.ts(i, P)].bitcast(F32), ACT.Copy).then_inc(c["f_hi"], 1)

            def hidden_hi(i):
                for b, (n0, n1) in enumerate(((0, 4), (4, FT))):
                    act.wait_ge(c["hid_t"], i + 1)
                    if not (isinstance(i, int) and i == 0):
                        act.wait_ge(c["down"], i)
                    nc.scalar.activation(hdT_hi[:, n0:n1, :], ps_h[b][:, 0:(n1 - n0) * P].rearrange("p (n t) -> p n t", t=P),
                                         ACT.Copy).then_inc(c["hdT_hi"], 1)

            def tile(i, r):
                tokens(i + 1, 1 - r)
                silu(i, 0)
                hidden_hi(i - 1)
                silu(i, 1)

            tokens(0, 0)
            ln_sd(act, lns[1], 1)
            logits(0)
            tokens(1, 1)
            silu(0, 0)
            ln_high(act, lns[1], PAIRS)
            ln_high(act, lns[1], PAIRS + 1)
            silu(0, 1)
            ln_high(act, lns[1], PAIRS + 2)
            ln_high(act, lns[1], PAIRS + 3)
            for m in (15, 16):
                turn_act(act, m)
            tokens(2, 0)
            silu(1, 0)
            for m in (17, 18, 19):
                turn_act(act, m)
            logits(1)
            silu(1, 1)
            act.wait_ge(c["x_lg"], 1)
            nc.scalar.activation(x_ex[:, :, :], x_lg[:, :, :], ACT.Exp, bias=zero_b[:, 0:1]).then_inc(c["x_ex"], 1)
            for m in (20, 21):
                turn_act(act, m)
            tokens(3, 1)
            silu(2, 0)
            hidden_hi(0)
            silu(2, 1)
            hidden_hi(1)
            with act.Fori(1, NT // 2 - 1) as m:
                tile(2 * m + 1, 1)
                tile(2 * m + 2, 0)
            silu(NT - 1, 0)
            ln_sd(act, lns[2], 0)
            hidden_hi(NT - 2)
            silu(NT - 1, 1)
            for i in range(PAIRS):
                ln_high(act, lns[2], i)
            hidden_hi(NT - 1)
            for j in range(2):
                att_wq_high(act, 1, 0, j)
            for j in range(2, J):
                att_wq_high(act, 1, 0, j)
            ln_sd(act, lns[2], 1)

        def moe_pool(pool):
            c = moe
            pool.wait_ge(*att[0]("y_added", 2 * G * PAIRS))
            nc.gpsimd.memset(x_top[:, :, :], -1.0).then_inc(c["top_clear"], 1)

            def tokens(i, r):
                if not (isinstance(i, int) and i < 2):
                    pool.wait_ge(c["u_done"], 2 * i - 2)
                nc.gpsimd.tensor_copy(f_lo[:, r, :, :], hT_lo[:, :, bass.ts(i, P)].bitcast(F32)).then_inc(c["f_lo"], 1)

            def weigh(i, half):
                pool.wait_ge(c["gu"], 2 * i + half + 1)
                if not (isinstance(i, int) and i == 0):
                    pool.wait_ge(c["hid_t"], i)
                w = x_w[:, bass.ds(i, 1), half * XH:(half + 1) * XH].rearrange("p o e -> p (o e)")
                nc.gpsimd.tensor_tensor(hid[:, half * FH:(half + 1) * FH].rearrange("p (e n) -> p e n", e=XH),
                                        gated_values(i)[:, half, :].rearrange("p (e n) -> p e n", e=XH), wide(w, INTER), ALU.mult).then_inc(c["hid"], 1)

            def tile(i, r, after):
                if after:
                    tokens(i + 1, 1 - r)
                weigh(i, 0)
                weigh(i, 1)

            pool.wait_ge(c["w_t"], 1 + FT)
            pool.wait_ge(*lns[1]("lo", PAIRS))
            tokens(0, 0)
            tokens(1, 1)
            tokens(2, 0)
            pool.wait_ge(c["x_w"], 1)
            tile(0, 0, False)
            tile(1, 1, False)
            tile(2, 0, True)
            with pool.Fori(1, NT // 2 - 1) as m:
                tile(2 * m + 1, 1, True)
                tile(2 * m + 2, 0, True)
            tile(NT - 1, 1, False)

        def moe_dve(dve):
            c = moe

            def gated(i, half):
                dve.wait_ge(c["silu"], 2 * i + half + 1)
                dve.wait_ge(c["u_done"], 2 * i + half + 1)
                if not (isinstance(i, int) and i < 2):
                    before = 0 if isinstance(i, int) and i == 2 else i - 1
                    dve.wait_ge(c["hid"], 2 * before + half + 1)
                nc.vector.tensor_tensor(gated_values(i)[:, half, :], ps_b[half][:, 0:FH], sg[:, half, :], ALU.mult).then_inc(c["gu"], 1)

            def hidden_lo(i):
                for b, (n0, n1) in enumerate(((0, 4), (4, FT))):
                    dve.wait_ge(c["hdT_hi"], 2 * i + b + 1)
                    nc.vector.tensor_tensor(hdT_lo[:, n0:n1, :], ps_h[b][:, 0:(n1 - n0) * P].rearrange("p (n t) -> p n t", t=P),
                                            hdT_hi[:, n0:n1, :].bitcast(F32), ALU.subtract).then_inc(c["hdT_lo"], 1)

            def add_output(i, r):
                dve.wait_ge(c["down"], i + 1)
                xi = x_sb[:, bass.ds(i, 1), :].rearrange("p o e -> p (o e)")
                nc.vector.scalar_tensor_tensor(xi, ps_b[2 + r][:, :], gates[:, 2:3], xi, ALU.mult, ALU.add).then_inc(c["x_added"], 1)

            def tile(i, r):
                gated(i, 0)
                hidden_lo(i - 1)
                gated(i, 1)
                add_output(i - 1, 1 - r)

            ln_rs(dve, lns[1], 1)
            ln_norm(dve, lns[1], PAIRS)
            ln_norm(dve, lns[1], PAIRS + 1)
            gated(0, 0)
            ln_low(dve, lns[1], PAIRS)
            ln_norm(dve, lns[1], PAIRS + 2)
            ln_low(dve, lns[1], PAIRS + 1)
            ln_norm(dve, lns[1], PAIRS + 3)
            gated(0, 1)
            ln_low(dve, lns[1], PAIRS + 2)
            ln_low(dve, lns[1], PAIRS + 3)
            for m in (15, 16, 17, 18):
                turn_dve(dve, m)
            gated(1, 0)
            turn_dve(dve, 19)
            lg = ps_h[0][:, 0:NT * NX].rearrange("p (i e) -> p i e", e=NX)
            dve.wait_ge(c["lg_t"], 1)
            nc.vector.tensor_reduce(x_mx[:, :], lg, AX, ALU.max).then_inc(c["route"], 1)
            dve.wait_ge(c["route"], 1)
            nc.vector.tensor_tensor(x_lg[:, :, :], lg, wide(x_mx[:, :], NX), ALU.subtract).then_inc(c["x_lg"], 1)
            dve.wait_ge(c["x_ex"], 1)
            nc.vector.tensor_reduce(x_sum[:, :], x_ex[:, :, :], AX, ALU.add).then_inc(c["route"], 1)
            dve.wait_ge(c["route"], 2)
            nc.vector.reciprocal(x_rec[:, :], x_sum[:, :]).then_inc(c["route"], 1)
            dve.wait_ge(c["route"], 3)
            nc.vector.tensor_tensor(x_p[:, :, :], x_ex[:, :, :], wide(x_rec[:, :], NX), ALU.mult).then_inc(c["route"], 1)
            dve.wait_ge(c["route"], 4)
            for i in range(NT):
                nc.vector.max(x_rep[:, i, 0:8], x_p[:, i, :]).then_inc(c["route"], 1)
            dve.wait_ge(c["route"], 4 + NT)
            dve.wait_ge(c["top_clear"], 1)
            nc.vector.tensor_copy(x_top[:, :, 0:2], x_rep[:, :, 0:2]).then_inc(c["route"], 1)
            nc.vector.tensor_tensor(x_two[:, :], x_rep[:, :, 0], x_rep[:, :, 1], ALU.add).then_inc(c["route"], 1)
            dve.wait_ge(c["route"], 6 + NT)
            nc.vector.reciprocal(x_rec[:, :], x_two[:, :]).then_inc(c["route"], 1)
            for i in range(NT):
                nc.vector.match_replace(x_rep[:, i, :], x_top[:, i, :], x_p[:, i, :], -1.0).then_inc(c["route"], 1)
            dve.wait_ge(c["route"], 7 + 2 * NT)
            nc.vector.tensor_scalar(x_rep[:, :, :], x_rep[:, :, :], 0.0, None, ALU.max).then_inc(c["route"], 1)
            dve.wait_ge(c["route"], 8 + 2 * NT)
            nc.vector.tensor_tensor(x_p[:, :, :], x_p[:, :, :], x_rep[:, :, :], ALU.subtract).then_inc(c["route"], 1)
            dve.wait_ge(c["route"], 9 + 2 * NT)
            nc.vector.tensor_tensor(x_w[:, :, :], x_p[:, :, :], wide(x_rec[:, :], NX), ALU.mult).then_inc(c["x_w"], 1)

            gated(1, 1)
            for m in (20, 21):
                turn_dve(dve, m)
            gated(2, 0)
            hidden_lo(0)
            add_output(0, 0)
            hidden_lo(1)
            gated(2, 1)
            add_output(1, 1)
            with dve.Fori(1, NT // 2 - 1) as m:
                tile(2 * m + 1, 1)
                tile(2 * m + 2, 0)
            ln_stats(dve, lns[2], 0, lambda i: (c["x_added"], i + 1))
            gated(NT - 1, 0)
            hidden_lo(NT - 2)
            ln_rs(dve, lns[2], 0)
            ln_norm(dve, lns[2], 0)
            ln_norm(dve, lns[2], 1)
            ln_low(dve, lns[2], 0)
            ln_norm(dve, lns[2], 2)
            ln_low(dve, lns[2], 1)
            ln_norm(dve, lns[2], 3)
            gated(NT - 1, 1)
            ln_low(dve, lns[2], 2)
            ln_low(dve, lns[2], 3)
            hidden_lo(NT - 1)
            for j in range(2):
                att_wq_low_turned(dve, 0, j)
            add_output(NT - 2, 0)
            for j in range(2, J):
                att_wq_low_turned(dve, 0, j)
            for i in range(PAIRS, NT - 1):
                ln_stat(dve, lns[2], i, lambda n: (c["x_added"], n + 1))
            add_output(NT - 1, 1)

        def lora_load(sp):
            c = lora
            sp.dma_start(a_raw[0:LM, :], lora_a.rearrange("e r f -> (e r) f")).then_inc(c["a_in"], 16)
            sp.dma_start(a_raw[LM:LM + LX, :], lora_r).then_inc(c["a_in"], 16)
            for e in range(LX):
                sp.dma_start(b_raw[:, :, e, :], lora_b[e].rearrange("(n p) r -> p n r", p=P)).then_inc(c["b_in"], 16)

        def lora_sync(sp):
            c = lora
            for i in range(NT):
                sp.wait_ge(c["x_added"], i + 1)
                sp.dma_start(ot[:, i, :], x_sb[:, i, :]).then_inc(c["out"], 16)
            sp.wait_ge(c["out"], 16 * NT)

        LN = LM + LX
        delta_banks = [ps_b[2], ps_b[3]] + ps_h

        def lora_mid(pe, h):
            pe.wait_ge(*lns[3]("lo", (h + 1) * PAIRS))
            for k in range(KC):
                last = three(ps_q[h][:, :], aT_hi[:, k, :], aT_lo[:, k, :], hT_hi[:, k, h * HALF:(h + 1) * HALF],
                             hT_lo[:, k, h * HALF:(h + 1) * HALF], k == 0, k == KC - 1)
            last.then_inc(lora["mid"], 1)

        def lora_mid_t(pe, h):
            pe.wait_ge(lora["m_T"], h + 1)
            for t in range(PAIRS):
                i = h * PAIRS + t
                last = nc.tensor.transpose(ps_b[h][:, t * P:t * P + LN], m_T[:, i * P:(i + 1) * P], ident[0:LN, 0:LN])
            last.then_inc(lora["mid_t"], 1)

        def lora_beside_pe(h, t):
            if (h, t) == (1, 2):
                nc.tensor.wait_ge(lora["w_lo"], 2)
                nc.tensor.wait_ge(lora["a_zero"], 2)
                lora_mid(nc.tensor, 0)
            if (h, t) == (1, 3):
                for i in range(PAIRS, NT - 2):
                    ln_turn(nc.tensor, lns[3], i)
                nc.tensor.wait_ge(*att[1]("y_added", 2 * G * PAIRS - 3))
                lora_mid_t(nc.tensor, 0)
            if (h, t) == (0, -1):
                nc.tensor.wait_ge(*att[1]("q_rot", J * 2 * G))
                nc.tensor.wait_ge(lora["a_in"], 32)
                for k in range(KC):
                    last = nc.tensor.transpose(ps_q[0][:, k * P:k * P + LN], a_raw[:, k * P:(k + 1) * P], ident[0:LN, 0:LN])
                last.then_inc(lora["w_t"], 1)
                nc.tensor.wait_ge(lora["b_in"], 16 * LX)
                for k in range(LO // P):
                    last = nc.tensor.transpose(ps_q[1][0:LM, k * P:(k + 1) * P], b_raw[:, k, :, :].rearrange("p e r -> p (e r)"), ident[:, :])
                last.then_inc(lora["w_t"], 1)

        def lora_mid_act(act, h):
            act.wait_ge(lora["mid"], h + 1)
            nc.scalar.activation(m_T[:, h * HALF:(h + 1) * HALF], ps_q[h][0:LN, :], ACT.Copy).then_inc(lora["m_T"], 1)

        def lora_beside_act(h, t):
            if (h, t) == (1, 2):
                ln_sd(nc.scalar, lns[3], 1, PARTS)
                lora_mid_act(nc.scalar, 0)
            if (h, t) == (0, -1):
                nc.scalar.wait_ge(lora["w_t"], 1)
                nc.scalar.activation(aT_hi[:, :, 0:LN], ps_q[0].rearrange("p (k i) -> p k i", k=KC)[:, :, 0:LN], ACT.Copy).then_inc(lora["w_hi"], 1)
                nc.scalar.wait_ge(lora["w_t"], 2)
                nc.scalar.activation(bT_hi[:, :], ps_q[1][0:LM, :], ACT.Copy, scale=LORA_SCALE).then_inc(lora["w_hi"], 1)

        def lora_beside_dve(h, t):
            if t == -2:
                nc.vector.memset(aT_hi[:, :, LN:P].bitcast(F32), 0.0).then_inc(lora["a_zero"], 1)
                nc.vector.memset(aT_lo[:, :, LN:P].bitcast(F32), 0.0).then_inc(lora["a_zero"], 1)
                nc.vector.wait_ge(*att[1]("q_done", J * 2 * G))
                nc.vector.memset(l_lg[:, :, :], -BIG).then_inc(lora["l_clear"], 1)
                nc.vector.memset(l_top[:, :, :], NO_MATCH).then_inc(lora["l_clear"], 1)
            if (h, t) == (1, 2):
                ln_rs(nc.vector, lns[3], 1, PARTS)
                ln_norm(nc.vector, lns[3], PAIRS)
                ln_norm(nc.vector, lns[3], PAIRS + 1)
            if (h, t) == (0, -1):
                nc.vector.wait_ge(lora["w_hi"], 1)
                nc.vector.tensor_tensor(aT_lo[:, :, 0:LN], ps_q[0].rearrange("p (k i) -> p k i", k=KC)[:, :, 0:LN],
                                        aT_hi[:, :, 0:LN].bitcast(F32), ALU.subtract).then_inc(lora["w_lo"], 1)
                nc.vector.wait_ge(lora["w_hi"], 2)
                nc.vector.scalar_tensor_tensor(bT_lo[:, :], ps_q[1][0:LM, :], LORA_SCALE, bT_hi[:, :].bitcast(F32), ALU.mult,
                                               ALU.subtract).then_inc(lora["w_lo"], 1)

        def lora_pe(pe):
            c = lora

            def gated_t(h):
                pe.wait_ge(c["gated"], h + 1)
                for t in range(PAIRS):
                    last = nc.tensor.transpose(ps_q[h][0:LM, t * P:(t + 1) * P], l_m[:, h * PAIRS + t, :, :].rearrange("p e r -> p (e r)"),
                                               ident[:, :])
                last.then_inc(c["gated_t"], 1)

            def delta(i):
                if i % PAIRS == 0:
                    pe.wait_ge(c["mT_lo"], i // PAIRS + 1)
                if i >= 4:
                    pe.wait_ge(c["x_added"], i - 3)
                three(delta_banks[i % 4][:, :], mT_hi[:, i * P:(i + 1) * P], mT_lo[:, i * P:(i + 1) * P], bT_hi[:, :], bT_lo[:, :],
                      True, True).then_inc(c["delta"], 1)

            ln_turn(pe, lns[3], NT - 2)
            ln_turn(pe, lns[3], NT - 1)
            lora_mid(pe, 1)
            gated_t(0)
            pe.wait_ge(*att[1]("y_added", 2 * G * PAIRS))
            lora_mid_t(pe, 1)
            for t in range(PAIRS):
                delta(t)
            gated_t(1)
            for t in range(PAIRS):
                delta(PAIRS + t)

        def lora_act(act):
            c = lora

            def exponentials(h):
                act.wait_ge(c["l_lg"], 2 * h + 2)
                own = slice(h * PAIRS, (h + 1) * PAIRS)
                nc.scalar.activation(l_ex[:, own, :], l_lg[:, own, 0:LX], ACT.Exp, bias=zero_b[:, 0:1]).then_inc(c["l_ex"], 1)

            def mid_high(h):
                act.wait_ge(c["gated_t"], h + 1)
                nc.scalar.activation(mT_hi[:, h * HALF:(h + 1) * HALF], ps_q[h][0:LM, :], ACT.Copy).then_inc(c["mT_hi"], 1)

            ln_high(act, lns[3], PAIRS)
            ln_sd(act, lns[3], 2, PARTS)
            for i in range(PAIRS + 1, NT):
                ln_high(act, lns[3], i)
            exponentials(0)
            lora_mid_act(act, 1)
            mid_high(0)
            exponentials(1)
            mid_high(1)

        def lora_dve(dve):
            c = lora
            steps = 7 + 2 * PAIRS

            def route(h):
                own = slice(h * PAIRS, (h + 1) * PAIRS)
                tiles = range(h * PAIRS, (h + 1) * PAIRS)
                mid = ps_b[h].rearrange("p (i m) -> p i m", m=P)
                done = steps * h
                dve.wait_ge(c["l_clear"], 2)
                dve.wait_ge(c["mid_t"], h + 1)
                nc.vector.tensor_copy(l_lg[:, own, 0:LX], mid[:, :, LM:LN]).then_inc(c["route"], 1)
                dve.wait_ge(c["route"], done + 1)
                for i in tiles:
                    nc.vector.max(l_rep[:, i, :], l_lg[:, i, :]).then_inc(c["route"], 1)
                dve.wait_ge(c["route"], done + 1 + PAIRS)
                nc.vector.tensor_copy(l_top[:, own, 0:2], l_rep[:, own, 0:2]).then_inc(c["route"], 1)
                nc.vector.tensor_copy(l_mx[:, own], l_rep[:, own, 0]).then_inc(c["route"], 1)
                dve.wait_ge(c["route"], done + 3 + PAIRS)
                for i in tiles:
                    nc.vector.match_replace(l_rep[:, i, :], l_top[:, i, :], l_lg[:, i, :], TAKEN).then_inc(c["route"], 1)
                dve.wait_ge(c["route"], done + 3 + 2 * PAIRS)
                nc.vector.tensor_scalar(l_rep[:, own, :], l_rep[:, own, :], TAKEN, -BIG, ALU.is_lt, ALU.mult).then_inc(c["route"], 1)
                nc.vector.tensor_tensor(l_lg[:, own, 0:LX], l_lg[:, own, 0:LX], wide(l_mx[:, own], LX), ALU.subtract).then_inc(c["l_lg"], 1)
                dve.wait_ge(c["route"], done + 4 + 2 * PAIRS)
                dve.wait_ge(c["l_lg"], 2 * h + 1)
                nc.vector.tensor_tensor(l_lg[:, own, 0:LX], l_lg[:, own, 0:LX], l_rep[:, own, 0:LX], ALU.add).then_inc(c["l_lg"], 1)

            def gate(h):
                own = slice(h * PAIRS, (h + 1) * PAIRS)
                mid = ps_b[h].rearrange("p (i m) -> p i m", m=P)
                done = steps * h + 4 + 2 * PAIRS
                dve.wait_ge(c["l_ex"], h + 1)
                nc.vector.tensor_reduce(l_sum[:, own], l_ex[:, own, :], AX, ALU.add).then_inc(c["route"], 1)
                dve.wait_ge(c["route"], done + 1)
                nc.vector.reciprocal(l_rec[:, own], l_sum[:, own]).then_inc(c["route"], 1)
                dve.wait_ge(c["route"], done + 2)
                nc.vector.tensor_tensor(l_ex[:, own, :], l_ex[:, own, :], wide(l_rec[:, own], LX), ALU.mult).then_inc(c["route"], 1)
                dve.wait_ge(c["route"], done + 3)
                for e in range(LX):
                    last = nc.vector.tensor_tensor(l_m[:, own, e, :], mid[:, :, e * LR:(e + 1) * LR], wide(l_ex[:, own, e], LR), ALU.mult)
                    last.then_inc(c["gated" if e == LX - 1 else "gating"], 1)

            def mid_low(h):
                dve.wait_ge(c["mT_hi"], h + 1)
                nc.vector.tensor_tensor(mT_lo[:, h * HALF:(h + 1) * HALF], ps_q[h][0:LM, :], mT_hi[:, h * HALF:(h + 1) * HALF].bitcast(F32),
                                        ALU.subtract).then_inc(c["mT_lo"], 1)

            def add_output(i):
                dve.wait_ge(c["delta"], i + 1)
                nc.vector.scalar_tensor_tensor(x_sb[:, i, :], delta_banks[i % 4][:, :], gates[:, 3:4], x_sb[:, i, :],
                                               ALU.mult, ALU.add).then_inc(c["x_added"], 1)

            ln_norm(dve, lns[3], NT - 2)
            ln_rs(dve, lns[3], 2, PARTS)
            dve.wait_ge(*lns[3]("rs", 3))
            ln_norm(dve, lns[3], NT - 1)
            for i in range(PAIRS, NT):
                ln_low(dve, lns[3], i)
            route(0)
            gate(0)
            mid_low(0)
            route(1)
            add_output(0)
            gate(1)
            add_output(1)
            add_output(2)
            mid_low(1)
            for i in range(3, NT):
                add_output(i)

        @block.sync
        def _(sp):
            prep_sync(sp)
            kv_sync(sp)
            att_sync(sp, 0)
            moe_sync(sp)
            att_sync(sp, 1)
            lora_sync(sp)

        @block.gpsimd
        def _(pool):
            prep_pool(pool)
            kv_pool(pool)
            att_pool(pool, 0)
            moe_pool(pool)
            att_pool(pool, 1)

        @block.scalar
        def _(act):
            act.wait_ge(prep["consts"], 4)
            prep_act(act)
            kv_act(act)
            act.wait_ge(prep["gates_in"], 32)
            nc.scalar.activation(gates[:, :], gates_in[:, :], ACT.Tanh, bias=zero_b[:, 0:1]).then_inc(prep["gates"], 1)
            att_act(act, 0, moe_beside_act)
            moe_act(act)
            att_act(act, 1, lora_beside_act)
            lora_act(act)

        @block.tensor
        def _(pe):
            prep_pe(pe)
            kv_pe(pe)
            att_pe(pe, 0, moe_beside_pe)
            moe_pe(pe)
            att_pe(pe, 1, lora_beside_pe)
            lora_pe(pe)

        @block.vector
        def _(dve):
            prep_dve(dve)
            kv_dve(dve)
            att_dve(dve, 0, moe_beside_dve)
            moe_dve(dve)
            att_dve(dve, 1, lora_beside_dve)
            lora_dve(dve)


_INS = ["x", "ctx_4096", "pos_BxS2", "mask_BxSxS2_ik0", "mask_1x1xSxS2_ff0", "g_xattn", "g_ffn", "L0_xattn_Wq", "L0_xattn_Wk",
        "L0_xattn_Wv", "L0_xattn_Wo", "L0_ffn_gate_w", "L0_ffn_u", "L0_ffn_g", "L0_ffn_d", "L1_xattn_Wq", "L1_xattn_Wk", "L1_xattn_Wv",
        "L1_xattn_Wo", "L1_xattn_q_norm_w", "L1_xattn_k_norm_w", "L1_ffn_A", "L1_ffn_B", "L1_ffn_Wr"]


def kernel(**inputs):
    import concourse.bacc as bacc
    from concourse.bass_utils import run_bass_kernel_spmd

    nc = bacc.Bacc("TRN2", target_bir_lowering=False, num_devices=1)
    arrays, args = {}, []
    for name in _INS:
        a = np.ascontiguousarray(inputs[name])
        arrays[f"in_{name}"] = a
        args.append(nc.dram_tensor(f"in_{name}", a.shape, mybir.dt.from_np(a.dtype), kind="ExternalInput").ap())
    for name, table in zip(("rope_q_table", "rope_k_table"), rope_constants()):
        arrays[name] = table
        args.append(nc.dram_tensor(name, table.shape, F32, kind="ExternalInput").ap())
    args.append(nc.dram_tensor("out", (B, S, E), F32, kind="ExternalOutput").ap())
    build(nc, *args)
    r = run_bass_kernel_spmd(nc, [arrays], core_ids=[0])
    return r.results[0]["out"]
```
